# Optimizing a Trainium2 kernel written in Bass

```python
import numpy as np
import jax
import jax.numpy as jnp

def _softmax(x, axis=-1):
    return jax.nn.softmax(x, axis=axis)

def _gelu(x):
    return jax.nn.gelu(x, approximate=True)

def _silu(x):
    return jax.nn.silu(x)

def _sigmoid(x):
    return jax.nn.sigmoid(x)

def _layernorm(x, axis=-1, eps=1e-05):
    m = jnp.mean(x, axis=axis, keepdims=True)
    v = jnp.var(x, axis=axis, keepdims=True)
    return (x - m) / jnp.sqrt(v + eps)

def _scatter_add(tgt, idx, src, axis=0):
    return tgt.at[idx].add(src)

def _segment_sum(src, seg, n):
    return jax.ops.segment_sum(src, seg, n)
kernel_name = 'mk_adaln_ffn_d2_seqx_r8_c73b8c'

def setup_inputs(seed: int=0):
    np.random.seed(seed)
    _w = jnp.asarray

    def _rec_inputs():
        import jax
        import jax.numpy as jnp
        _rk = jax.random.key(seed)
        x = -0.0003929 + 0.9999 * jax.random.normal(jax.random.fold_in(_rk, 1), (8, 128, 256), jnp.float32)
        _lenS = 128 - jax.random.randint(jax.random.fold_in(_rk, 7), (8,), 0, max(1, 128 // 4) + 1, jnp.int32)
        _lenS2 = 128 - jax.random.randint(jax.random.fold_in(_rk, 8), (8,), 0, max(1, 128 // 4) + 1, jnp.int32)
        cond_1 = jax.random.uniform(jax.random.fold_in(_rk, 11), (8, 1), jnp.float32, 0.0, 1.37214)
        itok_Bx257_0_4111 = jax.random.randint(jax.random.fold_in(_rk, 12), (8, 257), 0, 514, jnp.int32)
        itok_B_37_3939 = jax.random.randint(jax.random.fold_in(_rk, 13), (8,), 37, 3940, jnp.int32)
        return (x, cond_1, itok_Bx257_0_4111, itok_B_37_3939)
    x, cond_1, itok_Bx257_0_4111, itok_B_37_3939 = _rec_inputs()

    def _L0_cond_setup():
        import jax, jax.numpy as jnp
        import numpy as np
        B, S, D_MODEL, NHEAD = (4, 256, 256, 16)
        HEAD_DIM = D_MODEL // NHEAD
        key = jax.random.key(seed)
        ks = jax.random.split(key, 6)
        scale = 1.0 / np.sqrt(D_MODEL)
        return {'hidden_states': jax.random.normal(ks[0], (B, S, D_MODEL), dtype=jnp.float32), 'attention_precision': jax.random.uniform(ks[1], (B, 1, 1), dtype=jnp.float32, minval=0.5, maxval=2.0), 'Wq': jax.random.normal(ks[2], (D_MODEL, D_MODEL), dtype=jnp.float32) * scale, 'Wk': jax.random.normal(ks[3], (D_MODEL, D_MODEL), dtype=jnp.float32) * scale, 'Wv': jax.random.normal(ks[4], (D_MODEL, D_MODEL), dtype=jnp.float32) * scale, 'Wo': jax.random.normal(ks[5], (D_MODEL, D_MODEL), dtype=jnp.float32) * scale}
    _L0_cond_all = _L0_cond_setup()
    _L0_cond_in = {k: v for k, v in _L0_cond_all.items() if k in ('Wq', 'Wk', 'Wv', 'Wo')}
    del _L0_cond_all

    def _L0_ffn_setup():
        import jax, jax.numpy as jnp
        import numpy as np
        B, S, D = (2, 256, 256)
        H, KV, HD = (16, 4, 128)
        E, F, TOPK = (8, 512, 2)
        THETA = 1000000.0
        EPS = 1e-05

        def rmsnorm(x, w):
            var = jnp.mean(jnp.square(x), axis=-1, keepdims=True)
            return x * jax.lax.rsqrt(var + EPS) * w

        def rope_cos_sin(seq_len):
            inv_freq = 1.0 / THETA ** (jnp.arange(0, HD, 2, dtype=jnp.float32) / HD)
            ang = jnp.arange(seq_len, dtype=jnp.float32)[:, None] * inv_freq[None, :]
            return (jnp.cos(ang)[None, :, None, :], jnp.sin(ang)[None, :, None, :])

        def apply_rope(x, cos, sin):
            x1, x2 = jnp.split(x, 2, axis=-1)
            return jnp.concatenate([x1 * cos - x2 * sin, x2 * cos + x1 * sin], axis=-1)

        def attention(x, wq, wk, wv, wo):
            b, s, _ = x.shape
            q = (x @ wq).reshape(b, s, H, HD)
            k = (x @ wk).reshape(b, s, KV, HD)
            v = (x @ wv).reshape(b, s, KV, HD)
            cos, sin = rope_cos_sin(s)
            q = apply_rope(q, cos, sin)
            k = apply_rope(k, cos, sin)
            rep = H // KV
            k = jnp.repeat(k, rep, axis=2)
            v = jnp.repeat(v, rep, axis=2)
            scores = jnp.einsum('bqhd,bkhd->bhqk', q, k) / np.sqrt(HD)
            causal = jnp.tril(jnp.ones((s, s), dtype=bool))
            scores = jnp.where(causal[None, None], scores, jnp.finfo(scores.dtype).min)
            probs = jax.nn.softmax(scores, axis=-1)
            out = jnp.einsum('bhqk,bkhd->bqhd', probs, v).reshape(b, s, H * HD)
            return out @ wo

        def moe(x, gate_w, w1, w3, w2):
            b, s, d = x.shape
            xt = x.reshape(b * s, d)
            logits = xt @ gate_w
            topv, topi = jax.lax.top_k(logits, TOPK)
            probs = jax.nn.softmax(topv, axis=-1)
            w = jnp.zeros_like(logits)
            for kk in range(TOPK):
                w = w + jax.nn.one_hot(topi[:, kk], E, dtype=logits.dtype) * probs[:, kk:kk + 1]
            out = jnp.zeros_like(xt)
            for e in range(E):
                h = jax.nn.silu(xt @ w1[e]) * (xt @ w3[e])
                out = out + w[:, e:e + 1] * (h @ w2[e])
            return out.reshape(b, s, d)
        key = jax.random.key(seed)
        ks = jax.random.split(key, 10)
        init = lambda k, shape: jax.random.normal(k, shape, jnp.float32) * 0.02
        return {'hidden_states': jax.random.normal(ks[0], (B, S, D), jnp.float32), 'norm1_w': jnp.ones((D,), jnp.float32), 'norm2_w': jnp.ones((D,), jnp.float32), 'wq': init(ks[1], (D, H * HD)), 'wk': init(ks[2], (D, KV * HD)), 'wv': init(ks[3], (D, KV * HD)), 'wo': init(ks[4], (H * HD, D)), 'gate_w': init(ks[5], (D, E)), 'w1': init(ks[6], (E, D, F)), 'w3': init(ks[7], (E, D, F)), 'w2': init(ks[8], (E, F, D))}
    _L0_ffn_all = _L0_ffn_setup()
    _L0_ffn_in = {k: v for k, v in _L0_ffn_all.items() if k in ('norm1_w', 'norm2_w', 'wq', 'wk', 'wv', 'wo', 'gate_w', 'w1', 'w3', 'w2')}
    del _L0_ffn_all

    def _L1_cond_setup():
        import jax, jax.numpy as jnp
        import numpy as np
        H, G, HD = (8, 4, 32)
        GSZ = H // G
        BLOCK = 16
        WINDOW = 128
        SCALE = 256.0 ** (-0.5)
        EPS = 1e-06
        THETA = 10000.0
        B, T, D = (16, 4, 256)
        NBLK = 257

        def _rms(x, scale):
            var = jnp.mean(x * x, axis=-1, keepdims=True)
            return x * jax.lax.rsqrt(var + EPS) * (1.0 + scale)

        def _rope(x, pos):
            half = HD // 2
            inv = 1.0 / THETA ** (jnp.arange(half, dtype=jnp.float32) / half)
            ang = pos[:, :, None].astype(jnp.float32) * inv
            cos = jnp.cos(ang)[:, None, :, :]
            sin = jnp.sin(ang)[:, None, :, :]
            x1, x2 = (x[..., :half], x[..., half:])
            return jnp.concatenate([x1 * cos - x2 * sin, x2 * cos + x1 * sin], axis=-1)
        key = jax.random.key(seed)
        ks = jax.random.split(key, 10)
        inv_d = 1.0 / np.sqrt(D)
        return {'x': jax.random.normal(ks[0], (B, T, D), jnp.float32), 'Wq': jax.random.normal(ks[1], (H * HD, D), jnp.float32) * inv_d, 'Wk': jax.random.normal(ks[2], (G * HD, D), jnp.float32) * inv_d, 'Wv': jax.random.normal(ks[3], (G * HD, D), jnp.float32) * inv_d, 'Wo': jax.random.normal(ks[4], (D, H * HD), jnp.float32) * inv_d, 'q_norm_scale': jax.random.normal(ks[5], (HD,), jnp.float32) * 0.02, 'k_norm_scale': jax.random.normal(ks[6], (HD,), jnp.float32) * 0.02, 'k_blocks': jax.random.normal(ks[7], (B * NBLK, G, BLOCK, HD), jnp.float32), 'v_blocks': jax.random.normal(ks[8], (B * NBLK, G, BLOCK, HD), jnp.float32), 'block_tables': jnp.arange(B * NBLK, dtype=jnp.int32).reshape(B, NBLK), 'kv_lens': jax.random.randint(ks[9], (B,), 0, 512, dtype=jnp.int32)}
    _L1_cond_all = _L1_cond_setup()
    _L1_cond_in = {k: v for k, v in _L1_cond_all.items() if k in ('Wq', 'Wk', 'Wv', 'Wo', 'q_norm_scale', 'k_norm_scale', 'k_blocks', 'v_blocks')}
    del _L1_cond_all

    def _L1_ffn_setup():
        import jax, jax.numpy as jnp
        import numpy as np
        K = 2

        def gelu(v):
            return jax.nn.gelu(v, approximate=False)
        key = jax.random.key(seed)
        ks = jax.random.split(key, 10)
        B, S, D, H, E = (4, 256, 256, 128, 8)
        SH = 2 * H
        u = lambda k_, shape, b: jax.random.uniform(k_, shape, jnp.float32, -b, b)
        return {'x': jax.random.normal(ks[0], (B, S, D), jnp.float32), 'gate_w': u(ks[1], (D, E), 1.0 / D), 'w1': u(ks[2], (E, D, H), 1.0 / D), 'b1': u(ks[3], (E, H), 1.0 / np.sqrt(D)), 'w2': u(ks[4], (E, H, D), 1.0 / H), 'b2': u(ks[5], (E, D), 1.0 / np.sqrt(H)), 'shared_w1': u(ks[6], (D, SH), 1.0 / D), 'shared_b1': u(ks[7], (SH,), 1.0 / np.sqrt(D)), 'shared_w2': u(ks[8], (SH, D), 1.0 / SH), 'shared_b2': u(ks[9], (D,), 1.0 / np.sqrt(SH))}
    _L1_ffn_all = _L1_ffn_setup()
    _L1_ffn_in = {k: v for k, v in _L1_ffn_all.items() if k in ('gate_w', 'w1', 'b1', 'w2', 'b2', 'shared_w1', 'shared_b1', 'shared_w2', 'shared_b2')}
    del _L1_ffn_all
    return {'x': x, 'cond_1': cond_1, 'itok_Bx257_0_4111': itok_Bx257_0_4111, 'itok_B_37_3939': itok_B_37_3939, 'L0_cond_Wq': _L0_cond_in['Wq'], 'L0_cond_Wk': _L0_cond_in['Wk'], 'L0_cond_Wv': _L0_cond_in['Wv'], 'L0_cond_Wo': _L0_cond_in['Wo'], 'L0_ffn_norm1_w': _L0_ffn_in['norm1_w'], 'L0_ffn_norm2_w': _L0_ffn_in['norm2_w'], 'L0_ffn_wq': _L0_ffn_in['wq'], 'L0_ffn_wk': _L0_ffn_in['wk'], 'L0_ffn_wv': _L0_ffn_in['wv'], 'L0_ffn_wo': _L0_ffn_in['wo'], 'L0_ffn_gate_w': _L0_ffn_in['gate_w'], 'L0_ffn_w1': _L0_ffn_in['w1'], 'L0_ffn_w3': _L0_ffn_in['w3'], 'L0_ffn_w2': _L0_ffn_in['w2'], 'L1_cond_Wq': _L1_cond_in['Wq'], 'L1_cond_Wk': _L1_cond_in['Wk'], 'L1_cond_Wv': _L1_cond_in['Wv'], 'L1_cond_Wo': _L1_cond_in['Wo'], 'L1_cond_q_norm_scale': _L1_cond_in['q_norm_scale'], 'L1_cond_k_norm_scale': _L1_cond_in['k_norm_scale'], 'L1_cond_k_blocks': _L1_cond_in['k_blocks'], 'L1_cond_v_blocks': _L1_cond_in['v_blocks'], 'L1_ffn_gate_w': _L1_ffn_in['gate_w'], 'L1_ffn_w1': _L1_ffn_in['w1'], 'L1_ffn_b1': _L1_ffn_in['b1'], 'L1_ffn_w2': _L1_ffn_in['w2'], 'L1_ffn_b2': _L1_ffn_in['b2'], 'L1_ffn_shared_w1': _L1_ffn_in['shared_w1'], 'L1_ffn_shared_b1': _L1_ffn_in['shared_b1'], 'L1_ffn_shared_w2': _L1_ffn_in['shared_w2'], 'L1_ffn_shared_b2': _L1_ffn_in['shared_b2']}

def reference(x, cond_1, itok_Bx257_0_4111, itok_B_37_3939, L0_cond_Wq, L0_cond_Wk, L0_cond_Wv, L0_cond_Wo, L0_ffn_norm1_w, L0_ffn_norm2_w, L0_ffn_wq, L0_ffn_wk, L0_ffn_wv, L0_ffn_wo, L0_ffn_gate_w, L0_ffn_w1, L0_ffn_w3, L0_ffn_w2, L1_cond_Wq, L1_cond_Wk, L1_cond_Wv, L1_cond_Wo, L1_cond_q_norm_scale, L1_cond_k_norm_scale, L1_cond_k_blocks, L1_cond_v_blocks, L1_ffn_gate_w, L1_ffn_w1, L1_ffn_b1, L1_ffn_w2, L1_ffn_b2, L1_ffn_shared_w1, L1_ffn_shared_b1, L1_ffn_shared_w2, L1_ffn_shared_b2):
    import jax
    import jax.numpy as jnp

    def _L0_cond_ref(hidden_states, attention_precision, Wq, Wk, Wv, Wo):
        import jax, jax.numpy as jnp
        import numpy as np
        B, S, D_MODEL, NHEAD = (4, 256, 256, 16)
        HEAD_DIM = D_MODEL // NHEAD
        b, s, _ = hidden_states.shape

        def proj(x, W):
            y = jnp.einsum('bsd,ed->bse', x, W)
            return y.reshape(b, s, NHEAD, HEAD_DIM).transpose(0, 2, 1, 3)
        q = proj(hidden_states, Wq)
        k = proj(hidden_states, Wk)
        v = proj(hidden_states, Wv)
        beta = jnp.minimum(attention_precision, 4.0)[:, None]
        q = q * beta
        scores = jnp.einsum('bhqd,bhkd->bhqk', q, k) / np.sqrt(HEAD_DIM)
        causal = jnp.tril(jnp.ones((s, s), dtype=bool))
        scores = jnp.where(causal, scores, jnp.finfo(scores.dtype).min)
        attn = jax.nn.softmax(scores, axis=-1)
        out = jnp.einsum('bhqk,bhkd->bhqd', attn, v)
        out = out.transpose(0, 2, 1, 3).reshape(b, s, D_MODEL)
        return jnp.einsum('bsd,ed->bse', out, Wo)

    def _L0_ffn_ref(hidden_states, norm1_w, norm2_w, wq, wk, wv, wo, gate_w, w1, w3, w2):
        import jax, jax.numpy as jnp
        import numpy as np
        B, S, D = (2, 256, 256)
        H, KV, HD = (16, 4, 128)
        E, F, TOPK = (8, 512, 2)
        THETA = 1000000.0
        EPS = 1e-05

        def rmsnorm(x, w):
            var = jnp.mean(jnp.square(x), axis=-1, keepdims=True)
            return x * jax.lax.rsqrt(var + EPS) * w

        def rope_cos_sin(seq_len):
            inv_freq = 1.0 / THETA ** (jnp.arange(0, HD, 2, dtype=jnp.float32) / HD)
            ang = jnp.arange(seq_len, dtype=jnp.float32)[:, None] * inv_freq[None, :]
            return (jnp.cos(ang)[None, :, None, :], jnp.sin(ang)[None, :, None, :])

        def apply_rope(x, cos, sin):
            x1, x2 = jnp.split(x, 2, axis=-1)
            return jnp.concatenate([x1 * cos - x2 * sin, x2 * cos + x1 * sin], axis=-1)

        def attention(x, wq, wk, wv, wo):
            b, s, _ = x.shape
            q = (x @ wq).reshape(b, s, H, HD)
            k = (x @ wk).reshape(b, s, KV, HD)
            v = (x @ wv).reshape(b, s, KV, HD)
            cos, sin = rope_cos_sin(s)
            q = apply_rope(q, cos, sin)
            k = apply_rope(k, cos, sin)
            rep = H // KV
            k = jnp.repeat(k, rep, axis=2)
            v = jnp.repeat(v, rep, axis=2)
            scores = jnp.einsum('bqhd,bkhd->bhqk', q, k) / np.sqrt(HD)
            causal = jnp.tril(jnp.ones((s, s), dtype=bool))
            scores = jnp.where(causal[None, None], scores, jnp.finfo(scores.dtype).min)
            probs = jax.nn.softmax(scores, axis=-1)
            out = jnp.einsum('bhqk,bkhd->bqhd', probs, v).reshape(b, s, H * HD)
            return out @ wo

        def moe(x, gate_w, w1, w3, w2):
            b, s, d = x.shape
            xt = x.reshape(b * s, d)
            logits = xt @ gate_w
            topv, topi = jax.lax.top_k(logits, TOPK)
            probs = jax.nn.softmax(topv, axis=-1)
            w = jnp.zeros_like(logits)
            for kk in range(TOPK):
                w = w + jax.nn.one_hot(topi[:, kk], E, dtype=logits.dtype) * probs[:, kk:kk + 1]
            out = jnp.zeros_like(xt)
            for e in range(E):
                h = jax.nn.silu(xt @ w1[e]) * (xt @ w3[e])
                out = out + w[:, e:e + 1] * (h @ w2[e])
            return out.reshape(b, s, d)
        attn_out = attention(rmsnorm(hidden_states, norm1_w), wq, wk, wv, wo)
        h = hidden_states + attn_out
        out = h + moe(rmsnorm(h, norm2_w), gate_w, w1, w3, w2)
        return out

    def _L1_cond_ref(x, Wq, Wk, Wv, Wo, q_norm_scale, k_norm_scale, k_blocks, v_blocks, block_tables, kv_lens):
        import jax, jax.numpy as jnp
        import numpy as np
        H, G, HD = (8, 4, 32)
        GSZ = H // G
        BLOCK = 16
        WINDOW = 128
        SCALE = 256.0 ** (-0.5)
        EPS = 1e-06
        THETA = 10000.0
        B, T, D = (16, 4, 256)
        NBLK = 257

        def _rms(x, scale):
            var = jnp.mean(x * x, axis=-1, keepdims=True)
            return x * jax.lax.rsqrt(var + EPS) * (1.0 + scale)

        def _rope(x, pos):
            half = HD // 2
            inv = 1.0 / THETA ** (jnp.arange(half, dtype=jnp.float32) / half)
            ang = pos[:, :, None].astype(jnp.float32) * inv
            cos = jnp.cos(ang)[:, None, :, :]
            sin = jnp.sin(ang)[:, None, :, :]
            x1, x2 = (x[..., :half], x[..., half:])
            return jnp.concatenate([x1 * cos - x2 * sin, x2 * cos + x1 * sin], axis=-1)
        Bx, Tx, _ = x.shape
        q = jnp.einsum('btd,od->bto', x, Wq).reshape(Bx, Tx, H, HD).transpose(0, 2, 1, 3)
        k = jnp.einsum('btd,od->bto', x, Wk).reshape(Bx, Tx, G, HD).transpose(0, 2, 1, 3)
        v = jnp.einsum('btd,od->bto', x, Wv).reshape(Bx, Tx, G, HD).transpose(0, 2, 1, 3)
        q = _rms(q, q_norm_scale)
        k = _rms(k, k_norm_scale)
        pos = kv_lens[:, None] + jnp.arange(Tx, dtype=jnp.int32)
        q = _rope(q, pos)
        k = _rope(k, pos)
        slot = pos // BLOCK
        off = pos % BLOCK
        blk = jnp.take_along_axis(block_tables, slot, axis=1)
        k_blocks = k_blocks.at[blk, :, off, :].set(k.transpose(0, 2, 1, 3))
        v_blocks = v_blocks.at[blk, :, off, :].set(v.transpose(0, 2, 1, 3))
        k_all = k_blocks[block_tables].transpose(0, 2, 1, 3, 4).reshape(Bx, G, -1, HD)
        v_all = v_blocks[block_tables].transpose(0, 2, 1, 3, 4).reshape(Bx, G, -1, HD)
        S = k_all.shape[2]
        qg = q.reshape(Bx, G, GSZ, Tx, HD)
        scores = jnp.einsum('bghtd,bgsd->bghts', qg, k_all) * SCALE
        kpos = jnp.arange(S, dtype=jnp.int32)
        allowed = (kpos[None, None, :] <= pos[:, :, None]) & (kpos[None, None, :] > pos[:, :, None] - WINDOW)
        scores = jnp.where(allowed[:, None, None, :, :], scores, -jnp.inf)
        p = jax.nn.softmax(scores, axis=-1)
        o = jnp.einsum('bghts,bgsd->bghtd', p, v_all).reshape(Bx, H, Tx, HD)
        o = o.transpose(0, 2, 1, 3).reshape(Bx, Tx, H * HD)
        return jnp.einsum('bto,do->btd', o, Wo)

    def _L1_ffn_ref(x, gate_w, w1, b1, w2, b2, shared_w1, shared_b1, shared_w2, shared_b2):
        import jax, jax.numpy as jnp
        import numpy as np
        K = 2

        def gelu(v):
            return jax.nn.gelu(v, approximate=False)
        B, S, D = x.shape
        E = gate_w.shape[1]
        xf = x.reshape(-1, D)
        logits = xf @ gate_w
        top_logits, top_idx = jax.lax.top_k(logits, K)
        top_gates = jax.nn.softmax(top_logits, axis=-1)
        gates = jnp.sum(jax.nn.one_hot(top_idx, E, dtype=xf.dtype) * top_gates[..., None], axis=1)
        h = gelu(jnp.einsum('nd,edh->neh', xf, w1) + b1)
        out_e = jnp.einsum('neh,ehd->ned', h, w2) + b2
        routed = jnp.einsum('ne,ned->nd', gates, out_e)
        shared = gelu(xf @ shared_w1 + shared_b1) @ shared_w2 + shared_b2
        return (routed + shared).reshape(B, S, D)
    x = x + _L0_ffn_ref(_L0_cond_ref(x, cond_1[:, None, :], L0_cond_Wq, L0_cond_Wk, L0_cond_Wv, L0_cond_Wo), L0_ffn_norm1_w, L0_ffn_norm2_w, L0_ffn_wq, L0_ffn_wk, L0_ffn_wv, L0_ffn_wo, L0_ffn_gate_w, L0_ffn_w1, L0_ffn_w3, L0_ffn_w2)
    x = x + _L1_ffn_ref(_L1_cond_ref(x, L1_cond_Wq, L1_cond_Wk, L1_cond_Wv, L1_cond_Wo, L1_cond_q_norm_scale, L1_cond_k_norm_scale, L1_cond_k_blocks, L1_cond_v_blocks, itok_Bx257_0_4111, itok_B_37_3939), L1_ffn_gate_w, L1_ffn_w1, L1_ffn_b1, L1_ffn_w2, L1_ffn_b2, L1_ffn_shared_w1, L1_ffn_shared_b1, L1_ffn_shared_w2, L1_ffn_shared_b2)
    return x

_drawn_inputs = setup_inputs


def setup_inputs(seed=0):
    import zlib

    import numpy as np

    out = dict(_drawn_inputs(seed))
    spreads = {'L0_ffn_norm1_w': (1.0, 0.2), 'L0_ffn_norm2_w': (1.0, 0.6)}
    factors = {'L0_ffn_wq': 8.0,
     'L0_ffn_wk': 8.0,
     'L0_ffn_gate_w': 3.32,
     'L0_ffn_w1': 2.958,
     'L0_ffn_w3': 2.951,
     'L0_ffn_w2': 2.967,
     'L1_cond_Wq': 4.478,
     'L1_cond_Wk': 41.576,
     'L1_cond_q_norm_scale': 26.217,
     'L1_cond_k_norm_scale': 64.0,
     'L1_cond_k_blocks': 5.157,
     'L1_cond_v_blocks': 3.068,
     'L1_ffn_w1': 8.0,
     'L1_ffn_b1': 8.0,
     'L1_ffn_w2': 8.0,
     'L1_ffn_shared_w1': 8.0,
     'L1_ffn_shared_b1': 8.0,
     'L1_ffn_shared_w2': 8.0,
     'L1_cond_Wv': 3.539,
     'L1_ffn_b2': 2.874,
     'L1_ffn_shared_b2': 2.877}
    for name, (base, spread) in spreads.items():
        noise = np.random.default_rng([zlib.crc32(name.encode()), seed]).standard_normal(out[name].shape)
        drawn = base * np.exp(spread * noise) if base else spread * noise
        out[name] = jnp.asarray(drawn.astype(out[name].dtype))
    for name, factor in factors.items():
        out[name] = (out[name] * factor).astype(out[name].dtype)
    return out
```

```python
import concourse.bass as bass
from concourse import mybir
from concourse.alu_op_type import AluOpType as ALU
from contextlib import ExitStack

P = 128
NSEQ, D = 8, 256
KC = D // P
PAIRS = NSEQ // 2
CH, CHD = 16, 16
FH, FKV, FHD = 16, 4, 128
E0, F0 = 8, 512
TILES0 = (2 * NSEQ * P + E0 * (P - 1)) // P
G1, HD1 = 4, 32
C1 = 2
NBLK, BLOCK = 257, 16
E1, H1 = 8, 128
SH1 = 2 * H1
NEG = -1.0e30

CONST_COLS = dict(ident=P, causal=P, older=P, cos=P, sin=P, ones=P, before=P, key_row=P, expert=64,
                  expert8=64, below=64, tile_no=TILES0 * E0, even=1, odd=1, row=1, seq_base=16)
CONST_AT, _n = {}, 0
for _k, _w in CONST_COLS.items():
    CONST_AT[_k] = (_n, _w)
    _n += _w
CONST_N = _n


class Banks:

    def __init__(self, uses, before, times):
        self.base = list(before)
        self.per = [0] * 8
        self.at = {}
        for use, bank in uses:
            self.at[use] = (bank, self.per[bank])
            self.per[bank] += 1
        self.after = [b + times * p for b, p in zip(before, self.per)]

    def count(self, it, use):
        bank, k = self.at[use]
        return bank, it * self.per[bank] + (self.base[bank] + k)


class TileBanks:

    RINGS = dict(up=(0, 2), gate=(2, 2), hT=(4, 1), xT=(5, 1), down=(6, 2))

    def __init__(self, before, tiles):
        self.base = list(before)
        self.after = list(before)
        for first, ring in self.RINGS.values():
            for i in range(tiles):
                self.after[first + i % ring] += 1

    def count(self, j, use):
        name, c = use
        first, ring = self.RINGS[name]
        b = first + c % ring
        return b, (j + (self.base[b] + c // 2) if ring == 2 else j * 2 + (self.base[b] + c))


def program(nc, t, out):
    fp32, i32 = mybir.dt.float32, mybir.dt.int32
    ACT = mybir.ActivationFunctionType
    AX = mybir.AxisListType
    ctx = ExitStack()
    with ctx:
        def sb(name, shape, dt=fp32):
            return ctx.enter_context(nc.sbuf_tensor(name, shape, dt))

        def sem(name):
            return ctx.enter_context(nc.semaphore(name))

        bank = [ctx.enter_context(nc.psum_tensor(f"bank{i}", [P, 512], fp32)) for i in range(8)]
        bank_full = [sem(f"bank_full{i}") for i in range(8)]
        bank_free = [sem(f"bank_free{i}") for i in range(8)]

        xs_d = nc.dram_tensor("routed_rows", [TILES0 * P, D], fp32, kind="Internal").ap()
        ys_d = nc.dram_tensor("expert_rows", [TILES0 * P, D], fp32, kind="Internal").ap()
        kv_d = nc.dram_tensor("new_kv_rows", [NSEQ * P, D], fp32, kind="Internal").ap()
        wl_d = nc.dram_tensor("written_places", [NSEQ * P], fp32, kind="Internal").ap()

        const = sb("const", [P, CONST_N])

        def c(name):
            a, w = CONST_AT[name]
            return const[:, a:a + w]

        ident = c("ident")
        w_c = sb("cond_weights", [P, 4, KC, D])
        w_kv = sb("ffn_wk_wv", [P, 2, KC, FKV * FHD])
        w_qo = sb("ffn_wq_wo", [P, 8192])
        wq = w_qo[:, 0:4096].rearrange("p (c n) -> p c n", c=KC)
        wo = w_qo[:, 4096:8192].rearrange("p (h n) -> p h n", h=FH)
        w2e = w_qo[:, :].rearrange("p (e c n) -> p e c n", e=E0, c=F0 // P)
        w13 = sb("experts_w1_w3", [P, 2, E0, KC, F0])
        gate0 = sb("gate0", [P, KC, E0])
        norm1 = sb("norm1", [P, KC])
        norm2 = sb("norm2", [P, KC])
        beta = sb("beta", [P, NSEQ])
        x_in = sb("x_in", [P, 2, D])
        xT = sb("xT", [P, KC, 2 * P])
        cqT = sb("cond_qT", [P, KC, 2 * P])
        ckT = sb("cond_kT_masked", [P, KC, 2, 2 * P])
        cv = sb("cond_v", [P, 2, D])
        masked = sb("masked_scores", [P, 2, 512])
        probs = sb("probs", [P, 3, 512])
        probsT = sb("probsT", [P, 2, 512])
        o_sb = sb("attn_rows", [P, 2, D])
        oT = sb("attn_rowsT", [P, KC, 2 * P])
        y_sb = sb("cond_out", [P, 2, D])
        xn = sb("normed", [P, 2, D])
        xnT = sb("normedT", [P, KC, 2 * P])
        fqT = sb("ffn_qT", [P, 2, 4, 2 * P])
        fkT = sb("ffn_kT", [P, FKV, 2 * P])
        fv = sb("ffn_v", [P, 2, 512])
        swapped = sb("swapped", [P, 2, 512])
        foT = sb("ffn_oT", [P, 2, 512])
        junk = swapped[:, 0, 0:D]
        h_all = sb("h_all", [P, NSEQ, D])
        logits = sb("logits", [P, NSEQ, E0])
        row_max = sb("row_max", [P, 2, 4])
        neg_max = sb("neg_max", [P, 3, 4])
        row_sum = sb("row_sum", [P, 2, 16])
        row_inv = sb("row_inv", [P, 2, 16])
        fsum = sb("ffn_row_sum", [P, 3, 4])
        finv = sb("ffn_row_inv", [P, 3, 4])
        sq = sb("sum_squares", [P, 4])
        ms = sb("mean_squares", [P, 4])
        rstd = sb("rstd", [P, 4])
        rstd2 = sb("rstd2_all", [P, NSEQ])
        neg_half = sb("neg_half", [P, 16])
        carrier = sb("carrier", [1, 1])
        cos_b = c("cos")
        sin_b = c("sin")
        kv_old = sb("kv_old", [P, NSEQ, D])
        kv_new = sb("kv_new", [P, NSEQ, D])

        consts_loaded = sem("consts_loaded")
        neg_half_ready = sem("neg_half_ready")
        beta_ready = sem("beta_ready")
        cond_w_loaded = sem("cond_w_loaded")
        attn_w_loaded = sem("attn_w_loaded")
        expert_w_loaded = sem("expert_w_loaded")
        x_loaded = sem("x_loaded")

        def wait(eng, s, value):
            if not isinstance(value, int) or value > 0:
                eng.wait_ge(s, value)

        def carry_waits(v):
            v.memset(carrier[0:1, 0:1], 0.0)

        def claim(ph, it, use):
            b, n = ph.count(it, use)
            wait(nc.tensor, bank_free[b], n)
            return bank[b]

        def filled(eng, ph, it, use):
            b, n = ph.count(it, use)
            eng.wait_ge(bank_full[b], n + 1)
            return bank[b]

        def drained(eng, ph, it, use):
            b, n = ph.count(it, use)
            wait(eng, bank_free[b], n + 1)

        def full_sem(ph, use):
            return bank_full[ph.count(0, use)[0]]

        def free_sem(ph, use):
            return bank_free[ph.count(0, use)[0]]

        NC_ = 8
        uses = [("xT", 7), ("cq", 4), ("ck", 5), ("cv", 6)]
        for n in range(NC_ + 3):
            if n < NC_:
                uses.append((("cS", n), n % 4))
            if 0 <= n - 2 < NC_:
                uses.append((("cT", n - 2), 4 + n % 2))
            if 0 <= n - 3 and (n - 3) % 4 == 3:
                s = (n - 3) // 4
                uses.append((("cO", s), 6 + s))
            if n == 8:
                uses.append((("cOT", 0), 0))
            if n == 9:
                uses.append((("cY", 0), 6))
        uses += [(("cOT", 1), 1), (("xn", 0), 2), (("cY", 1), 7), (("fv", 0), 4), (("xn", 1), 3), (("fv", 1), 5)]
        uses += [(("rope", r), (3, 7)[r % 2]) for r in range(6)]
        NF = 8
        for n in range(NF + 4):
            if n < NF:
                uses.append((("fS", n), n % 3))
            if n in (1, 3):
                uses += [(("rope", r), (3, 7)[r % 2]) for r in (6 + n - 1, 7 + n - 1)]
            if 0 <= n - 2 < NF:
                uses.append((("fT", n - 2), 4))
            if 0 <= n - 3 < NF:
                uses.append((("fO", n - 3), 5))
            if n - 4 == NF - 1:
                uses.append(("wo", 6))
        uses += [("x2", 4), ("logit", 5)]
        A = Banks(uses, [0] * 8, PAIRS)

        cond_max = sem("cond_max_ready")
        cond_probs = sem("cond_probs_ready")
        cond_pv = sem("cond_pv_done")
        cond_inv = sem("cond_inverse_sums_ready")
        cond_q0 = sem("cond_q_first_half_copied")
        y_copied = sem("cond_out_copied")
        y_squares = sem("cond_out_squares_ready")
        mean_sq = sem("mean_squares_ready")
        y_rstd = sem("cond_out_rstd_ready")
        xn_ready = sem("normed_rows_ready")
        swap_ready = sem("rope_halves_swapped")
        sin_ready = sem("rope_sine_part_ready")
        cos_ready = sem("rope_cosine_part_ready")
        ffn_max = sem("ffn_max_ready")
        ffn_probs = sem("ffn_probs_ready")
        ffn_inv = sem("ffn_inverse_sums_ready")
        ffn_scaled = sem("ffn_probs_scaled")
        wo_done = sem("wo_step_done")
        h_squares = sem("h_squares_ready")
        h_mean = sem("h_mean_squares_ready")
        h_rstd = sem("h_rstd_ready")
        x2_ready = sem("x2_rows_ready")

        def heads_of(j):
            return [fc * 8 + 2 * j + par for fc in range(2) for par in range(2)]

        def A_pe(it):
            pe, te = nc.tensor, nc.tensor
            wait(pe, x_loaded, 16 * (it + 1) if isinstance(it, int) else it * 16 + 16)
            b = claim(A, it, "xT")
            for k in range(KC):
                for s in range(2):
                    last = te.transpose(b[:, (k * 2 + s) * P:(k * 2 + s + 1) * P], x_in[:, s, k * P:(k + 1) * P], ident)
            last.then_inc(full_sem(A, "xT"), 1)
            drained(pe, A, it, "xT")
            for use, w in (("cq", 0), ("ck", 1)):
                b = claim(A, it, use)
                for fc in range(KC):
                    for k in range(KC):
                        last = te.matmul(b[:, fc * 256:(fc + 1) * 256], w_c[:, w, k, fc * P:(fc + 1) * P], xT[:, k, :],
                                         start=(k == 0), stop=(k == KC - 1))
                last.then_inc(full_sem(A, use), 1)
            b = claim(A, it, "cv")
            for s in range(2):
                for k in range(KC):
                    last = te.matmul(b[:, s * 256:(s + 1) * 256], xT[:, k, s * P:(s + 1) * P], w_c[:, 2, k, :],
                                     start=(k == 0), stop=(k == KC - 1))
            last.then_inc(full_sem(A, "cv"), 1)
            drained(pe, A, it, "cq")
            drained(pe, A, it, "ck")

            def scores(n):
                s, j = n // 4, n % 4
                b = claim(A, it, ("cS", n))
                for fc in range(2):
                    last = te.matmul(b[:, fc * 256:(fc + 1) * 256], cqT[32 * j:32 * j + 32, fc, s * P:(s + 1) * P],
                                     ckT[32 * j:32 * j + 32, fc, :, s * P:(s + 1) * P], start=True, stop=True)
                last.then_inc(full_sem(A, ("cS", n)), 1)

            def transpose_probs(n):
                pe.wait_ge(cond_probs, it * NC_ + (n + 1))
                b = claim(A, it, ("cT", n))
                for i in range(4):
                    last = te.transpose(b[:, i * P:(i + 1) * P], probs[:, n % 3, i * P:(i + 1) * P], ident)
                last.then_inc(full_sem(A, ("cT", n)), 1)

            def values(n):
                s, j = n // 4, n % 4
                if n == 0:
                    drained(pe, A, it, "cv")
                drained(pe, A, it, ("cT", n))
                b = claim(A, it, ("cO", s)) if j == 0 else bank[6 + s]
                for i, h in enumerate(heads_of(j)):
                    last = te.matmul(b[:, h * CHD:(h + 1) * CHD], probsT[:, n % 2, i * P:(i + 1) * P],
                                     cv[:, s, h * CHD:(h + 1) * CHD], start=True, stop=True)
                if j < 3:
                    last.then_inc(cond_pv, 1)
                else:
                    last.then_inc(full_sem(A, ("cO", s)), 1)

            def transpose_rows(use, s, src):
                b = claim(A, it, (use, s))
                for k in range(KC):
                    last = te.transpose(b[:, k * P:(k + 1) * P], src[:, s, k * P:(k + 1) * P], ident)
                last.then_inc(full_sem(A, (use, s)), 1)

            def cond_out(s):
                drained(pe, A, it, ("cOT", s))
                b = claim(A, it, ("cY", s))
                for k in range(KC):
                    last = te.matmul(b[:, 0:256], oT[:, k, s * P:(s + 1) * P], w_c[:, 3, k, :],
                                     start=(k == 0), stop=(k == KC - 1))
                last.then_inc(full_sem(A, ("cY", s)), 1)

            for n in range(NC_ + 3):
                if n < NC_:
                    scores(n)
                if 0 <= n - 2 < NC_:
                    transpose_probs(n - 2)
                if 0 <= n - 3:
                    values(n - 3)
                if n == 8:
                    drained(pe, A, it, ("cO", 0))
                    transpose_rows("cOT", 0, o_sb)
                if n == 9:
                    cond_out(0)
            drained(pe, A, it, ("cO", 1))
            transpose_rows("cOT", 1, o_sb)
            pe.wait_ge(xn_ready, it * 2 + 1)
            transpose_rows("xn", 0, xn)
            cond_out(1)

            def ffn_values_proj(s):
                drained(pe, A, it, ("xn", s))
                b = claim(A, it, ("fv", s))
                for k in range(KC):
                    last = te.matmul(b[:, :], xnT[:, k, s * P:(s + 1) * P], w_kv[:, 1, k, :],
                                     start=(k == 0), stop=(k == KC - 1))
                last.then_inc(full_sem(A, ("fv", s)), 1)

            if isinstance(it, int):
                pe.wait_ge(attn_w_loaded, 64)
            ffn_values_proj(0)
            pe.wait_ge(xn_ready, it * 2 + 2)
            transpose_rows("xn", 1, xn)
            ffn_values_proj(1)

            def rope_proj(r):
                b = claim(A, it, ("rope", r))
                for i in range(2):
                    for k in range(KC):
                        f = (2 * r + i) * FHD if r < 2 else (2 * (r - 2) + i) * FHD
                        w = w_kv[:, 0, k, f:f + FHD] if r < 2 else wq[:, k, f:f + FHD]
                        last = te.matmul(b[:, i * 256:(i + 1) * 256], w, xnT[:, k, :],
                                         start=(k == 0), stop=(k == KC - 1))
                last.then_inc(full_sem(A, ("rope", r)), 1)

            for r in range(6):
                rope_proj(r)

            def ffn_scores(n):
                g, s = n // 2, n % 2
                if s == 0:
                    for r in ((0, 2, 3), (4, 5), (1, 6, 7), (8, 9))[g]:
                        drained(pe, A, it, ("rope", r))
                b = claim(A, it, ("fS", n))
                for i in range(4):
                    last = te.matmul(b[:, i * P:(i + 1) * P], fqT[:, g % 2, i, s * P:(s + 1) * P],
                                     fkT[:, g, s * P:(s + 1) * P], start=True, stop=True)
                last.then_inc(full_sem(A, ("fS", n)), 1)

            def ffn_transpose(n):
                pe.wait_ge(ffn_scaled, it * NF + (n + 1))
                b = claim(A, it, ("fT", n))
                for i in range(4):
                    last = te.transpose(b[:, i * P:(i + 1) * P], probs[:, n % 3, i * P:(i + 1) * P], ident)
                last.then_inc(full_sem(A, ("fT", n)), 1)

            def ffn_values(n):
                g, s = n // 2, n % 2
                if n < 2:
                    drained(pe, A, it, ("fv", n))
                drained(pe, A, it, ("fT", n))
                b = claim(A, it, ("fO", n))
                te.matmul(b[:, :], fv[:, s, g * FHD:(g + 1) * FHD], probsT[:, n % 2, :],
                          start=True, stop=True).then_inc(full_sem(A, ("fO", n)), 1)

            def ffn_out(n):
                g, s = n // 2, n % 2
                if n == 0:
                    claim(A, it, "wo")
                drained(pe, A, it, ("fO", n))
                for i in range(4):
                    last = te.matmul(bank[6][:, s * 256:(s + 1) * 256], foT[:, n % 2, i * P:(i + 1) * P],
                                     wo[:, 4 * g + i, :], start=(n == 0 and i == 0), stop=(g == 3 and i == 3),
                                     skip_group_check=True)
                last.then_inc(wo_done if n < NF - 1 else full_sem(A, "wo"), 1)

            for n in range(NF + 4):
                if n < NF:
                    ffn_scores(n)
                if n in (1, 3):
                    rope_proj(6 + n - 1)
                    rope_proj(7 + n - 1)
                if 0 <= n - 2 < NF:
                    ffn_transpose(n - 2)
                if 0 <= n - 3 < NF:
                    ffn_values(n - 3)
                if 0 <= n - 4:
                    ffn_out(n - 4)
            pe.wait_ge(x2_ready, it * 2 + 2)
            b = claim(A, it, "x2")
            for k in range(KC):
                for s in range(2):
                    last = te.transpose(b[:, (k * 2 + s) * P:(k * 2 + s + 1) * P], xn[:, s, k * P:(k + 1) * P], ident)
            last.then_inc(full_sem(A, "x2"), 1)
            drained(pe, A, it, "x2")
            b = claim(A, it, "logit")
            for s in range(2):
                for k in range(KC):
                    last = te.matmul(b[:, s * E0:(s + 1) * E0], xnT[:, k, s * P:(s + 1) * P], gate0[:, k, :],
                                     start=(k == 0), stop=(k == KC - 1))
            last.then_inc(full_sem(A, "logit"), 1)

        def A_dve(it):
            dve, v = nc.vector, nc.vector
            b = filled(dve, A, it, "xT")
            v.tensor_copy(xT[:, :, :].rearrange("p a b -> p (a b)"), b[:, :]).then_inc(free_sem(A, "xT"), 1)
            b = filled(dve, A, it, "ck")
            bk = b[:, :].rearrange("p (a b) -> p a b", a=2)
            v.tensor_scalar(ckT[:, :, 0, :], bk, c("even"), None, ALU.mult)
            v.tensor_scalar(ckT[:, :, 1, :], bk, c("odd"), None, ALU.mult).then_inc(free_sem(A, "ck"), 1)

            def mask_max(use, n, m_ready, per, scale, p_ready):
                b, cnt = A.count(it, (use, n))
                dve.wait_ge(bank_full[b], cnt + 1)
                wait(dve, p_ready, it * per + (n - 1))
                carry_waits(v)
                for i in range(4):
                    last = v.tensor_tensor_reduce(out=masked[:, n % 2, i * P:(i + 1) * P], in0=bank[b][:, i * P:(i + 1) * P],
                                                  in1=c("causal"), scale=1.0, scalar=-3.0e38, op0=ALU.add, op1=ALU.max,
                                                  accum_out=row_max[:, n % 2, i:i + 1])
                last.then_inc(bank_free[b], 1)
                dve.wait_ge(bank_free[b], cnt + 1)
                v.tensor_scalar(neg_max[:, n % 3, :], row_max[:, n % 2, :], -scale, None, ALU.mult).then_inc(m_ready, 1)

            def probsT_copy(use, n):
                b = filled(dve, A, it, (use, n))
                if use == "cT":
                    if n >= 2:
                        s, j = (n - 2) // 4, (n - 2) % 4
                        if j < 3:
                            dve.wait_ge(cond_pv, it * 6 + (3 * s + j + 1))
                        else:
                            filled(dve, A, it, ("cO", s))
                elif n >= 2:
                    filled(dve, A, it, ("fO", n - 2))
                v.tensor_copy(probsT[:, n % 2, :], b[:, :]).then_inc(free_sem(A, (use, n)), 1)

            def cond_norm(s):
                dve.wait_ge(cond_probs, it * NC_ + (4 * s + 4))
                v.reciprocal(row_inv[:, s, :], row_sum[:, s, :]).then_inc(cond_inv, 1)
                dve.wait_ge(cond_inv, it * 2 + (s + 1))
                b = filled(dve, A, it, ("cO", s))
                v.tensor_tensor(o_sb[:, s, :].rearrange("p (h d) -> p h d", h=CH),
                                b[:, 0:256].rearrange("p (h d) -> p h d", h=CH),
                                row_inv[:, s, :].unsqueeze(2).broadcast_to([P, CH, CHD]), ALU.mult)\
                    .then_inc(free_sem(A, ("cO", s)), 1)

            def oT_copy(s):
                b = filled(dve, A, it, ("cOT", s))
                v.tensor_copy(oT[:, :, s * P:(s + 1) * P], b[:, 0:256].rearrange("p (a b) -> p a b", a=2))\
                    .then_inc(free_sem(A, ("cOT", s)), 1)

            def norm_rows(s):
                dve.wait_ge(y_rstd, it * 2 + (s + 1))
                dve.wait_ge(y_copied, it * 2 + (s + 1))
                v.tensor_scalar(xn[:, s, :], y_sb[:, s, :], rstd[:, s:s + 1], None, ALU.mult).then_inc(xn_ready, 1)

            def xnT_copy(s):
                b = filled(dve, A, it, ("xn", s))
                for k in range(KC):
                    last = v.tensor_scalar(xnT[:, k, s * P:(s + 1) * P], b[:, k * P:(k + 1) * P], norm1[:, k:k + 1],
                                           None, ALU.mult)
                last.then_inc(free_sem(A, ("xn", s)), 1)

            for n in range(NC_ + 2):
                if n < NC_:
                    mask_max("cS", n, cond_max, NC_, CHD ** -0.5 * 0 + 1.0, cond_probs)
                if 0 <= n - 2:
                    probsT_copy("cT", n - 2)
                if n == 7:
                    cond_norm(0)
                if n == 9:
                    oT_copy(0)
            cond_norm(1)
            norm_rows(0)
            oT_copy(1)
            xnT_copy(0)
            norm_rows(1)
            xnT_copy(1)

            def rope(r):
                b = filled(dve, A, it, ("rope", r))
                if r < 2:
                    dst = fkT[:, 2 * r:2 * r + 2, :].rearrange("p a b -> p (a b)")
                else:
                    g, i = (r - 2) // 2, (r - 2) % 2
                    dst = fqT[:, g % 2, 2 * i:2 * i + 2, :].rearrange("p a b -> p (a b)")
                dve.wait_ge(swap_ready, it * 10 + (r + 1))
                v.tensor_tensor(dst.rearrange("p (a b) -> p a b", a=4), b[:, :].rearrange("p (a b) -> p a b", a=4),
                                cos_b.unsqueeze(1).broadcast_to([P, 4, P]), ALU.mult).then_inc(cos_ready, 1)
                dve.wait_ge(cos_ready, it * 10 + (r + 1))
                dve.wait_ge(sin_ready, it * 10 + (r + 1))
                v.tensor_tensor(dst, dst, swapped[:, r % 2, :], ALU.add).then_inc(free_sem(A, ("rope", r)), 1)

            for r in range(6):
                rope(r)

            def scale_probs(n):
                dve.wait_ge(ffn_probs, it * NF + (n + 1))
                v.reciprocal(finv[:, n % 3, :], fsum[:, n % 3, :]).then_inc(ffn_inv, 1)
                dve.wait_ge(ffn_inv, it * NF + (n + 1))
                pr = probs[:, n % 3, :].rearrange("p (a b) -> p a b", a=4)
                v.tensor_tensor(pr, pr, finv[:, n % 3, :].unsqueeze(2).broadcast_to([P, 4, P]), ALU.mult)\
                    .then_inc(ffn_scaled, 1)

            for n in range(NF + 2):
                if n < NF:
                    mask_max("fS", n, ffn_max, NF, FHD ** -0.5, ffn_probs)
                if n in (1, 3):
                    rope(6 + n - 1)
                    rope(7 + n - 1)
                if 0 <= n - 1 < NF:
                    scale_probs(n - 1)
                if 0 <= n - 2:
                    probsT_copy("fT", n - 2)
            b = filled(dve, A, it, "wo")
            v.tensor_tensor(h_all[:, bass.ds(it * 2, 2), :], b[:, :].rearrange("p (a b) -> p a b", a=2), y_sb[:, :, :],
                            ALU.add).then_inc(free_sem(A, "wo"), 1)
            for s in range(2):
                dve.wait_ge(h_rstd, it * 2 + (s + 1))
                v.tensor_scalar(xn[:, s, :], h_all[:, bass.ds(it * 2 + s, 1), :].rearrange("p a b -> p (a b)"),
                                rstd[:, 2 + s:3 + s], None, ALU.mult).then_inc(x2_ready, 1)
            v.tensor_copy(rstd2[:, bass.ds(it * 2, 2)], rstd[:, 2:4])
            b = filled(dve, A, it, "x2")
            for k in range(KC):
                last = v.tensor_scalar(xnT[:, k, :], b[:, k * 256:(k + 1) * 256], norm2[:, k:k + 1], None, ALU.mult)
            last.then_inc(free_sem(A, "x2"), 1)
            b = filled(dve, A, it, "logit")
            v.tensor_copy(logits[:, bass.ds(it * 2, 2), :], b[:, 0:2 * E0].rearrange("p (a b) -> p a b", a=2))\
                .then_inc(free_sem(A, "logit"), 1)

        def A_act(it):
            act, a = nc.scalar, nc.scalar
            b = filled(act, A, it, "cq")
            for s in range(2):
                last = a.activation(cqT[:, :, s * P:(s + 1) * P],
                                    b[:, :].rearrange("p (f t) -> p f t", f=2)[:, :, s * P:(s + 1) * P],
                                    ACT.Copy, scale=beta[:, bass.ds(it * 2 + s, 1)])
            last.then_inc(free_sem(A, "cq"), 1)
            b = filled(act, A, it, "cv")
            a.activation(cv[:, :, :].rearrange("p a b -> p (a b)"), b[:, :], ACT.Copy).then_inc(free_sem(A, "cv"), 1)

            def exps(n, m_ready, per, scale, T, p_ready, sums):
                act.wait_ge(m_ready, it * per + (n + 1))
                if n >= 3:
                    filled(act, A, it, (T, n - 3))
                for i in range(4):
                    last = a.activation(probs[:, n % 3, i * P:(i + 1) * P], masked[:, n % 2, i * P:(i + 1) * P],
                                        ACT.Exp, bias=neg_max[:, n % 3, i:i + 1], scale=scale, accum_out=sums(n, i))
                last.then_inc(p_ready, 1)

            def cond_copy(s):
                b = filled(act, A, it, ("cY", s))
                a.activation(y_sb[:, s, :], b[:, 0:256], ACT.Copy).then_inc(y_copied, 1)
                a.activation(junk, b[:, 0:256], ACT.Square, accum_out=sq[:, s:s + 1])\
                    .then_inc(y_squares, 1)
                act.wait_ge(y_squares, it * 2 + (s + 1))
                a.activation(ms[:, s:s + 1], sq[:, s:s + 1], ACT.Copy, scale=1.0 / D, bias=1e-5).then_inc(free_sem(A, ("cY", s)), 1)

            for n in range(NC_):
                exps(n, cond_max, NC_, 1.0, "cT", cond_probs,
                     lambda n, i: row_sum[:, n // 4, heads_of(n % 4)[i]:heads_of(n % 4)[i] + 1])
            cond_copy(0)
            cond_copy(1)
            for s in range(2):
                b = filled(act, A, it, ("fv", s))
                a.activation(fv[:, s, :], b[:, :], ACT.Copy).then_inc(free_sem(A, ("fv", s)), 1)

            def swap(r):
                b = filled(act, A, it, ("rope", r))
                wait(act, free_sem(A, ("rope", r)), A.count(it, ("rope", r))[1])
                a.activation(swapped[0:64, r % 2, :], b[64:128, :], ACT.Copy)
                a.activation(swapped[64:128, r % 2, :], b[0:64, :], ACT.Copy).then_inc(swap_ready, 1)

            for r in range(6):
                swap(r)

            def o_copy(n):
                b = filled(act, A, it, ("fO", n))
                if n >= 2:
                    act.wait_ge(wo_done, it * 7 + (n - 1))
                a.activation(foT[:, n % 2, :], b[:, :], ACT.Copy).then_inc(free_sem(A, ("fO", n)), 1)

            for n in range(NF + 3):
                if n < NF:
                    exps(n, ffn_max, NF, FHD ** -0.5, "fT", ffn_probs, lambda n, i: fsum[:, n % 3, i:i + 1])
                if n in (1, 3):
                    swap(6 + n - 1)
                    swap(7 + n - 1)
                if 0 <= n - 3:
                    o_copy(n - 3)
            drained(act, A, it, "wo")
            for s in range(2):
                a.activation(junk, h_all[:, bass.ds(it * 2 + s, 1), :].rearrange("p a b -> p (a b)"), ACT.Square,
                             accum_out=sq[:, 2 + s:3 + s]).then_inc(h_squares, 1)
                act.wait_ge(h_squares, it * 2 + (s + 1))
                a.activation(ms[:, 2 + s:3 + s], sq[:, 2 + s:3 + s], ACT.Copy, scale=1.0 / D, bias=1e-5).then_inc(h_mean, 1)

        def A_pool(it):
            pool, g = nc.gpsimd, nc.gpsimd
            for s in range(2):
                drained(pool, A, it, ("cY", s))
                g.tensor_tensor(rstd[:, s:s + 1], ms[:, s:s + 1], neg_half[:, 0:1], ALU.pow).then_inc(y_rstd, 1)

            def sine(r):
                pool.wait_ge(swap_ready, it * 10 + (r + 1))
                sw = swapped[:, r % 2, :].rearrange("p (a b) -> p a b", a=4)
                g.tensor_tensor(sw, sw, sin_b.unsqueeze(1).broadcast_to([P, 4, P]), ALU.mult).then_inc(sin_ready, 1)

            for r in range(10):
                sine(r)
            for s in range(2):
                pool.wait_ge(h_mean, it * 2 + (s + 1))
                g.tensor_tensor(rstd[:, 2 + s:3 + s], ms[:, 2 + s:3 + s], neg_half[:, 0:1], ALU.pow).then_inc(h_rstd, 1)


        B = Banks([("rank", 0)], A.after, 1)
        route = {n: sb("route_" + n, [P, NSEQ, E0]) for n in ("eq", "one1", "one2", "rest", "slot")}
        rmax = sb("route_max", [P, 2, NSEQ])
        rcand = sb("route_first", [P, NSEQ])
        p12 = sb("route_probs", [P, 2, NSEQ])
        pexp = sb("route_exp", [P, 2, NSEQ])
        cum = sb("rows_before", [P, NSEQ + 1, E0])
        tiles_f = sb("tiles_of_expert", [P, 4, E0])
        tiles_i = sb("tiles_of_expert_int", [P, 2, E0], i32)
        slots_i = sb("slots", [P, 2, NSEQ], i32)
        slots_f = sb("slots_float", [P, 2, NSEQ])
        tile_e = sb("expert_of_tile", [1, TILES0], i32)
        tile_ef = sb("expert_of_tile_float", [1, TILES0])
        tile_cmp = sb("tile_compare", [1, TILES0 * E0])
        x2_all = fqT[:, :, :, :].rearrange("p a b c -> p (a b c)").rearrange("p (b d) -> p b d", b=NSEQ)

        route_step = sem("routing_step")
        exp_ready = sem("route_exp_ready")
        ones_ready = sem("route_counts_ready")
        x2_all_ready = sem("x2_all_ready")
        slots_ready = sem("slots_ready")
        tile_e_ready = sem("expert_of_tile_ready")
        zero_filled = sem("routed_rows_zero_filled")
        zero_ready = sem("zero_tile_ready")
        scattered = sem("rows_scattered")
        w2_loaded = sem("w2_loaded")
        l1_loaded = sem("layer1_weights_loaded")

        def top2(lg, n, link):
            v = nc.vector
            one, rest, eq = (route["one1"], route["one2"]), route["rest"], route["eq"]
            src = lg
            for i in range(2):
                link(v.tensor_reduce(rmax[:, i, 0:n], src, AX.X, ALU.max))
                link(v.tensor_tensor(eq[:, 0:n, :], src, rmax[:, i, 0:n].unsqueeze(2).broadcast_to([P, n, E0]), ALU.is_equal))
                link(v.scalar_tensor_tensor(eq[:, 0:n, :], eq[:, 0:n, :], -8.0,
                                            c("expert8").rearrange("p (a b) -> p a b", b=E0)[:, 0:n, :], ALU.mult, ALU.add))
                link(v.tensor_reduce(rcand[:, 0:n], eq[:, 0:n, :], AX.X, ALU.min))
                link(v.tensor_tensor(one[i][:, 0:n, :], c("expert").rearrange("p (a b) -> p a b", b=E0)[:, 0:n, :],
                                     rcand[:, 0:n].unsqueeze(2).broadcast_to([P, n, E0]), ALU.is_equal))
                if i == 0:
                    link(v.scalar_tensor_tensor(rest[:, 0:n, :], one[0][:, 0:n, :], NEG, lg, ALU.mult, ALU.add))
                    src = rest[:, 0:n, :]
            link(v.tensor_tensor(pexp[:, 0, 0:n], rmax[:, 1, 0:n], rmax[:, 0, 0:n], ALU.subtract))

        def top2_probs(n, link):
            v = nc.vector
            link(v.tensor_scalar(p12[:, 1, 0:n], pexp[:, 1, 0:n], 1.0, None, ALU.add))
            link(v.reciprocal(p12[:, 0, 0:n], p12[:, 1, 0:n]))
            link(v.tensor_tensor(p12[:, 1, 0:n], pexp[:, 1, 0:n], p12[:, 0, 0:n], ALU.mult))

        def B_dve():
            dve, v = nc.vector, nc.vector
            steps = [0]

            def link(ins):
                steps[0] += 1
                ins.then_inc(route_step, 1)
                dve.wait_ge(route_step, steps[0])

            drained(dve, A, PAIRS - 1, "logit")
            top2(logits[:, :, :], NSEQ, link)
            v.tensor_tensor(route["eq"][:, :, :], route["one1"][:, :, :], route["one2"][:, :, :], ALU.add)\
                .then_inc(ones_ready, 1)
            for b in range(NSEQ):
                last = v.tensor_scalar(x2_all[:, b, :], h_all[:, b, :], rstd2[:, b:b + 1], None, ALU.mult)
            last.then_inc(x2_all_ready, 1)
            link(v.memset(cum[:, 0, :], 0.0))
            b = filled(dve, B, 0, "rank")
            for i in range(NSEQ):
                link(v.tensor_tensor(cum[:, i + 1, :], cum[:, i, :], b[:, 64 + i * E0:64 + (i + 1) * E0], ALU.add))
            link(v.tensor_scalar(tiles_i[:, 0, :], cum[:, NSEQ, :], float(P - 1), None, ALU.add))
            link(v.tensor_scalar(tiles_i[:, 1, :], tiles_i[:, 0, :], 7, None, ALU.arith_shift_right))
            link(v.tensor_copy(tiles_f[:, 0, :], tiles_i[:, 1, :]))
            link(v.tensor_tensor(route["rest"][:, :, :], c("below").rearrange("p (a b) -> p a b", b=E0),
                                 tiles_f[:, 0, :].unsqueeze(1).broadcast_to([P, E0, E0]), ALU.mult))
            link(v.tensor_reduce(tiles_f[:, 1, :], route["rest"][:, :, :], AX.X, ALU.add))
            link(v.tensor_tensor(tiles_f[:, 2, :], tiles_f[:, 1, :], tiles_f[:, 0, :], ALU.add))
            link(v.tensor_scalar(tiles_f[:, 3, :], tiles_f[:, 1, :], float(P), None, ALU.mult))
            link(v.tensor_tensor(route["slot"][:, :, :].rearrange("p a b -> p (a b)"),
                                 cum[:, 0:NSEQ, :].rearrange("p a b -> p (a b)"), b[:, 0:64], ALU.add))
            link(v.tensor_tensor(route["slot"][:, :, :], route["slot"][:, :, :],
                                 tiles_f[:, 3, :].unsqueeze(1).broadcast_to([P, NSEQ, E0]), ALU.add))
            for i in range(2):
                link(v.tensor_tensor(route["rest"][:, :, :], route["one%d" % (i + 1)][:, :, :], route["slot"][:, :, :], ALU.mult))
                link(v.tensor_reduce(slots_f[:, i, :], route["rest"][:, :, :], AX.X, ALU.add))
            v.tensor_copy(slots_i[:, :, :], slots_f[:, :, :]).then_inc(slots_ready, 1)
            link(v.tensor_tensor(tile_cmp[:, :].rearrange("p (a b) -> p a b", b=E0),
                                 c("tile_no")[0:1, :].rearrange("p (a b) -> p a b", b=E0),
                                 tiles_f[0:1, 2, :].unsqueeze(1).broadcast_to([1, TILES0, E0]), ALU.is_ge))
            link(v.tensor_reduce(tile_ef[:, :], tile_cmp[:, :].rearrange("p (a b) -> p a b", b=E0), AX.X, ALU.add))
            v.tensor_scalar(tile_e[:, :], tile_ef[:, :], float(E0 - 1), None, ALU.min).then_inc(tile_e_ready, 1)
            dve.wait_ge(exp_ready, 1)
            top2_probs(NSEQ, link)
            dve.wait_ge(slots_ready, 1)
            nc.vector.memset(carrier[0:1, 0:1], 0.0).then_inc(free_sem(B, "rank"), 1)

        def B_pe():
            pe, te = nc.tensor, nc.tensor
            pe.wait_ge(ones_ready, 1)
            b = claim(B, 0, "rank")
            m = route["eq"][:, :, :].rearrange("p a b -> p (a b)")
            te.matmul(b[:, 0:64], c("before"), m, start=True, stop=True)
            te.matmul(b[:, 64:128], c("ones"), m, start=True, stop=True).then_inc(full_sem(B, "rank"), 1)

        def B_act():
            act = nc.scalar
            act.wait_ge(route_step, 12)
            nc.scalar.activation(pexp[:, 1, :], pexp[:, 0, :], ACT.Exp).then_inc(exp_ready, 1)

        def B_pool():
            pool = nc.gpsimd
            pool.wait_ge(slots_ready, 1)
            pool.wait_ge(x2_all_ready, 1)
            pool.wait_ge(zero_filled, 48)
            for b in range(NSEQ):
                for i in range(2):
                    nc.gpsimd.indirect_dma_start(
                        out=xs_d, out_offset=bass.IndirectOffsetOnAxis(ap=slots_i[:, i, b:b + 1], axis=0),
                        in_=x2_all[:, b, :], in_offset=None).then_inc(scattered, 16)

        kvl = sb("kv_lens", [P, NSEQ], i32)
        pos = sb("positions", [P, 2 * NSEQ], i32)
        slot = sb("block_slots", [P, 2 * NSEQ], i32)
        off = sb("block_offsets", [P, 2 * NSEQ], i32)
        off_f = sb("block_offsets_float", [P, 2 * NSEQ])
        cache_f = sb("cache_rows_float", [P, NSEQ])
        table_at = sb("table_rows", [P, 2 * NSEQ], i32)
        block_no = sb("blocks", [P, 2 * NSEQ], i32)
        place = sb("places", [P, 24])
        winner = sb("last_writers", [P, 24])
        winner_i = sb("last_writers_int", [P, 2 * NSEQ], i32)
        winner_f = sb("last_writers_index", [P, 2 * NSEQ])
        cache_at = sb("cache_rows", [P, G1, NSEQ], i32)
        early = sb("positions_below_zero", [P, NSEQ])
        cs_all = sb("rope_rows", [P, NSEQ, 2 * BLOCK])
        written = kv_new[:, 0:4, :].rearrange("p a b -> p (a b)")
        row_no = kv_new[:, 4:8, :].rearrange("p a b -> p (a b)")
        winner_tmp = swapped[:, :, :].rearrange("p a b -> p (a b)")
        kvl_loaded = sem("kv_lens_loaded")
        place_step = sem("places_step")
        table_at_ready = sem("table_rows_ready")
        table_read = sem("table_read")
        pool_step = sem("pool_places_step")
        place_ready = sem("places_ready")
        written_out = sem("places_in_dram")
        written_in = sem("places_of_all_loaded")
        cache_read = sem("cache_read")
        winner_step = sem("winner_compared")
        winner_ready = sem("winner_ready")
        rope_loaded = sem("rope_rows_loaded")

        def places_dve():
            dve, v = nc.vector, nc.vector
            steps = [0]

            def link(ins):
                steps[0] += 1
                ins.then_inc(place_step, 1)
                dve.wait_ge(place_step, steps[0])

            v.memset(kv_old[:, :, :], 0.0).then_inc(zero_ready, 1)
            v.memset(place[:, :], 0.0)
            dve.wait_ge(kvl_loaded, 16)
            v.tensor_scalar(early[:, :], kvl[:, :], -1.0, float(P), ALU.mult, ALU.add)
            v.tensor_scalar(pos[:, 0:NSEQ], kvl[:, :], c("row"), None, ALU.add)
            link(v.tensor_scalar(pos[:, NSEQ:], kvl[:, :], c("row"), -float(P), ALU.add, ALU.add))
            link(v.tensor_scalar(pos[:, NSEQ:], pos[:, NSEQ:], 0.0, None, ALU.max))
            v.tensor_scalar(off[:, :], pos[:, :], BLOCK - 1, None, ALU.bitwise_and)
            link(v.tensor_scalar(slot[:, :], pos[:, :], 4, None, ALU.arith_shift_right))
            v.tensor_copy(off_f[:, :], off[:, :])
            v.scalar_tensor_tensor(table_at[:, :], slot[:, :], float(NBLK - 1), c("seq_base"), ALU.min, ALU.add)\
                .then_inc(table_at_ready, 1)

        def places_pool():
            pool, g = nc.gpsimd, nc.gpsimd
            pool.wait_ge(table_at_ready, 1)
            for n in range(2 * NSEQ):
                g.indirect_dma_start(out=block_no[:, n:n + 1], out_offset=None, in_=t["table"],
                                     in_offset=bass.IndirectOffsetOnAxis(ap=table_at[:, n:n + 1], axis=0)).then_inc(table_read, 16)
            pool.wait_ge(table_read, 16 * 2 * NSEQ)
            n = [0]

            def link(ins):
                n[0] += 1
                ins.then_inc(pool_step, 1)
                pool.wait_ge(pool_step, n[0])

            link(g.tensor_scalar(place[:, 0:16], block_no[:, :], float(BLOCK), None, ALU.mult))
            link(g.tensor_tensor(place[:, 0:16], place[:, 0:16], off_f[:, :], ALU.add))
            g.dma_start(wl_d.rearrange("(b p) -> p b", p=P), place[:, 0:NSEQ], allow_slow_non_contiguous=True).then_inc(written_out, 16)
            link(g.tensor_scalar(cache_f[:, :], block_no[:, NSEQ:], float(BLOCK * G1), None, ALU.mult))
            link(g.tensor_tensor(cache_f[:, :], cache_f[:, :], off_f[:, NSEQ:], ALU.add))
            for i in range(G1):
                link(g.tensor_scalar(cache_at[:, i, :], cache_f[:, :], float(BLOCK * i), None, ALU.add))
            pool.wait_ge(written_out, 16)
            g.dma_start(written, wl_d.rearrange("(o n) -> o n", o=1).broadcast_to([P, NSEQ * P])).then_inc(written_in, 16)
            g.dma_start(row_no, t["row_no"].rearrange("(o n) -> o n", o=1).broadcast_to([P, NSEQ * P])).then_inc(written_in, 16)

        def cache_pool():
            for name, at in (("k_blocks", 0), ("v_blocks", P)):
                rows = t[name].rearrange("n g o d -> (n g o) d")
                for b in range(NSEQ):
                    for i in range(G1):
                        nc.gpsimd.indirect_dma_start(
                            out=kv_old[:, b, at + i * HD1:at + (i + 1) * HD1], out_offset=None, in_=rows,
                            in_offset=bass.IndirectOffsetOnAxis(ap=cache_at[:, i, b:b + 1], axis=0)).then_inc(cache_read, 16)

        C = TileBanks(B.after, TILES0)
        rows_in = x_in
        rowsT = xT[:, :, :].rearrange("p a (r b) -> p r a b", r=2)
        silu = masked
        hid = probs
        hidT = probsT[:, :, :].rearrange("p r (a b) -> p r a b", b=P)
        rows_out = o_sb
        row_loaded = [sem("row_loaded0"), sem("row_loaded1")]
        row_stored = [sem("row_stored0"), sem("row_stored1")]

        STEPS = (TILES0 - 1) // 2

        def C_pe_step(j, k, more=True):
            pe, te = nc.tensor, nc.tensor
            i = j * 2 + k
            e = pe.value_load(tile_e[0:1, bass.ds(i, 1)], min_val=0, max_val=E0 - 1)
            drained(pe, C, j, ("xT", k))

            def half(use, w):
                b = claim(C, j, (use, k))
                for q in range(KC):
                    last = te.matmul(b[:, :], rowsT[:, k % 2, q, :], w13[:, w, bass.ds(e, 1), q, :],
                                     start=(q == 0), stop=(q == KC - 1))
                last.then_inc(full_sem(C, (use, k)), 1)

            half("up", 0)
            if k > 0 or not isinstance(j, int) or j > 0:
                C_transpose_hidden(j, k - 1)
            half("gate", 1)
            if more:
                C_transpose_rows(j, k + 1)
            if k > 0 or not isinstance(j, int) or j > 0:
                C_down(j, k - 1)

        def C_transpose_rows(j, k):
            pe, te = nc.tensor, nc.tensor
            wait(pe, row_loaded[k % 2], (j + (k // 2 + 1)) * 16)
            b = claim(C, j, ("xT", k))
            for q in range(KC):
                last = te.transpose(b[:, q * P:(q + 1) * P], rows_in[:, k % 2, q * P:(q + 1) * P], ident)
            last.then_inc(full_sem(C, ("xT", k)), 1)

        def C_transpose_hidden(j, k):
            pe, te = nc.tensor, nc.tensor
            drained(pe, C, j, ("gate", k))
            b = claim(C, j, ("hT", k))
            for q in range(F0 // P):
                last = te.transpose(b[:, q * P:(q + 1) * P], hid[:, k % 2, q * P:(q + 1) * P], ident)
            last.then_inc(full_sem(C, ("hT", k)), 1)

        def C_down(j, k):
            pe, te = nc.tensor, nc.tensor
            e = pe.value_load(tile_e[0:1, bass.ds(j * 2 + k, 1)], min_val=0, max_val=E0 - 1)
            drained(pe, C, j, ("hT", k))
            b = claim(C, j, ("down", k))
            for q in range(F0 // P):
                last = te.matmul(b[:, 0:256], hidT[:, k % 2, q, :], w2e[:, bass.ds(e, 1), q, :],
                                 start=(q == 0), stop=(q == F0 // P - 1))
            last.then_inc(full_sem(C, ("down", k)), 1)

        def C_rowsT_copy(j, k):
            b = filled(nc.vector, C, j, ("xT", k))
            for q in range(KC):
                last = nc.vector.tensor_scalar(rowsT[:, k % 2, q, :], b[:, q * P:(q + 1) * P], norm2[:, q:q + 1], None, ALU.mult)
            last.then_inc(free_sem(C, ("xT", k)), 1)

        def last_writer(j, k):
            v = nc.vector
            col = bass.ds(j * 2 + (k - 1), 1)
            n = j * 4 + 2 * (k - 1)
            wait(v, winner_step, n)
            v.scalar_tensor_tensor(winner_tmp, written, place[:, col], row_no, ALU.is_equal, ALU.mult).then_inc(winner_step, 1)
            v.wait_ge(winner_step, n + 1)
            v.tensor_reduce(winner[:, col], winner_tmp, AX.X, ALU.max).then_inc(winner_step, 1)

        def C_hidT_copy(j, k):
            b = filled(nc.vector, C, j, ("hT", k))
            nc.vector.tensor_copy(hidT[:, k % 2, :, :].rearrange("p a b -> p (a b)"), b[:, :]).then_inc(free_sem(C, ("hT", k)), 1)

        def C_dve_step(j, k, more=True):
            dve, v = nc.vector, nc.vector
            if k > 0 or not isinstance(j, int) or j > 0:
                C_hidT_copy(j, k - 1)
            b = filled(dve, C, j, ("gate", k))
            drained(dve, C, j, ("up", k))
            v.tensor_tensor(hid[:, k % 2, :], silu[:, k % 2, :], b[:, :], ALU.mult).then_inc(free_sem(C, ("gate", k)), 1)
            if more:
                C_rowsT_copy(j, k + 1)
            if 0 < k and more:
                last_writer(j, k)

        def C_act_down(j, k):
            act = nc.scalar
            b = filled(act, C, j, ("down", k))
            if k >= 2 or not isinstance(j, int) or j > 0:
                wait(act, row_stored[k % 2], (j + k // 2) * 16)
            nc.scalar.activation(rows_out[:, k % 2, :], b[:, 0:256], ACT.Copy).then_inc(free_sem(C, ("down", k)), 1)

        def C_act_step(j, k):
            act = nc.scalar
            b = filled(act, C, j, ("up", k))
            if k >= 2 or not isinstance(j, int) or j > 0:
                drained(act, C, j, ("gate", k - 2))
            nc.scalar.activation(silu[:, k % 2, :], b[:, :], ACT.Silu).then_inc(free_sem(C, ("up", k)), 1)
            if k > 0 or not isinstance(j, int) or j > 0:
                C_act_down(j, k - 1)

        def C_load(j, k):
            sp = nc.sync
            if k >= 2 or not isinstance(j, int) or j > 0:
                filled(sp, C, j, ("xT", k - 2))
            sp.dma_start(rows_in[:, k % 2, :], xs_d[bass.ds((j * 2 + k) * P, P), :]).then_inc(row_loaded[k % 2], 16)

        def C_store(j, k):
            sp = nc.sync
            drained(sp, C, j, ("down", k))
            sp.dma_start(ys_d[bass.ds((j * 2 + k) * P, P), :], rows_out[:, k % 2, :]).then_inc(row_stored[k % 2], 16)

        def C_run(eng, first, step, last):
            first()
            step(0, 1)
            step(0, 2)
            with eng.Fori(1, STEPS - 1) as j:
                step(j, 1)
                step(j, 2)
            step(STEPS - 1, 1)
            last()

        Dp = Banks([("x1T", 0), (("qkv", 0), 1), (("qkv", 1), 2), (("qT", 0), 3), (("qT", 1), 4)], C.after, PAIRS)
        w13f = w13[:, :, :, :, :].rearrange("p a e c f -> p (a e c f)")
        y_rows = [w13f[:, i * 2048:(i + 1) * 2048].rearrange("p (b d) -> p b d", b=NSEQ) for i in range(2)]
        x1_s = y_sb
        x1T = xT
        sq_rows = masked
        qn = probs
        qn_sin = oT[:, :, :].rearrange("p a b -> p (a b)")
        qkv_rows = swapped
        norm_w = cqT[:, :, :].rearrange("p a b -> p (a b)")
        w_qkv = fv[:, :, :].rearrange("p s n -> p (s n)").rearrange("p (c n) -> p c n", c=KC)
        w1_1 = w_c[:, :, :, :].rearrange("p a b c -> p (a b c)").rearrange("p (e c n) -> p e c n", e=E1, c=KC)
        w2_1 = w_kv[:, :, :, :].rearrange("p a b c -> p (a b c)").rearrange("p (e n) -> p e n", e=E1)
        sw1 = fkT[:, 0:2, :]
        sw2 = fkT[:, 2:4, :]
        wo_1 = foT[:, 0, :].rearrange("p (c n) -> p c n", c=C1)
        small = foT[:, 1, :]
        b1_s = small[:, 0:8]
        sb1_s = small[:, 8:10]
        gate1 = small[:, 16:32].rearrange("p (c n) -> p c n", c=KC)
        b2_s = small[0:9, 64:320]
        qT_all = fqT[:, :, :, :].rearrange("p a b c -> p (a b c)").rearrange("p (c b q) -> p c b q", c=C1, b=NSEQ)
        NQK = 12
        ssq = sb("qk_sum_squares", [P, 2, 16])
        rqk = sb("qk_rstd", [P, 2, 16])

        y_gathered = sem("expert_rows_gathered")
        x1_step = sem("x1_step")
        x1_ready = sem("x1_rows_ready")
        x1_kept = sem("x1_rows_kept")
        x_again = sem("x_loaded_again")
        sq_ready = sem("qk_squares_ready")
        ms_step = sem("qk_mean_squares_step")
        ms_ready = sem("qk_mean_squares_ready")
        rqk_ready = sem("qk_rstd_ready")
        qn_step = sem("qk_norm_step")
        qn_ready = sem("qk_normed")
        qsin_ready = sem("qk_sine_part_ready")
        v_copied = sem("new_v_copied")
        rows_ready = sem("qkv_rows_ready")
        kv_stored = sem("new_kv_stored")
        norm_w_ready = sem("qk_norm_weights_ready")

        def D_gather():
            pool = nc.gpsimd
            for i in range(2):
                tiles = (TILES0 + 1 - i) // 2
                pool.wait_ge(row_stored[i], 16 * tiles)
            for b in range(NSEQ):
                for i in range(2):
                    nc.gpsimd.indirect_dma_start(
                        out=y_rows[i][:, b, :], out_offset=None, in_=ys_d,
                        in_offset=bass.IndirectOffsetOnAxis(ap=slots_i[:, i, b:b + 1], axis=0)).then_inc(y_gathered, 16)

        def D_pe(it):
            pe, te = nc.tensor, nc.tensor
            pe.wait_ge(x1_ready, it * 2 + 2)
            b = claim(Dp, it, "x1T")
            for k in range(KC):
                for s in range(2):
                    last = te.transpose(b[:, (k * 2 + s) * P:(k * 2 + s + 1) * P], x1_s[:, s, k * P:(k + 1) * P], ident)
            last.then_inc(full_sem(Dp, "x1T"), 1)
            drained(pe, Dp, it, "x1T")
            for s in range(2):
                b = claim(Dp, it, ("qkv", s))
                for k in range(KC):
                    last = te.matmul(b[:, :], x1T[:, k, s * P:(s + 1) * P], w_qkv[:, k, :], start=(k == 0), stop=(k == KC - 1))
                last.then_inc(full_sem(Dp, ("qkv", s)), 1)
            for s in range(2):
                pe.wait_ge(rows_ready, it * 2 + (s + 1))
                b = claim(Dp, it, ("qT", s))
                for k in range(C1):
                    last = te.transpose(b[:, k * P:(k + 1) * P], qkv_rows[:, s, k * P:(k + 1) * P], ident)
                last.then_inc(full_sem(Dp, ("qT", s)), 1)

        def D_dve(it):
            dve, v = nc.vector, nc.vector
            dve.wait_ge(x_again, it * 16 + 16)
            if not isinstance(it, int) or it > 0:
                dve.wait_ge(x1_kept, it)
            for s in range(2):
                n = it * 6 + 3 * s
                v.tensor_tensor(x1_s[:, s, :], x_in[:, s, :], h_all[:, bass.ds(it * 2 + s, 1), :].rearrange("p a b -> p (a b)"),
                                ALU.add).then_inc(x1_step, 1)
                for i in range(2):
                    dve.wait_ge(x1_step, n + (i + 1))
                    v.scalar_tensor_tensor(x1_s[:, s, :], y_rows[i][:, bass.ds(it * 2 + s, 1), :].rearrange("p a b -> p (a b)"),
                                           p12[:, i, bass.ds(it * 2 + s, 1)], x1_s[:, s, :], ALU.mult, ALU.add)\
                        .then_inc(x1_step if i == 0 else x1_ready, 1)
                    if i == 1:
                        v.memset(carrier[0:1, 0:1], 0.0).then_inc(x1_step, 1)
            b = filled(dve, Dp, it, "x1T")
            v.tensor_copy(x1T[:, :, :].rearrange("p a b -> p (a b)"), b[:, :]).then_inc(free_sem(Dp, "x1T"), 1)
            for s in range(2):
                dve.wait_ge(sq_ready, it * 2 + (s + 1))
                v.tensor_reduce(ssq[:, s, 0:NQK], sq_rows[:, s, 0:NQK * HD1].rearrange("p (h d) -> p h d", d=HD1), AX.X, ALU.add)\
                    .then_inc(ms_step, 1)
                dve.wait_ge(ms_step, it * 2 + (s + 1))
                v.tensor_scalar(ssq[:, s, 0:NQK], ssq[:, s, 0:NQK], 1.0 / HD1, 1e-6, ALU.mult, ALU.add).then_inc(ms_ready, 1)
            for s in range(2):
                dve.wait_ge(rqk_ready, it * 2 + (s + 1))
                b = filled(dve, Dp, it, ("qkv", s))
                dve.wait_ge(v_copied, it * 2 + (s + 1))
                q = qn[:, s, 0:NQK * HD1]
                v.tensor_tensor(q.rearrange("p (h d) -> p h d", d=HD1), b[:, 0:NQK * HD1].rearrange("p (h d) -> p h d", d=HD1),
                                rqk[:, s, 0:NQK].unsqueeze(2).broadcast_to([P, NQK, HD1]), ALU.mult).then_inc(free_sem(Dp, ("qkv", s)), 1)
                drained(dve, Dp, it, ("qkv", s))
                v.tensor_tensor(q, q, norm_w[:, 0:NQK * HD1], ALU.mult).then_inc(qn_ready, 1)
                dve.wait_ge(qn_ready, it * 2 + (s + 1))
                if not isinstance(it, int) or it > 0:
                    dve.wait_ge(kv_stored, (it * 2 + (s - 1)) * 16 if s == 1 else it * 32)
                q4 = q.rearrange("p (h a d) -> p h a d", a=2, d=HD1 // 2)
                cs = cs_all[:, bass.ds(it * 2 + s, 1), :].rearrange("p a b -> p (a b)")
                sq4 = sq_rows[:, s, 0:NQK * HD1].rearrange("p (h a d) -> p h a d", a=2, d=HD1 // 2)
                for a in range(2):
                    last = v.tensor_tensor(sq4[:, :, a, :], q4[:, :, a, :],
                                           cs[:, 0:HD1 // 2].unsqueeze(1).broadcast_to([P, NQK, HD1 // 2]), ALU.mult)
                last.then_inc(qn_step, 1)
                dve.wait_ge(qn_step, it * 2 + (s + 1))
                dve.wait_ge(qsin_ready, it * 2 + (s + 1))
                r4 = qkv_rows[:, s, 0:NQK * HD1].rearrange("p (h a d) -> p h a d", a=2, d=HD1 // 2)
                n4 = qn_sin4(s)
                v.tensor_tensor(r4[:, :, 0, :], sq4[:, :, 0, :], n4[:, :, 1, :], ALU.subtract)
                v.tensor_tensor(r4[:, :, 1, :], sq4[:, :, 1, :], n4[:, :, 0, :], ALU.add).then_inc(rows_ready, 1)
            for s in range(2):
                b = filled(dve, Dp, it, ("qT", s))
                v.tensor_copy(qT_all[:, :, bass.ds(it * 2 + s, 1), :].rearrange("p c b q -> p c (b q)"),
                              b[:, 0:256].rearrange("p (c q) -> p c q", c=C1)).then_inc(free_sem(Dp, ("qT", s)), 1)

        def qn_sin4(s):
            return w13f[:, 4096 + 512 * s:4096 + 512 * s + NQK * HD1].rearrange("p (h a d) -> p h a d", a=2, d=HD1 // 2)

        def D_act(it):
            act, a = nc.scalar, nc.scalar
            act.wait_ge(x1_ready, it * 2 + 2)
            a.activation(h_all[:, bass.ds(it * 2, 2), :].rearrange("p a b -> p (a b)"),
                         x1_s[:, :, :].rearrange("p a b -> p (a b)"), ACT.Copy).then_inc(x1_kept, 1)
            for s in range(2):
                b = filled(act, Dp, it, ("qkv", s))
                if s == 0:
                    wait(act, rows_ready, it * 2)
                wait(act, kv_stored, it * 32)
                a.activation(sq_rows[:, s, 0:NQK * HD1], b[:, 0:NQK * HD1], ACT.Square).then_inc(sq_ready, 1)
                a.activation(qkv_rows[:, s, NQK * HD1:], b[:, NQK * HD1:], ACT.Copy).then_inc(v_copied, 1)

        def D_pool(it):
            pool, g = nc.gpsimd, nc.gpsimd
            for s in range(2):
                pool.wait_ge(ms_ready, it * 2 + (s + 1))
                g.tensor_tensor(rqk[:, s, 0:NQK], ssq[:, s, 0:NQK], neg_half[:, 0:NQK], ALU.pow).then_inc(rqk_ready, 1)
            for s in range(2):
                pool.wait_ge(qn_ready, it * 2 + (s + 1))
                q4 = qn[:, s, 0:NQK * HD1].rearrange("p (h a d) -> p h a d", a=2, d=HD1 // 2)
                cs = cs_all[:, bass.ds(it * 2 + s, 1), :].rearrange("p a b -> p (a b)")
                for a in range(2):
                    last = g.tensor_tensor(qn_sin4(s)[:, :, a, :], q4[:, :, a, :],
                                           cs[:, HD1 // 2:].unsqueeze(1).broadcast_to([P, NQK, HD1 // 2]), ALU.mult)
                last.then_inc(qsin_ready, 1)

        def D_store(it):
            sp = nc.sync
            if not isinstance(it, int) or it < PAIRS - 1:
                sp.wait_ge(x1_ready, it * 2 + 2)
                sp.dma_start(x_in[:, :, :], t["x"][bass.ds((it + 1) * 2, 2), :, :].rearrange("s p d -> p s d")).then_inc(x_again, 16)
            for s in range(2):
                sp.wait_ge(rows_ready, it * 2 + (s + 1))
                sp.wait_ge(v_copied, it * 2 + (s + 1))
                sp.dma_start(kv_d[bass.ds((it * 2 + s) * P, P), :], qkv_rows[:, s, 256:512]).then_inc(kv_stored, 16)

        E = Banks([(("kT", p), p) for p in range(PAIRS)], Dp.after, 1)
        kT_all = w_qo[:, 0:2048].rearrange("p (b k) -> p b k", b=NSEQ)
        kv_gathered = [sem("kv_gathered%d" % b) for b in range(NSEQ)]

        def E_pool():
            pool = nc.gpsimd
            pool.wait_ge(winner_ready, 1)
            pool.wait_ge(cache_read, 16 * 2 * NSEQ * G1)
            pool.wait_ge(kv_stored, 16 * NSEQ)
            for b in range(NSEQ):
                for dst, col in ((kv_old, NSEQ + b), (kv_new, b)):
                    nc.gpsimd.indirect_dma_start(
                        out=dst[:, b, :], out_offset=None, in_=kv_d,
                        in_offset=bass.IndirectOffsetOnAxis(ap=winner_i[:, col:col + 1], axis=0),
                        bounds_check=NSEQ * P - 1, oob_is_err=False).then_inc(kv_gathered[b], 16)

        def winners_dve():
            dve, v = nc.vector, nc.vector
            n = 2 * (2 * (STEPS - 1) + 1)
            dve.wait_ge(winner_step, n)
            v.tensor_scalar(winner_f[:, :], winner[:, 0:16], 0.0, 4096.0, ALU.is_equal, ALU.mult).then_inc(winner_step, 1)
            dve.wait_ge(winner_step, n + 1)
            v.scalar_tensor_tensor(winner_i[:, :], winner[:, 0:16], -1.0, winner_f[:, :], ALU.add, ALU.add).then_inc(winner_ready, 1)

        def E_pe():
            pe, te = nc.tensor, nc.tensor
            for p in range(PAIRS):
                b = claim(E, 0, ("kT", p))
                for s in range(2):
                    pe.wait_ge(kv_gathered[2 * p + s], 32)
                    for i, src in enumerate((kv_old, kv_new)):
                        last = te.transpose(b[:, (2 * s + i) * P:(2 * s + i + 1) * P], src[:, 2 * p + s, 0:P], ident)
                last.then_inc(full_sem(E, ("kT", p)), 1)

        def E_dve():
            for p in range(PAIRS):
                b = filled(nc.vector, E, 0, ("kT", p))
                nc.vector.tensor_copy(kT_all[:, 2 * p:2 * p + 2, :].rearrange("p a b -> p (a b)"), b[:, :])\
                    .then_inc(free_sem(E, ("kT", p)), 1)

        NL = 8
        uses = []
        for n in range(NL + 3):
            if n < NL:
                uses.append((("S", n), n % 4))
            if 0 <= n - 2 < NL:
                uses.append((("T", n - 2), 4 + n % 2))
            if 0 <= n - 3 and (n - 3) % 4 == 3:
                uses.append((("O", (n - 3) // 4), 6 + (n - 3) // 4))
            if n == 8:
                uses.append((("OT", 0), 0))
            if n == 9:
                uses.append((("Y", 0), 6))
        uses += [(("OT", 1), 1), (("XT", 0), 2), (("Y", 1), 7), (("XT", 1), 3), ("logit", 4), (("H", 0), 5), (("H", 1), 0),
                 ("gatesT", 1), (("H", 2), 2), (("H", 3), 3), ("SH", 4), ("SY", 6)]
        uses += [(("E", e), (5, 7, 0, 1)[e % 4]) for e in range(E1)]
        Fp = Banks(uses, E.after, PAIRS)

        def wf(at, n):
            return w13f[:, 8192 + at:8192 + at + n]

        q_s = wf(0, 512).rearrange("p (c s q) -> p c s q", c=C1, s=2)
        k_s = wf(512, 512).rearrange("p (s k) -> p s k", s=2)
        v_s = wf(1024, 512).rearrange("p (s i d) -> p s i d", s=2, i=2)
        mask_s = wf(1536, 512).rearrange("p (s k) -> p s k", s=2)
        hT = wf(2048, 2048).rearrange("p (e n) -> p e n", e=E1)
        shT = wf(4096, 512).rearrange("p (c n) -> p c n", c=2)
        acc = wf(4608, 512).rearrange("p (s d) -> p s d", s=2)
        gates = wf(5120, 32).rearrange("p (s e) -> p s e", s=2)
        gatesT = wf(5152, 256).rearrange("p (s q) -> p s q", s=2)[0:9, :, :]
        lg1 = wf(5408, 16).rearrange("p (s e) -> p s e", s=2)
        gtmp = wf(5424, 16).rearrange("p (s e) -> p s e", s=2)
        out_s = wf(5440, 512).rearrange("p (s d) -> p s d", s=2)

        l1_max = sem("l1_max_ready")
        l1_probs = sem("l1_probs_ready")
        l1_pv = sem("l1_pv_done")
        l1_inv = sem("l1_inverse_sums_ready")
        kvq_copied = sem("q_k_v_copied")
        mask_step = sem("l1_mask_step")
        mask_ready = sem("l1_mask_ready")
        gate_step = sem("l1_gate_step")
        gate_exp = sem("l1_gate_exp_ready")
        gates_ready = sem("l1_gates_ready")
        acc_step = sem("l1_sum_step")
        out_ready = sem("out_rows_ready")
        out_stored = sem("out_stored")
        GATE_STEPS = 17

        def F_pool(it):
            pool, g = nc.gpsimd, nc.gpsimd
            if not isinstance(it, int) or it > 0:
                filled(pool, Fp, it - 1, ("O", 1))
            two = bass.ds(it * 2, 2)
            g.tensor_copy(q_s, qT_all[:, :, two, :])
            g.tensor_copy(k_s, kT_all[:, two, :])
            g.tensor_copy(v_s[:, :, 0, :], kv_old[:, two, P:])
            g.tensor_copy(v_s[:, :, 1, :], kv_new[:, two, P:]).then_inc(kvq_copied, 1)

        def F_pe(it):
            pe, te = nc.tensor, nc.tensor
            pe.wait_ge(kvq_copied, it + 1)

            def scores(n):
                s, g = n // 4, n % 4
                b = claim(Fp, it, ("S", n))
                for cc in range(C1):
                    last = te.matmul(b[:, cc * 256:(cc + 1) * 256], q_s[32 * g:32 * g + 32, cc, s, :],
                                     k_s[32 * g:32 * g + 32, s, :], start=True, stop=True)
                last.then_inc(full_sem(Fp, ("S", n)), 1)

            def transpose_probs(n):
                pe.wait_ge(l1_probs, it * NL + (n + 1))
                b = claim(Fp, it, ("T", n))
                for i in range(4):
                    last = te.transpose(b[:, i * P:(i + 1) * P], probs[:, n % 3, i * P:(i + 1) * P], ident)
                last.then_inc(full_sem(Fp, ("T", n)), 1)

            def values(n):
                s, g = n // 4, n % 4
                drained(pe, Fp, it, ("T", n))
                b = claim(Fp, it, ("O", s)) if g == 0 else bank[6 + s]
                for cc in range(C1):
                    for i in range(2):
                        last = te.matmul(b[:, cc * P + g * HD1:cc * P + (g + 1) * HD1],
                                         probsT[:, n % 2, (2 * cc + i) * P:(2 * cc + i + 1) * P],
                                         v_s[:, s, i, g * HD1:(g + 1) * HD1], start=(i == 0), stop=(i == 1))
                last.then_inc(l1_pv if g < 3 else full_sem(Fp, ("O", s)), 1)

            def transpose_rows(use, s, src):
                b = claim(Fp, it, (use, s))
                for k in range(KC):
                    last = te.transpose(b[:, k * P:(k + 1) * P], src[:, s, k * P:(k + 1) * P], ident)
                last.then_inc(full_sem(Fp, (use, s)), 1)

            def out_proj(s):
                drained(pe, Fp, it, ("OT", s))
                b = claim(Fp, it, ("Y", s))
                for k in range(KC):
                    last = te.matmul(b[:, 0:256], oT[:, k, s * P:(s + 1) * P], wo_1[:, k, :], start=(k == 0), stop=(k == KC - 1))
                last.then_inc(full_sem(Fp, ("Y", s)), 1)

            for n in range(NL + 3):
                if n < NL:
                    scores(n)
                if 0 <= n - 2 < NL:
                    transpose_probs(n - 2)
                if 0 <= n - 3:
                    values(n - 3)
                if n == 8:
                    drained(pe, Fp, it, ("O", 0))
                    transpose_rows("OT", 0, o_sb)
                if n == 9:
                    out_proj(0)
            drained(pe, Fp, it, ("O", 1))
            transpose_rows("OT", 1, o_sb)
            drained(pe, Fp, it, ("Y", 0))
            transpose_rows("XT", 0, y_sb)
            out_proj(1)
            drained(pe, Fp, it, ("Y", 1))
            transpose_rows("XT", 1, y_sb)
            drained(pe, Fp, it, ("XT", 0))
            drained(pe, Fp, it, ("XT", 1))
            b = claim(Fp, it, "logit")
            for s in range(2):
                for k in range(KC):
                    last = te.matmul(b[:, s * E1:(s + 1) * E1], xnT[:, k, s * P:(s + 1) * P], gate1[:, k, :],
                                     start=(k == 0), stop=(k == KC - 1))
            last.then_inc(full_sem(Fp, "logit"), 1)

            def up(hp):
                b = claim(Fp, it, ("H", hp))
                for i in range(2):
                    for k in range(KC):
                        last = te.matmul(b[:, i * 256:(i + 1) * 256], w1_1[:, 2 * hp + i, k, :], xnT[:, k, :],
                                         start=(k == 0), stop=(k == KC - 1))
                last.then_inc(full_sem(Fp, ("H", hp)), 1)

            up(0)
            up(1)
            pe.wait_ge(gates_ready, it + 1)
            b = claim(Fp, it, "gatesT")
            for s in range(2):
                last = te.transpose(b[0:9, s * P:(s + 1) * P], gates[:, s, 0:9], ident)
            last.then_inc(full_sem(Fp, "gatesT"), 1)
            up(2)
            up(3)
            b = claim(Fp, it, "SH")
            for i in range(2):
                for k in range(KC):
                    last = te.matmul(b[:, i * 256:(i + 1) * 256], sw1[:, k, i * P:(i + 1) * P], xnT[:, k, :],
                                     start=(k == 0), stop=(k == KC - 1))
            last.then_inc(full_sem(Fp, "SH"), 1)

            def down(e):
                drained(pe, Fp, it, ("H", e // 2))
                b = claim(Fp, it, ("E", e))
                for s in range(2):
                    last = te.matmul(b[:, s * 256:(s + 1) * 256], hT[:, e, s * P:(s + 1) * P], w2_1[:, e, :], start=True, stop=True)
                last.then_inc(full_sem(Fp, ("E", e)), 1)

            drained(pe, Fp, it, "gatesT")
            drained(pe, Fp, it, "SH")
            b = claim(Fp, it, "SY")
            for s in range(2):
                for k in range(2):
                    te.matmul(b[:, s * 256:(s + 1) * 256], shT[:, k, s * P:(s + 1) * P], sw2[:, k, :], start=(k == 0), stop=False)
                last = te.matmul(b[:, s * 256:(s + 1) * 256], gatesT[:, s, :], b2_s, start=False, stop=True)
            last.then_inc(full_sem(Fp, "SY"), 1)
            for e in range(E1):
                down(e)

        def F_dve(it):
            dve, v = nc.vector, nc.vector
            if not isinstance(it, int) or it > 0:
                drained(dve, Fp, it - 1, ("S", NL - 1))
            for s in range(2):
                v.tensor_scalar(mask_s[:, s, 0:P], c("key_row"), early[:, bass.ds(it * 2 + s, 1)], NEG, ALU.is_lt, ALU.mult)\
                    .then_inc(mask_step, 1)
                v.tensor_copy(mask_s[:, s, P:], c("causal"))
                dve.wait_ge(mask_step, it * 2 + (s + 1))
                v.tensor_tensor(mask_s[:, s, 0:P], mask_s[:, s, 0:P], c("older"), ALU.add).then_inc(mask_ready, 1)
            dve.wait_ge(mask_ready, it * 2 + 2)

            def mask_max(n):
                s = n // 4
                b, cnt = Fp.count(it, ("S", n))
                dve.wait_ge(bank_full[b], cnt + 1)
                wait(dve, l1_probs, it * NL + (n - 1))
                carry_waits(v)
                for cc in range(C1):
                    last = v.tensor_tensor_reduce(out=masked[:, n % 2, cc * 256:(cc + 1) * 256], in0=bank[b][:, cc * 256:(cc + 1) * 256],
                                                  in1=mask_s[:, s, :], scale=1.0, scalar=-3.0e38, op0=ALU.add, op1=ALU.max,
                                                  accum_out=row_max[:, n % 2, cc:cc + 1])
                last.then_inc(bank_free[b], 1)
                dve.wait_ge(bank_free[b], cnt + 1)
                v.tensor_scalar(neg_max[:, n % 3, 0:C1], row_max[:, n % 2, 0:C1], -(256.0 ** -0.5), None, ALU.mult).then_inc(l1_max, 1)

            def probsT_copy(n):
                b = filled(dve, Fp, it, ("T", n))
                if n >= 2:
                    s, g = (n - 2) // 4, (n - 2) % 4
                    if g < 3:
                        dve.wait_ge(l1_pv, it * 6 + (3 * s + g + 1))
                    else:
                        filled(dve, Fp, it, ("O", s))
                v.tensor_copy(probsT[:, n % 2, :], b[:, :]).then_inc(free_sem(Fp, ("T", n)), 1)

            def norm(s):
                dve.wait_ge(l1_probs, it * NL + (4 * s + 4))
                v.reciprocal(row_inv[:, s, 0:8], row_sum[:, s, 0:8]).then_inc(l1_inv, 1)
                dve.wait_ge(l1_inv, it * 2 + (s + 1))
                b = filled(dve, Fp, it, ("O", s))
                v.tensor_tensor(o_sb[:, s, :].rearrange("p (h d) -> p h d", h=8), b[:, 0:256].rearrange("p (h d) -> p h d", h=8),
                                row_inv[:, s, 0:8].unsqueeze(2).broadcast_to([P, 8, HD1]), ALU.mult).then_inc(free_sem(Fp, ("O", s)), 1)

            def halves_copy(use, s, dst):
                b = filled(dve, Fp, it, (use, s))
                v.tensor_copy(dst[:, :, s * P:(s + 1) * P], b[:, 0:256].rearrange("p (a b) -> p a b", a=2))\
                    .then_inc(free_sem(Fp, (use, s)), 1)

            for n in range(NL + 2):
                if n < NL:
                    mask_max(n)
                if 0 <= n - 2:
                    probsT_copy(n - 2)
                if n == 7:
                    norm(0)
                if n == 9:
                    halves_copy("OT", 0, oT)
            norm(1)
            halves_copy("OT", 1, oT)
            halves_copy("XT", 0, xnT)
            halves_copy("XT", 1, xnT)
            steps = [0]

            def link(ins):
                steps[0] += 1
                ins.then_inc(gate_step, 1)
                dve.wait_ge(gate_step, it * GATE_STEPS + steps[0])

            b = filled(dve, Fp, it, "logit")
            v.tensor_copy(lg1, b[:, 0:16].rearrange("p (s e) -> p s e", s=2)).then_inc(free_sem(Fp, "logit"), 1)
            drained(dve, Fp, it, "logit")
            top2(lg1, 2, link)
            dve.wait_ge(gate_exp, it + 1)
            top2_probs(2, link)
            link(v.tensor_tensor(gtmp, route["one1"][:, 0:2, :], p12[:, 0, 0:2].unsqueeze(2).broadcast_to([P, 2, E1]), ALU.mult))
            link(v.tensor_tensor(gates[:, :, 0:E1], route["one2"][:, 0:2, :], p12[:, 1, 0:2].unsqueeze(2).broadcast_to([P, 2, E1]), ALU.mult))
            v.memset(gates[:, :, E1:E1 + 1], 1.0)
            v.tensor_tensor(gates[:, :, 0:E1], gates[:, :, 0:E1], gtmp, ALU.add).then_inc(gates_ready, 1)
            assert steps[0] == GATE_STEPS
            b = filled(dve, Fp, it, "gatesT")
            v.tensor_copy(gatesT, b[0:9, 0:256].rearrange("p (s q) -> p s q", s=2)).then_inc(free_sem(Fp, "gatesT"), 1)
            b = filled(dve, Fp, it, "SY")
            v.tensor_tensor(acc[:, :, :], b[:, :].rearrange("p (s d) -> p s d", s=2), h_all[:, bass.ds(it * 2, 2), :], ALU.add)\
                .then_inc(free_sem(Fp, "SY"), 1)
            drained(dve, Fp, it, "SY")
            dve.wait_ge(gates_ready, it + 1)
            for e in range(E1):
                b = filled(dve, Fp, it, ("E", e))
                if e > 0:
                    drained(dve, Fp, it, ("E", e - 1))
                if e == E1 - 1:
                    wait(dve, out_stored, it * 16)
                for s in range(2):
                    last = v.scalar_tensor_tensor((acc if e < E1 - 1 else out_s)[:, s, :], b[:, s * 256:(s + 1) * 256],
                                                  gates[:, s, e:e + 1], acc[:, s, :], ALU.mult, ALU.add)
                last.then_inc(free_sem(Fp, ("E", e)), 1)

        def F_act(it):
            act, a = nc.scalar, nc.scalar
            for n in range(NL):
                act.wait_ge(l1_max, it * NL + (n + 1))
                if n >= 3:
                    filled(act, Fp, it, ("T", n - 3))
                for cc in range(C1):
                    h = cc * G1 + n % 4
                    last = a.activation(probs[:, n % 3, cc * 256:(cc + 1) * 256], masked[:, n % 2, cc * 256:(cc + 1) * 256],
                                        ACT.Exp, bias=neg_max[:, n % 3, cc:cc + 1], scale=256.0 ** -0.5,
                                        accum_out=row_sum[:, n // 4, h:h + 1])
                last.then_inc(l1_probs, 1)
            for s in range(2):
                b = filled(act, Fp, it, ("Y", s))
                a.activation(y_sb[:, s, :], b[:, 0:256], ACT.Copy).then_inc(free_sem(Fp, ("Y", s)), 1)
            act.wait_ge(gate_step, it * GATE_STEPS + 12)
            a.activation(pexp[:, 1, 0:2], pexp[:, 0, 0:2], ACT.Exp).then_inc(gate_exp, 1)
            for hp in range(4):
                b = filled(act, Fp, it, ("H", hp))
                for i in range(2):
                    e = 2 * hp + i
                    last = a.activation(hT[:, e, :], b[:, i * 256:(i + 1) * 256], ACT.Gelu, bias=b1_s[:, e:e + 1])
                last.then_inc(free_sem(Fp, ("H", hp)), 1)
            b = filled(act, Fp, it, "SH")
            for i in range(2):
                last = a.activation(shT[:, i, :], b[:, i * 256:(i + 1) * 256], ACT.Gelu, bias=sb1_s[:, i:i + 1])
            last.then_inc(free_sem(Fp, "SH"), 1)

        def F_store(it):
            sp = nc.sync
            drained(sp, Fp, it, ("E", E1 - 1))
            sp.dma_start(out[bass.ds(it * 2, 2), :, :].rearrange("s p d -> p s d"), out_s[:, :, :]).then_inc(out_stored, 16)

        def loop(eng, body, n):
            body(0)
            with eng.Fori(1, n) as it:
                body(it)

        block = ctx.enter_context(nc.Block())

        @block.sync
        def _(sp):
            sp.dma_start(const[:, :], t["const"]).then_inc(consts_loaded, 16)
            sp.dma_start(kvl[:, :], t["kv_lens"].rearrange("(o n) -> o n", o=1).broadcast_to([P, NSEQ])).then_inc(kvl_loaded, 16)
            sp.dma_start(x_in[:, :, :], t["x"][0:2, :, :].rearrange("s p d -> p s d")).then_inc(x_loaded, 16)
            for i, n in enumerate(("cWq", "cWk", "cWv", "cWo")):
                sp.dma_start(w_c[:, i, :, :], t[n].rearrange("(c p) n -> p c n", p=P)).then_inc(cond_w_loaded, 16)
            sp.dma_start(beta[:, :], t["cond_1"].rearrange("b o -> o b").broadcast_to([P, NSEQ])).then_inc(cond_w_loaded, 16)
            sp.dma_start(norm1[:, :], t["norm1"].rearrange("(c p) -> p c", p=P), allow_slow_non_contiguous=True).then_inc(cond_w_loaded, 16)
            sp.dma_start(norm2[:, :], t["norm2"].rearrange("(c p) -> p c", p=P), allow_slow_non_contiguous=True).then_inc(cond_w_loaded, 16)
            sp.dma_start(gate0[:, :, :], t["gate0"].rearrange("(c p) n -> p c n", p=P)).then_inc(cond_w_loaded, 16)
            sp.dma_start(w_kv[:, 1, :, :], t["wv"].rearrange("(c p) n -> p c n", p=P)).then_inc(attn_w_loaded, 16)
            sp.dma_start(w_kv[:, 0, :, :], t["wk"].rearrange("(c p) n -> p c n", p=P)).then_inc(attn_w_loaded, 16)
            sp.dma_start(wq, t["wq"].rearrange("(c p) n -> p c n", p=P)).then_inc(attn_w_loaded, 16)
            sp.dma_start(wo, t["wo"].rearrange("(h p) n -> p h n", p=P)).then_inc(attn_w_loaded, 16)
            sp.wait_ge(zero_ready, 1)
            zero_rows = xs_d.rearrange("(i p) d -> p i d", p=P)
            for a in range(0, TILES0, NSEQ):
                z = min(a + NSEQ, TILES0)
                sp.dma_start(zero_rows[:, a:z, :], kv_old[:, 0:z - a, :]).then_inc(zero_filled, 16)
            sp.wait_ge(kvl_loaded, 16)
            for b in range(NSEQ):
                n = sp.value_load(kvl[0:1, b:b + 1], min_val=0, max_val=NBLK * BLOCK - P)
                sp.dma_start(cs_all[:, b, :], t["rope"][bass.ds(n, P), :]).then_inc(rope_loaded, 16)

            def next_x(it):
                filled(sp, A, it, "xT")
                sp.dma_start(x_in[:, :, :], t["x"][bass.ds((it + 1) * 2, 2), :, :].rearrange("s p d -> p s d"))\
                    .then_inc(x_loaded, 16)

            next_x(0)
            for w, n in enumerate(("w1", "w3")):
                for e in range(E0):
                    sp.dma_start(w13[:, w, e, :, :], t[n][e, :, :].rearrange("(c p) n -> p c n", p=P)).then_inc(expert_w_loaded, 16)
            with sp.Fori(1, PAIRS - 1) as it:
                next_x(it)
            drained(sp, A, PAIRS - 1, "logit")
            for e in range(E0):
                sp.dma_start(w2e[:, e, :, :], t["w2"][e, :, :].rearrange("(c p) n -> p c n", p=P)).then_inc(w2_loaded, 16)
            sp.wait_ge(scattered, 16 * 2 * NSEQ)
            C_load(0, 0)
            C_load(0, 1)
            C_load(0, 2)

            def step(j, k):
                C_load(j, k + 2)
                C_store(j, k - 1)

            step(0, 1)
            sp.dma_start(w_qkv, t["Wqkv1"].rearrange("(c p) n -> p c n", p=P)).then_inc(l1_loaded, 16)
            sp.dma_start(norm_w[:, 0:NQK * HD1], t["qk_scale"].rearrange("(o n) -> o n", o=1).broadcast_to([P, NQK * HD1])).then_inc(l1_loaded, 16)
            sp.dma_start(w1_1, t["l1w1"].rearrange("e (c p) n -> p e c n", p=P)).then_inc(l1_loaded, 16)
            sp.dma_start(w2_1, t["l1w2"].rearrange("e p n -> p e n")).then_inc(l1_loaded, 16)
            sp.dma_start(sw1, t["sw1"].rearrange("(c p) n -> p c n", p=P)).then_inc(l1_loaded, 16)
            sp.dma_start(sw2, t["sw2"].rearrange("(c p) n -> p c n", p=P)).then_inc(l1_loaded, 16)
            sp.dma_start(wo_1, t["Wo1"].rearrange("(c p) n -> p c n", p=P)).then_inc(l1_loaded, 16)
            sp.dma_start(gate1, t["gate1"].rearrange("(c p) n -> p c n", p=P)).then_inc(l1_loaded, 16)
            sp.dma_start(b1_s, t["b1"].rearrange("e p -> p e"), allow_slow_non_contiguous=True).then_inc(l1_loaded, 16)
            sp.dma_start(sb1_s, t["sb1"].rearrange("(c p) -> p c", p=P), allow_slow_non_contiguous=True).then_inc(l1_loaded, 16)
            sp.dma_start(b2_s[0:8, :], t["b2"]).then_inc(l1_loaded, 16)
            sp.dma_start(b2_s[8:9, :], t["sb2"].rearrange("(o n) -> o n", o=1)).then_inc(l1_loaded, 16)
            step(0, 2)
            with sp.Fori(1, STEPS - 1) as j:
                step(j, 1)
                step(j, 2)
            C_store(STEPS - 1, 0)
            C_store(STEPS - 1, 1)
            C_store(STEPS - 1, 2)
            sp.dma_start(x_in[:, :, :], t["x"][0:2, :, :].rearrange("s p d -> p s d")).then_inc(x_again, 16)
            D_store(0)
            with sp.Fori(1, PAIRS - 1) as it:
                D_store(it)
            D_store(PAIRS - 1)
            loop(sp, F_store, PAIRS)
            for i in range(2):
                sp.wait_ge(row_stored[i], 16 * ((TILES0 + 1 - i) // 2))
            sp.wait_ge(kv_stored, 16 * NSEQ)
            sp.wait_ge(zero_filled, 48)
            sp.wait_ge(scattered, 16 * 2 * NSEQ)
            sp.wait_ge(written_out, 16)
            sp.wait_ge(out_stored, 16 * PAIRS)

        @block.gpsimd
        def _(pool):
            nc.gpsimd.memset(neg_half[:, :], -0.5).then_inc(neg_half_ready, 1)
            pool.wait_ge(neg_half_ready, 1)
            pool.wait_ge(consts_loaded, 16)
            places_pool()
            loop(pool, A_pool, PAIRS)
            B_pool()
            cache_pool()
            D_gather()
            pool.wait_ge(rope_loaded, 16 * NSEQ)
            loop(pool, D_pool, PAIRS)
            E_pool()
            for b in range(NSEQ):
                pool.wait_ge(kv_gathered[b], 32)
            drained(pool, E, 0, ("kT", PAIRS - 1))
            loop(pool, F_pool, PAIRS)

        @block.scalar
        def _(act):
            act.wait_ge(beta_ready, 1)
            loop(act, A_act, PAIRS)
            B_act()

            def first():
                C_act_step(0, 0)

            C_run(act, first, C_act_step, lambda: (C_act_step(STEPS - 1, 2), C_act_down(STEPS - 1, 2)))
            loop(act, D_act, PAIRS)
            act.wait_ge(l1_loaded, 16 * 12)
            loop(act, F_act, PAIRS)

        @block.vector
        def _(dve):
            dve.wait_ge(consts_loaded, 16)
            places_dve()
            dve.wait_ge(cond_w_loaded, 128)
            nc.vector.tensor_scalar(beta[:, :], beta[:, :], 4.0, CHD ** -0.5, ALU.min, ALU.mult).then_inc(beta_ready, 1)
            loop(dve, A_dve, PAIRS)
            B_dve()
            dve.wait_ge(written_in, 32)

            def first():
                C_rowsT_copy(0, 0)
                C_dve_step(0, 0)

            C_run(dve, first, C_dve_step, lambda: (C_dve_step(STEPS - 1, 2, more=False), C_hidT_copy(STEPS - 1, 2)))
            winners_dve()
            dve.wait_ge(l1_loaded, 16 * 12)
            dve.wait_ge(rope_loaded, 16 * NSEQ)
            nc.vector.tensor_scalar(norm_w[:, 0:NQK * HD1], norm_w[:, 0:NQK * HD1], 1.0, None, ALU.add).then_inc(norm_w_ready, 1)
            dve.wait_ge(norm_w_ready, 1)
            dve.wait_ge(y_gathered, 16 * 2 * NSEQ)
            loop(dve, D_dve, PAIRS)
            E_dve()
            loop(dve, F_dve, PAIRS)

        @block.tensor
        def _(pe):
            pe.wait_ge(consts_loaded, 16)
            pe.wait_ge(cond_w_loaded, 128)
            loop(pe, A_pe, PAIRS)
            B_pe()
            pe.wait_ge(expert_w_loaded, 16 * 2 * E0)
            pe.wait_ge(tile_e_ready, 1)

            def first():
                C_transpose_rows(0, 0)
                C_pe_step(0, 0)
                pe.wait_ge(w2_loaded, 16 * E0)

            C_run(pe, first, C_pe_step, lambda: (C_pe_step(STEPS - 1, 2, more=False), C_transpose_hidden(STEPS - 1, 2),
                                                 C_down(STEPS - 1, 2)))
            pe.wait_ge(l1_loaded, 16 * 12)
            loop(pe, D_pe, PAIRS)
            E_pe()
            loop(pe, F_pe, PAIRS)


def constants(np):
    a = {k: np.zeros((P, w), np.float32) for k, w in CONST_COLS.items()}
    i = np.arange(P)
    a["ident"][:] = np.eye(P)
    a["causal"][:] = np.where(i[None, :] <= i[:, None], 0.0, NEG)
    a["older"][:] = np.where(i[None, :] > i[:, None], 0.0, NEG)
    inv = (1.0 / np.float32(1000000.0) ** (np.arange(0, FHD, 2, dtype=np.float32) / np.float32(FHD))).astype(np.float32)
    ang = i.astype(np.float32)[None, :] * inv[:, None]
    a["cos"][:] = np.concatenate([np.cos(ang), np.cos(ang)])
    a["sin"][:] = np.concatenate([-np.sin(ang), np.sin(ang)])
    a["ones"][:] = 1.0
    a["before"][:] = i[:, None] < i[None, :]
    a["key_row"][:] = i[None, :]
    a["expert"][:] = np.tile(np.arange(8), 8)[None, :]
    a["expert8"][:] = np.tile(np.arange(8) + 8, 8)[None, :]
    a["below"][:] = np.tril(np.ones((8, 8)), -1).reshape(1, 64)
    a["tile_no"][:] = np.repeat(np.arange(TILES0), E0)[None, :]
    a["even"][:, 0] = (i // CHD) % 2 == 0
    a["odd"][:, 0] = (i // CHD) % 2 == 1
    a["row"][:, 0] = i
    a["seq_base"][:] = np.tile(np.arange(NSEQ) * NBLK, 2)[None, :]
    return np.ascontiguousarray(np.concatenate([a[k] for k in CONST_COLS], axis=1))


def kernel(**inputs):
    import numpy as np
    import concourse.bacc as bacc
    from concourse import mybir as mb
    from concourse.bass_utils import run_bass_kernel_spmd

    nc = bacc.Bacc("TRN2", target_bir_lowering=False, num_devices=1)
    g = {k: np.asarray(v) for k, v in inputs.items()}
    arrays = {"const": constants(np), "x": g["x"], "cond_1": g["cond_1"]}
    for n in ("Wq", "Wk", "Wv", "Wo"):
        arrays["c" + n] = np.ascontiguousarray(g["L0_cond_" + n].T)
    for n, k in (("norm1", "norm1_w"), ("norm2", "norm2_w"), ("wq", "wq"), ("wk", "wk"), ("wv", "wv"), ("wo", "wo"),
                 ("gate0", "gate_w"), ("w1", "w1"), ("w3", "w3"), ("w2", "w2")):
        arrays[n] = np.ascontiguousarray(g["L0_ffn_" + k])
    wq1 = g["L1_cond_Wq"].reshape(G1, C1, HD1, D).transpose(1, 0, 2, 3).reshape(D, D)
    arrays["Wqkv1"] = np.ascontiguousarray(np.concatenate([wq1, g["L1_cond_Wk"], g["L1_cond_Wv"]], axis=0).T)
    arrays["Wo1"] = np.ascontiguousarray(g["L1_cond_Wo"].reshape(D, G1, C1, HD1).transpose(2, 1, 3, 0).reshape(D, D))
    arrays["qk_scale"] = np.concatenate([np.tile(g["L1_cond_q_norm_scale"], 8), np.tile(g["L1_cond_k_norm_scale"], G1)])
    arrays["k_blocks"], arrays["v_blocks"] = g["L1_cond_k_blocks"], g["L1_cond_v_blocks"]
    arrays["table"] = g["itok_Bx257_0_4111"].reshape(NSEQ * NBLK, 1)
    arrays["kv_lens"] = g["itok_B_37_3939"]
    for n, k in (("gate1", "gate_w"), ("l1w1", "w1"), ("b1", "b1"), ("l1w2", "w2"), ("b2", "b2"), ("sw1", "shared_w1"),
                 ("sb1", "shared_b1"), ("sw2", "shared_w2"), ("sb2", "shared_b2")):
        arrays[n] = np.ascontiguousarray(g["L1_ffn_" + k])
    inv = (1.0 / np.float32(10000.0) ** (np.arange(HD1 // 2, dtype=np.float32) / np.float32(HD1 // 2))).astype(np.float32)
    ang = np.arange(NBLK * BLOCK, dtype=np.float32)[:, None] * inv[None, :]
    arrays["rope"] = np.concatenate([np.cos(ang), np.sin(ang)], axis=1).astype(np.float32)
    arrays["row_no"] = np.arange(1, NSEQ * P + 1, dtype=np.float32)
    t = {n: nc.dram_tensor("in_" + n, a.shape, mb.dt.from_np(a.dtype), kind="ExternalInput").ap() for n, a in arrays.items()}
    out = nc.dram_tensor("out", (NSEQ, P, D), mb.dt.float32, kind="ExternalOutput").ap()
    program(nc, t, out)
    r = run_bass_kernel_spmd(nc, [{"in_" + n: a for n, a in arrays.items()}], core_ids=[0])
    return r.results[0]["out"]
```

```python
import concourse.bass as bass
from concourse import mybir
from concourse.alu_op_type import AluOpType as ALU
from contextlib import ExitStack

P = 128
NSEQ, D = 8, 256
KC = D // P
PAIRS = NSEQ // 2
CH, CHD = 16, 16
FH, FKV, FHD = 16, 4, 128
E0, F0 = 8, 512
TILES0 = (2 * NSEQ * P + E0 * (P - 1)) // P
G1, HD1 = 4, 32
C1 = 2
NBLK, BLOCK = 257, 16
E1, H1 = 8, 128
SH1 = 2 * H1
NEG = -1.0e30

CONST_COLS = dict(ident=P, causal=P, older=P, cos=P, sin=P, ones=P, before=P, key_row=P, expert=64,
                  expert8=64, below=64, tile_no=TILES0 * E0, even=1, odd=1, row=1, seq_base=16)
CONST_AT, _n = {}, 0
for _k, _w in CONST_COLS.items():
    CONST_AT[_k] = (_n, _w)
    _n += _w
CONST_N = _n


class Banks:

    def __init__(self, uses, before, times):
        self.base = list(before)
        self.per = [0] * 8
        self.at = {}
        for use, bank in uses:
            self.at[use] = (bank, self.per[bank])
            self.per[bank] += 1
        self.after = [b + times * p for b, p in zip(before, self.per)]

    def count(self, it, use):
        bank, k = self.at[use]
        return bank, it * self.per[bank] + (self.base[bank] + k)


class TileBanks:

    RINGS = dict(up=(0, 2), gate=(2, 2), hT=(4, 1), xT=(5, 1), down=(6, 2))

    def __init__(self, before, tiles):
        self.base = list(before)
        self.after = list(before)
        for first, ring in self.RINGS.values():
            for i in range(tiles):
                self.after[first + i % ring] += 1

    def count(self, j, use):
        name, c = use
        first, ring = self.RINGS[name]
        b = first + c % ring
        return b, (j + (self.base[b] + c // 2) if ring == 2 else j * 2 + (self.base[b] + c))


def program(nc, t, out):
    fp32, i32 = mybir.dt.float32, mybir.dt.int32
    ACT = mybir.ActivationFunctionType
    AX = mybir.AxisListType
    ctx = ExitStack()
    with ctx:
        def sb(name, shape, dt=fp32):
            return ctx.enter_context(nc.sbuf_tensor(name, shape, dt))

        def sem(name):
            return ctx.enter_context(nc.semaphore(name))

        bank = [ctx.enter_context(nc.psum_tensor(f"bank{i}", [P, 512], fp32)) for i in range(8)]
        bank_full = [sem(f"bank_full{i}") for i in range(8)]
        bank_free = [sem(f"bank_free{i}") for i in range(8)]

        xs_d = nc.dram_tensor("routed_rows", [TILES0 * P, D], fp32, kind="Internal").ap()
        ys_d = nc.dram_tensor("expert_rows", [TILES0 * P, D], fp32, kind="Internal").ap()
        kv_d = nc.dram_tensor("new_kv_rows", [NSEQ * P, D], fp32, kind="Internal").ap()
        wl_d = nc.dram_tensor("written_places", [NSEQ * P], fp32, kind="Internal").ap()

        const = sb("const", [P, CONST_N])

        def c(name):
            a, w = CONST_AT[name]
            return const[:, a:a + w]

        ident = c("ident")
        w_c = sb("cond_weights", [P, 4, KC, D])
        w_kv = sb("ffn_wk_wv", [P, 2, KC, FKV * FHD])
        w_qo = sb("ffn_wq_wo", [P, 8192])
        wq = w_qo[:, 0:4096].rearrange("p (c n) -> p c n", c=KC)
        wo = w_qo[:, 4096:8192].rearrange("p (h n) -> p h n", h=FH)
        w2e = w_qo[:, :].rearrange("p (e c n) -> p e c n", e=E0, c=F0 // P)
        w13 = sb("experts_w1_w3", [P, 2, E0, KC, F0])
        gate0 = sb("gate0", [P, KC, E0])
        norm1 = sb("norm1", [P, KC])
        norm2 = sb("norm2", [P, KC])
        beta = sb("beta", [P, NSEQ])
        x_in = sb("x_in", [P, 2, D])
        xT = sb("xT", [P, KC, 2 * P])
        cqT = sb("cond_qT", [P, KC, 2 * P])
        ckT = sb("cond_kT_masked", [P, KC, 2, 2 * P])
        cv = sb("cond_v", [P, 2, D])
        masked = sb("masked_scores", [P, 2, 512])
        probs = sb("probs", [P, 3, 512])
        probsT = sb("probsT", [P, 2, 512])
        o_sb = sb("attn_rows", [P, 2, D])
        oT = sb("attn_rowsT", [P, KC, 2 * P])
        y_sb = sb("cond_out", [P, 2, D])
        xn = sb("normed", [P, 2, D])
        xnT = sb("normedT", [P, KC, 2 * P])
        fqT = sb("ffn_qT", [P, 2, 4, 2 * P])
        fkT = sb("ffn_kT", [P, FKV, 2 * P])
        fv = sb("ffn_v", [P, 2, 512])
        swapped = sb("swapped", [P, 2, 512])
        foT = sb("ffn_oT", [P, 2, 512])
        junk = swapped[:, 0, 0:D]
        h_all = sb("h_all", [P, NSEQ, D])
        logits = sb("logits", [P, NSEQ, E0])
        row_max = sb("row_max", [P, 2, 4])
        neg_max = sb("neg_max", [P, 3, 4])
        row_sum = sb("row_sum", [P, 2, 16])
        row_inv = sb("row_inv", [P, 2, 16])
        fsum = sb("ffn_row_sum", [P, 3, 4])
        finv = sb("ffn_row_inv", [P, 3, 4])
        sq = sb("sum_squares", [P, 4])
        ms = sb("mean_squares", [P, 4])
        rstd = sb("rstd", [P, 4])
        rstd2 = sb("rstd2_all", [P, NSEQ])
        neg_half = sb("neg_half", [P, 16])
        carrier = sb("carrier", [1, 1])
        cos_b = c("cos")
        sin_b = c("sin")
        kv_old = sb("kv_old", [P, NSEQ, D])
        kv_new = sb("kv_new", [P, NSEQ, D])

        consts_loaded = sem("consts_loaded")
        neg_half_ready = sem("neg_half_ready")
        beta_ready = sem("beta_ready")
        cond_w_loaded = sem("cond_w_loaded")
        attn_w_loaded = sem("attn_w_loaded")
        expert_w_loaded = sem("expert_w_loaded")
        x_loaded = sem("x_loaded")

        def wait(eng, s, value):
            if not isinstance(value, int) or value > 0:
                eng.wait_ge(s, value)

        def carry_waits(v):
            v.memset(carrier[0:1, 0:1], 0.0)

        def claim(ph, it, use):
            b, n = ph.count(it, use)
            wait(nc.tensor, bank_free[b], n)
            return bank[b]

        def filled(eng, ph, it, use):
            b, n = ph.count(it, use)
            eng.wait_ge(bank_full[b], n + 1)
            return bank[b]

        def drained(eng, ph, it, use):
            b, n = ph.count(it, use)
            wait(eng, bank_free[b], n + 1)

        def full_sem(ph, use):
            return bank_full[ph.count(0, use)[0]]

        def free_sem(ph, use):
            return bank_free[ph.count(0, use)[0]]

        NU = 8
        STEPS_A = NU + 5

        def cond_unit(t):
            return t - 1

        def ffn_unit(t):
            return t - 3

        def ropes_of(t):
            return (2 * t - 2, 2 * t - 1) if t in (1, 2) else (t + 1,) if 3 <= t <= 8 else ()

        NR = 10
        uses = []
        for t_ in range(STEPS_A):
            v_ = cond_unit(t_)
            if t_ == 0:
                uses += [("xT", 2), ("cq", 0), ("ck", 2), ("cv", 3)]
            if 0 <= v_ < NU:
                uses.append((("cS", v_), 0))
            if 0 <= v_ - 1 < NU:
                uses.append((("cT", v_ - 1), 2))
                if (v_ - 1) % 4 == 0:
                    uses.append((("cO", (v_ - 1) // 4), 3))
            uses += {6: [(("cOT", 0), 2)], 7: [(("cY", 0), 2)], 10: [(("cOT", 1), 2), (("xn", 0), 2)],
                     11: [(("cY", 1), 2)], 12: [(("xn", 1), 2)]}.get(t_, [])
        Ac = Banks(uses, [0] * 8, PAIRS)
        uses = [(("fv", 0), 5), (("fv", 1), 1)]
        for t_ in range(STEPS_A):
            u_ = ffn_unit(t_)
            if 0 <= u_ < NU:
                uses.append((("fS", u_), 4))
            uses += [(("rope", r), (5, 1)[r % 2]) for r in ropes_of(t_)]
            if 0 <= u_ - 1 < NU:
                uses += [(("fT", u_ - 1), 6), (("fO", u_ - 1), 6)]
        uses += [("wo", 7), ("x2", 7), ("logit", 7)]
        Af = Banks(uses, [0] * 8, PAIRS)
        after_A = [a + b for a, b in zip(Ac.after, Af.after)]

        cprobs = kv_new[:, 0:6, :].rearrange("p (r a) d -> p r (a d)", r=3)
        y_keep = kv_new[:, 6:8, :]
        cprobsT = masked
        xn2 = kv_old[:, 0:2, :]
        x2T = kv_old[:, 2:4, :]
        junk = kv_old[:, 5, :]
        crow_max = kv_old[:, 4, 0:12].rearrange("p (r h) -> p r h", r=3)
        cneg_max = kv_old[:, 4, 16:28].rearrange("p (r h) -> p r h", r=3)
        frow_max = kv_old[:, 4, 32:44].rearrange("p (r h) -> p r h", r=3)

        cond_max = sem("cond_max_ready")
        cond_probs = sem("cond_probs_ready")
        cond_pv = sem("cond_pv_done")
        cond_inv = sem("cond_inverse_sums_ready")
        y_copied = sem("cond_out_copied")
        y_squares = sem("cond_out_squares_ready")
        y_kept = sem("cond_out_kept")
        y_rstd = sem("cond_out_rstd_ready")
        xn_ready = sem("normed_rows_ready")
        swap_ready = sem("rope_halves_swapped")
        sin_ready = sem("rope_sine_part_ready")
        rope_done = sem("rope_done")
        ffn_max = sem("ffn_max_ready")
        ffn_probs = sem("ffn_probs_ready")
        ffn_inv = sem("ffn_inverse_sums_ready")
        ffn_scaled = sem("ffn_probs_scaled")
        wo_done = sem("wo_step_done")
        h_squares = sem("h_squares_ready")
        h_mean = sem("h_mean_squares_ready")
        h_rstd = sem("h_rstd_ready")
        x2_ready = sem("x2_rows_ready")

        def heads_of(j):
            return [fc * 8 + 2 * j + par for fc in range(2) for par in range(2)]

        def pe_transpose_probs(ph, it, use, n, ready, src):
            pe, te = nc.tensor, nc.tensor
            pe.wait_ge(ready, it * NU + (n + 1))
            b = claim(ph, it, (use, n))
            for i in range(4):
                last = te.transpose(b[:, i * P:(i + 1) * P], src[:, n % 3, i * P:(i + 1) * P], ident)
            last.then_inc(full_sem(ph, (use, n)), 1)

        def pe_transpose_rows(ph, it, use, s, src):
            b = claim(ph, it, (use, s))
            for k in range(KC):
                last = nc.tensor.transpose(b[:, k * P:(k + 1) * P], src[:, s, k * P:(k + 1) * P], ident)
            last.then_inc(full_sem(ph, (use, s)), 1)

        def pe_cond_start(i):
            pe, te = nc.tensor, nc.tensor
            pe.wait_ge(x_loaded, i * 16 + 16)
            b = claim(Ac, i, "xT")
            for k in range(KC):
                for s in range(2):
                    last = te.transpose(b[:, (k * 2 + s) * P:(k * 2 + s + 1) * P], x_in[:, s, k * P:(k + 1) * P], ident)
            last.then_inc(full_sem(Ac, "xT"), 1)

        def pe_cond_proj(i):
            pe, te = nc.tensor, nc.tensor
            drained(pe, Ac, i, "xT")
            for use, w in (("cq", 0), ("ck", 1)):
                b = claim(Ac, i, use)
                for fc in range(KC):
                    for k in range(KC):
                        last = te.matmul(b[:, fc * 256:(fc + 1) * 256], w_c[:, w, k, fc * P:(fc + 1) * P], xT[:, k, :],
                                         start=(k == 0), stop=(k == KC - 1))
                last.then_inc(full_sem(Ac, use), 1)
            b = claim(Ac, i, "cv")
            for s in range(2):
                for k in range(KC):
                    last = te.matmul(b[:, s * 256:(s + 1) * 256], xT[:, k, s * P:(s + 1) * P], w_c[:, 2, k, :],
                                     start=(k == 0), stop=(k == KC - 1))
            last.then_inc(full_sem(Ac, "cv"), 1)

        def pe_cond_scores(i, n):
            pe, te = nc.tensor, nc.tensor
            s, j = n // 4, n % 4
            if n == 0:
                drained(pe, Ac, i, "cq")
                drained(pe, Ac, i, "ck")
            b = claim(Ac, i, ("cS", n))
            for fc in range(2):
                last = te.matmul(b[:, fc * 256:(fc + 1) * 256], cqT[32 * j:32 * j + 32, fc, s * P:(s + 1) * P],
                                 ckT[32 * j:32 * j + 32, fc, :, s * P:(s + 1) * P], start=True, stop=True)
            last.then_inc(full_sem(Ac, ("cS", n)), 1)

        def pe_cond_values(i, n):
            pe, te = nc.tensor, nc.tensor
            s, j = n // 4, n % 4
            if n == 0:
                drained(pe, Ac, i, "cv")
            drained(pe, Ac, i, ("cT", n))
            b = claim(Ac, i, ("cO", s)) if j == 0 else bank[3]
            for q, h in enumerate(heads_of(j)):
                last = te.matmul(b[:, h * CHD:(h + 1) * CHD], cprobsT[:, n % 2, q * P:(q + 1) * P],
                                 cv[:, s, h * CHD:(h + 1) * CHD], start=True, stop=True)
            last.then_inc(cond_pv if j < 3 else full_sem(Ac, ("cO", s)), 1)

        def pe_cond_late(i, t_):
            pe, te = nc.tensor, nc.tensor
            if t_ in (6, 10):
                s = (t_ - 6) // 4
                drained(pe, Ac, i, ("cO", s))
                pe_transpose_rows(Ac, i, "cOT", s, o_sb)
            if t_ in (7, 11):
                s = (t_ - 7) // 4
                drained(pe, Ac, i, ("cOT", s))
                b = claim(Ac, i, ("cY", s))
                for k in range(KC):
                    last = te.matmul(b[:, 0:256], oT[:, k, s * P:(s + 1) * P], w_c[:, 3, k, :],
                                     start=(k == 0), stop=(k == KC - 1))
                last.then_inc(full_sem(Ac, ("cY", s)), 1)
            if t_ in (10, 12):
                s = (t_ - 10) // 2
                pe.wait_ge(xn_ready, i * 2 + (s + 1))
                pe_transpose_rows(Ac, i, "xn", s, xn)

        def pe_values_proj(it, s):
            drained(nc.tensor, Ac, it, ("xn", s))
            b = claim(Af, it, ("fv", s))
            for k in range(KC):
                last = nc.tensor.matmul(b[:, :], xnT[:, k, s * P:(s + 1) * P], w_kv[:, 1, k, :],
                                        start=(k == 0), stop=(k == KC - 1))
            last.then_inc(full_sem(Af, ("fv", s)), 1)

        def pe_rope_proj(it, r):
            b = claim(Af, it, ("rope", r))
            for i in range(2):
                for k in range(KC):
                    f = (2 * r + i) * FHD if r < 2 else (2 * (r - 2) + i) * FHD
                    w = w_kv[:, 0, k, f:f + FHD] if r < 2 else wq[:, k, f:f + FHD]
                    last = nc.tensor.matmul(b[:, i * 256:(i + 1) * 256], w, xnT[:, k, :],
                                            start=(k == 0), stop=(k == KC - 1))
            last.then_inc(full_sem(Af, ("rope", r)), 1)

        def pe_ffn_scores(it, n):
            pe, te = nc.tensor, nc.tensor
            g, s = n // 2, n % 2
            if s == 0:
                pe.wait_ge(rope_done, it * NR + (2 * g + 4))
            b = claim(Af, it, ("fS", n))
            for i in range(4):
                last = te.matmul(b[:, i * P:(i + 1) * P], fqT[:, g % 2, i, s * P:(s + 1) * P],
                                 fkT[:, g, s * P:(s + 1) * P], start=True, stop=True)
            last.then_inc(full_sem(Af, ("fS", n)), 1)

        def pe_ffn_values(it, n):
            pe, te = nc.tensor, nc.tensor
            g, s = n // 2, n % 2
            if n < 2:
                drained(pe, Af, it, ("fv", n))
            drained(pe, Af, it, ("fT", n))
            b = claim(Af, it, ("fO", n))
            te.matmul(b[:, :], fv[:, s, g * FHD:(g + 1) * FHD], probsT[:, n % 2, :],
                      start=True, stop=True).then_inc(full_sem(Af, ("fO", n)), 1)

        def pe_ffn_out(it, n):
            pe, te = nc.tensor, nc.tensor
            g, s = n // 2, n % 2
            if n == 0:
                claim(Af, it, "wo")
            drained(pe, Af, it, ("fO", n))
            for i in range(4):
                last = te.matmul(bank[7][:, s * 256:(s + 1) * 256], foT[:, n % 2, i * P:(i + 1) * P],
                                 wo[:, 4 * g + i, :], start=(n == 0 and i == 0), stop=(g == 3 and i == 3),
                                 skip_group_check=True)
            if n == NU - 1:
                last.then_inc(full_sem(Af, "wo"), 1)

        def pe_tail(i, t_):
            pe, te = nc.tensor, nc.tensor
            if t_ == 2:
                pe.wait_ge(x2_ready, i * 2 + 2)
                b = claim(Af, i, "x2")
                for k in range(KC):
                    for s in range(2):
                        last = te.transpose(b[:, (k * 2 + s) * P:(k * 2 + s + 1) * P], xn2[:, s, k * P:(k + 1) * P], ident)
                last.then_inc(full_sem(Af, "x2"), 1)
            if t_ == 3:
                drained(pe, Af, i, "x2")
                b = claim(Af, i, "logit")
                for s in range(2):
                    for k in range(KC):
                        last = te.matmul(b[:, s * E0:(s + 1) * E0], x2T[:, k, s * P:(s + 1) * P], gate0[:, k, :],
                                         start=(k == 0), stop=(k == KC - 1))
                last.then_inc(full_sem(Af, "logit"), 1)

        def A_pe(it, ffn, cond, tail):
            for t_ in range(STEPS_A):
                u, v = ffn_unit(t_), cond_unit(t_)
                if t_ == 0 and cond:
                    pe_cond_start(it + 1)
                if t_ == 0 and ffn:
                    pe_values_proj(it, 0)
                    pe_values_proj(it, 1)
                if t_ == 0 and cond:
                    pe_cond_proj(it + 1)
                if ffn and 0 <= u < NU:
                    pe_ffn_scores(it, u)
                if cond and 0 <= v < NU:
                    pe_cond_scores(it + 1, v)
                if ffn:
                    for r in ropes_of(t_):
                        pe_rope_proj(it, r)
                if ffn and 0 <= u - 1 < NU:
                    pe_transpose_probs(Af, it, "fT", u - 1, ffn_scaled, probs)
                if cond and 0 <= v - 1 < NU:
                    pe_transpose_probs(Ac, it + 1, "cT", v - 1, cond_probs, cprobs)
                if tail:
                    pe_tail(it - 1, t_)
                if ffn and 0 <= u - 2 < NU:
                    pe_ffn_out(it, u - 2)
                if ffn and 0 <= u - 1 < NU:
                    pe_ffn_values(it, u - 1)
                if cond and 0 <= v - 1 < NU:
                    pe_cond_values(it + 1, v - 1)
                if cond:
                    pe_cond_late(it + 1, t_)

        def dve_mask_max(ph, it, use, n, buf, rmax, nmax, scale, ready):
            dve, v = nc.vector, nc.vector
            b = filled(dve, ph, it, (use, n))
            carry_waits(v)
            for i in range(4):
                last = v.tensor_tensor_reduce(out=buf[:, n % 3, i * P:(i + 1) * P], in0=b[:, i * P:(i + 1) * P],
                                              in1=c("causal"), scale=1.0, scalar=-3.0e38, op0=ALU.add, op1=ALU.max,
                                              accum_out=rmax[:, n % 3, i:i + 1])
            last.then_inc(free_sem(ph, (use, n)), 1)
            drained(dve, ph, it, (use, n))
            v.tensor_scalar(nmax[:, n % 3, :], rmax[:, n % 3, :], -scale, None, ALU.mult).then_inc(ready, 1)

        def dve_copy(ph, it, use, dst, src=lambda b: b[:, :]):
            b = filled(nc.vector, ph, it, use)
            nc.vector.tensor_copy(dst, src(b)).then_inc(free_sem(ph, use), 1)

        def halves(b):
            return b[:, 0:256].rearrange("p (a b) -> p a b", a=2)

        def dve_cond_start(i):
            v = nc.vector
            dve_copy(Ac, i, "xT", xT[:, :, :].rearrange("p a b -> p (a b)"))

        def dve_cond_keys(i):
            v = nc.vector
            b = filled(v, Ac, i, "ck")
            bk = b[:, :].rearrange("p (a b) -> p a b", a=2)
            v.tensor_scalar(ckT[:, :, 0, :], bk, c("even"), None, ALU.mult)
            v.tensor_scalar(ckT[:, :, 1, :], bk, c("odd"), None, ALU.mult).then_inc(free_sem(Ac, "ck"), 1)

        def dve_cond_late(i, t_):
            dve, v = nc.vector, nc.vector
            if t_ in (6, 10):
                s = (t_ - 6) // 4
                dve.wait_ge(cond_probs, i * NU + (4 * s + 4))
                v.reciprocal(row_inv[:, s, :], row_sum[:, s, :]).then_inc(cond_inv, 1)
                dve.wait_ge(cond_inv, i * 2 + (s + 1))
                b = filled(dve, Ac, i, ("cO", s))
                v.tensor_tensor(o_sb[:, s, :].rearrange("p (h d) -> p h d", h=CH),
                                b[:, 0:256].rearrange("p (h d) -> p h d", h=CH),
                                row_inv[:, s, :].unsqueeze(2).broadcast_to([P, CH, CHD]), ALU.mult)\
                    .then_inc(free_sem(Ac, ("cO", s)), 1)
            if t_ in (7, 11):
                s = (t_ - 7) // 4
                dve_copy(Ac, i, ("cOT", s), oT[:, :, s * P:(s + 1) * P], halves)
            if t_ in (9, 12):
                s = (t_ - 9) // 3
                dve.wait_ge(y_rstd, i * 2 + (s + 1))
                dve.wait_ge(y_copied, i * 2 + (s + 1))
                v.tensor_scalar(xn[:, s, :], y_sb[:, s, :], rstd[:, s:s + 1], None, ALU.mult).then_inc(xn_ready, 1)

        def dve_xnT(i, s):
            b = filled(nc.vector, Ac, i, ("xn", s))
            for k in range(KC):
                last = nc.vector.tensor_scalar(xnT[:, k, s * P:(s + 1) * P], b[:, k * P:(k + 1) * P], norm1[:, k:k + 1],
                                               None, ALU.mult)
            last.then_inc(free_sem(Ac, ("xn", s)), 1)

        def rope_dst(r):
            if r < 2:
                return fkT[:, 2 * r:2 * r + 2, :].rearrange("p a b -> p (a b)")
            g, i = (r - 2) // 2, (r - 2) % 2
            return fqT[:, g % 2, 2 * i:2 * i + 2, :].rearrange("p a b -> p (a b)")

        def dve_rope_cos(it, r):
            dve, v = nc.vector, nc.vector
            b = filled(dve, Af, it, ("rope", r))
            dve.wait_ge(swap_ready, it * NR + (r + 1))
            v.tensor_tensor(rope_dst(r).rearrange("p (a b) -> p a b", a=4), b[:, :].rearrange("p (a b) -> p a b", a=4),
                            cos_b.unsqueeze(1).broadcast_to([P, 4, P]), ALU.mult).then_inc(free_sem(Af, ("rope", r)), 1)

        def dve_rope_add(it, r):
            dve, v = nc.vector, nc.vector
            drained(dve, Af, it, ("rope", r))
            dve.wait_ge(sin_ready, it * NR + (r + 1))
            v.tensor_tensor(rope_dst(r), rope_dst(r), swapped[:, r % 2, :], ALU.add).then_inc(rope_done, 1)

        def dve_scale_probs(it, n):
            dve, v = nc.vector, nc.vector
            dve.wait_ge(ffn_probs, it * NU + (n + 1))
            v.reciprocal(finv[:, n % 3, :], fsum[:, n % 3, :]).then_inc(ffn_inv, 1)
            dve.wait_ge(ffn_inv, it * NU + (n + 1))
            pr = probs[:, n % 3, :].rearrange("p (a b) -> p a b", a=4)
            v.tensor_tensor(pr, pr, finv[:, n % 3, :].unsqueeze(2).broadcast_to([P, 4, P]), ALU.mult)\
                .then_inc(ffn_scaled, 1)

        def dve_tail(i, t_):
            dve, v = nc.vector, nc.vector
            if t_ == 0:
                b = filled(dve, Af, i, "wo")
                dve.wait_ge(y_kept, i + 1)
                v.tensor_tensor(h_all[:, bass.ds(i * 2, 2), :], b[:, :].rearrange("p (a b) -> p a b", a=2), y_keep,
                                ALU.add).then_inc(free_sem(Af, "wo"), 1)
            if t_ == 1:
                for s in range(2):
                    dve.wait_ge(h_rstd, i * 2 + (s + 1))
                    v.tensor_scalar(xn2[:, s, :], h_all[:, bass.ds(i * 2 + s, 1), :].rearrange("p a b -> p (a b)"),
                                    rstd[:, 2 + s:3 + s], None, ALU.mult).then_inc(x2_ready, 1)
                v.tensor_copy(rstd2[:, bass.ds(i * 2, 2)], rstd[:, 2:4])
            if t_ == 2:
                b = filled(dve, Af, i, "x2")
                for k in range(KC):
                    last = v.tensor_scalar(x2T[:, k, :], b[:, k * 256:(k + 1) * 256], norm2[:, k:k + 1], None, ALU.mult)
                last.then_inc(free_sem(Af, "x2"), 1)
            if t_ == 4:
                dve_copy(Af, i, "logit", logits[:, bass.ds(i * 2, 2), :],
                         lambda b: b[:, 0:2 * E0].rearrange("p (a b) -> p a b", a=2))

        def A_dve(it, ffn, cond, tail):
            for t_ in range(STEPS_A):
                u, v = ffn_unit(t_), cond_unit(t_)
                if tail and t_ == 0:
                    dve_tail(it - 1, t_)
                if cond and t_ == 0:
                    dve_cond_start(it + 1)
                if cond:
                    dve_cond_late(it + 1, t_)
                if cond and t_ == 11:
                    dve_xnT(it + 1, 0)
                if cond and t_ == 0:
                    dve_cond_keys(it + 1)
                if ffn and 0 <= u < NU:
                    dve_mask_max(Af, it, "fS", u, probs, frow_max, neg_max, FHD ** -0.5, ffn_max)
                if cond and 0 <= v < NU:
                    dve_mask_max(Ac, it + 1, "cS", v, cprobs, crow_max, cneg_max, 1.0, cond_max)
                if tail and t_ > 0:
                    dve_tail(it - 1, t_)
                if ffn:
                    for r in ropes_of(t_):
                        dve_rope_cos(it, r)
                if ffn and 0 <= u - 1 < NU:
                    dve_copy(Af, it, ("fT", u - 1), probsT[:, (u - 1) % 2, :])
                if cond and 0 <= v - 1 < NU:
                    dve_copy(Ac, it + 1, ("cT", v - 1), cprobsT[:, (v - 1) % 2, :])
                if ffn:
                    for r in ropes_of(t_):
                        dve_rope_add(it, r)
                if ffn and 0 <= u < NU:
                    dve_scale_probs(it, u)
            if cond:
                dve_xnT(it + 1, 1)

        def act_exps(it, n, m_ready, buf, nmax, scale, p_ready, sums):
            act, a = nc.scalar, nc.scalar
            act.wait_ge(m_ready, it * NU + (n + 1))
            for i in range(4):
                x = buf[:, n % 3, i * P:(i + 1) * P]
                last = a.activation(x, x, ACT.Exp, bias=nmax[:, n % 3, i:i + 1], scale=scale, accum_out=sums(n, i))
            last.then_inc(p_ready, 1)

        def act_cond_start(i):
            act, a = nc.scalar, nc.scalar
            b = filled(act, Ac, i, "cq")
            for s in range(2):
                last = a.activation(cqT[:, :, s * P:(s + 1) * P],
                                    b[:, :].rearrange("p (f t) -> p f t", f=2)[:, :, s * P:(s + 1) * P],
                                    ACT.Copy, scale=beta[:, bass.ds(i * 2 + s, 1)])
            last.then_inc(free_sem(Ac, "cq"), 1)
            b = filled(act, Ac, i, "cv")
            a.activation(cv[:, :, :].rearrange("p a b -> p (a b)"), b[:, :], ACT.Copy).then_inc(free_sem(Ac, "cv"), 1)

        def act_cond_rows(i, s):
            act, a = nc.scalar, nc.scalar
            b = filled(act, Ac, i, ("cY", s))
            wait(act, y_kept, i)
            a.activation(y_sb[:, s, :], b[:, 0:256], ACT.Copy).then_inc(y_copied, 1)
            a.activation(junk, b[:, 0:256], ACT.Square, accum_out=sq[:, s:s + 1]).then_inc(y_squares, 1)
            act.wait_ge(y_squares, i * 2 + (s + 1))
            a.activation(ms[:, s:s + 1], sq[:, s:s + 1], ACT.Copy, scale=1.0 / D, bias=1e-5).then_inc(free_sem(Ac, ("cY", s)), 1)

        def act_swap(it, r):
            act, a = nc.scalar, nc.scalar
            b = filled(act, Af, it, ("rope", r))
            wait(act, rope_done, it * NR + (r - 1))
            a.activation(swapped[0:64, r % 2, :], b[64:128, :], ACT.Copy)
            a.activation(swapped[64:128, r % 2, :], b[0:64, :], ACT.Copy).then_inc(swap_ready, 1)

        def act_tail(i):
            act, a = nc.scalar, nc.scalar
            drained(act, Af, i, "wo")
            for s in range(2):
                a.activation(junk, h_all[:, bass.ds(i * 2 + s, 1), :].rearrange("p a b -> p (a b)"), ACT.Square,
                             accum_out=sq[:, 2 + s:3 + s]).then_inc(h_squares, 1)
                act.wait_ge(h_squares, i * 2 + (s + 1))
                a.activation(ms[:, 2 + s:3 + s], sq[:, 2 + s:3 + s], ACT.Copy, scale=1.0 / D, bias=1e-5).then_inc(h_mean, 1)

        def A_act(it, ffn, cond, tail):
            act, a = nc.scalar, nc.scalar
            for t_ in range(STEPS_A):
                u, v = ffn_unit(t_), cond_unit(t_)
                if tail and t_ == 0:
                    act_tail(it - 1)
                if ffn and t_ == 0:
                    if tail:
                        drained(act, Af, it - 1, "wo")
                    act.wait_ge(y_copied, it * 2 + 2)
                    a.activation(y_keep, y_sb[:, :, :], ACT.Copy).then_inc(y_kept, 1)
                    for s in range(2):
                        b = filled(act, Af, it, ("fv", s))
                        a.activation(fv[:, s, :], b[:, :], ACT.Copy).then_inc(free_sem(Af, ("fv", s)), 1)
                if cond and t_ == 0:
                    act_cond_start(it + 1)
                if cond and t_ in (8, 12):
                    act_cond_rows(it + 1, (t_ - 8) // 4)
                if ffn and 0 <= u < NU:
                    act_exps(it, u, ffn_max, probs, neg_max, FHD ** -0.5, ffn_probs, lambda n, i: fsum[:, n % 3, i:i + 1])
                if ffn:
                    for r in ropes_of(t_):
                        act_swap(it, r)
                if cond and 0 <= v < NU:
                    act_exps(it + 1, v, cond_max, cprobs, cneg_max, 1.0, cond_probs,
                             lambda n, i: row_sum[:, n // 4, heads_of(n % 4)[i]:heads_of(n % 4)[i] + 1])
                if ffn and 0 <= u - 1 < NU:
                    b = filled(act, Af, it, ("fO", u - 1))
                    a.activation(foT[:, (u - 1) % 2, :], b[:, :], ACT.Copy).then_inc(free_sem(Af, ("fO", u - 1)), 1)

        def A_pool(it, ffn, cond, tail):
            pool, g = nc.gpsimd, nc.gpsimd
            for t_ in range(STEPS_A):
                if tail and t_ == 0:
                    for s in range(2):
                        pool.wait_ge(h_mean, (it - 1) * 2 + (s + 1))
                        g.tensor_tensor(rstd[:, 2 + s:3 + s], ms[:, 2 + s:3 + s], neg_half[:, 0:1], ALU.pow).then_inc(h_rstd, 1)
                if ffn:
                    for r in ropes_of(t_):
                        pool.wait_ge(swap_ready, it * NR + (r + 1))
                        sw = swapped[:, r % 2, :].rearrange("p (a b) -> p a b", a=4)
                        g.tensor_tensor(sw, sw, sin_b.unsqueeze(1).broadcast_to([P, 4, P]), ALU.mult).then_inc(sin_ready, 1)
                if cond and t_ in (8, 12):
                    s = (t_ - 8) // 4
                    drained(pool, Ac, it + 1, ("cY", s))
                    g.tensor_tensor(rstd[:, s:s + 1], ms[:, s:s + 1], neg_half[:, 0:1], ALU.pow).then_inc(y_rstd, 1)

        def A_run(eng, body):
            body(-1, ffn=False, cond=True, tail=False)
            if eng is nc.tensor:
                eng.wait_ge(attn_w_loaded, 64)
            if eng is nc.gpsimd:
                places_pool()
            body(0, ffn=True, cond=True, tail=False)
            with eng.Fori(1, PAIRS - 1) as it:
                body(it, ffn=True, cond=True, tail=True)
            body(PAIRS - 1, ffn=True, cond=False, tail=True)
            body(PAIRS, ffn=False, cond=False, tail=True)

        B = Banks([("rank", 0)], after_A, 1)
        route = {n: sb("route_" + n, [P, NSEQ, E0]) for n in ("eq", "one1", "one2", "rest", "slot")}
        rmax = sb("route_max", [P, 2, NSEQ])
        rcand = sb("route_first", [P, NSEQ])
        p12 = sb("route_probs", [P, 2, NSEQ])
        pexp = sb("route_exp", [P, 2, NSEQ])
        cum = sb("rows_before", [P, NSEQ + 1, E0])
        tiles_f = sb("tiles_of_expert", [P, 4, E0])
        tiles_i = sb("tiles_of_expert_int", [P, 2, E0], i32)
        slots_i = sb("slots", [P, 2, NSEQ], i32)
        slots_f = sb("slots_float", [P, 2, NSEQ])
        tile_e = sb("expert_of_tile", [1, TILES0], i32)
        tile_ef = sb("expert_of_tile_float", [1, TILES0])
        tile_cmp = sb("tile_compare", [1, TILES0 * E0])
        x2_all = fqT[:, :, :, :].rearrange("p a b c -> p (a b c)").rearrange("p (b d) -> p b d", b=NSEQ)

        route_step = sem("routing_step")
        exp_ready = sem("route_exp_ready")
        ones_ready = sem("route_counts_ready")
        x2_all_ready = sem("x2_all_ready")
        slots_ready = sem("slots_ready")
        tile_e_ready = sem("expert_of_tile_ready")
        zero_filled = sem("routed_rows_zero_filled")
        zero_ready = sem("zero_tile_ready")
        scattered = sem("rows_scattered")
        w2_loaded = sem("w2_loaded")
        l1_loaded = sem("layer1_weights_loaded")

        def top2(lg, n, link):
            v = nc.vector
            one, rest, eq = (route["one1"], route["one2"]), route["rest"], route["eq"]
            src = lg
            for i in range(2):
                link(v.tensor_reduce(rmax[:, i, 0:n], src, AX.X, ALU.max))
                link(v.tensor_tensor(eq[:, 0:n, :], src, rmax[:, i, 0:n].unsqueeze(2).broadcast_to([P, n, E0]), ALU.is_equal))
                link(v.scalar_tensor_tensor(eq[:, 0:n, :], eq[:, 0:n, :], -8.0,
                                            c("expert8").rearrange("p (a b) -> p a b", b=E0)[:, 0:n, :], ALU.mult, ALU.add))
                link(v.tensor_reduce(rcand[:, 0:n], eq[:, 0:n, :], AX.X, ALU.min))
                link(v.tensor_tensor(one[i][:, 0:n, :], c("expert").rearrange("p (a b) -> p a b", b=E0)[:, 0:n, :],
                                     rcand[:, 0:n].unsqueeze(2).broadcast_to([P, n, E0]), ALU.is_equal))
                if i == 0:
                    link(v.scalar_tensor_tensor(rest[:, 0:n, :], one[0][:, 0:n, :], NEG, lg, ALU.mult, ALU.add))
                    src = rest[:, 0:n, :]
            link(v.tensor_tensor(pexp[:, 0, 0:n], rmax[:, 1, 0:n], rmax[:, 0, 0:n], ALU.subtract))

        def top2_probs(n, link):
            v = nc.vector
            link(v.tensor_scalar(p12[:, 1, 0:n], pexp[:, 1, 0:n], 1.0, None, ALU.add))
            link(v.reciprocal(p12[:, 0, 0:n], p12[:, 1, 0:n]))
            link(v.tensor_tensor(p12[:, 1, 0:n], pexp[:, 1, 0:n], p12[:, 0, 0:n], ALU.mult))

        def B_dve():
            dve, v = nc.vector, nc.vector
            steps = [0]

            def link(ins):
                steps[0] += 1
                ins.then_inc(route_step, 1)
                dve.wait_ge(route_step, steps[0])

            drained(dve, Af, PAIRS - 1, "logit")
            top2(logits[:, :, :], NSEQ, link)
            v.tensor_tensor(route["eq"][:, :, :], route["one1"][:, :, :], route["one2"][:, :, :], ALU.add)\
                .then_inc(ones_ready, 1)
            for b in range(NSEQ):
                last = v.tensor_scalar(x2_all[:, b, :], h_all[:, b, :], rstd2[:, b:b + 1], None, ALU.mult)
            last.then_inc(x2_all_ready, 1)
            link(v.memset(cum[:, 0, :], 0.0))
            b = filled(dve, B, 0, "rank")
            for i in range(NSEQ):
                link(v.tensor_tensor(cum[:, i + 1, :], cum[:, i, :], b[:, 64 + i * E0:64 + (i + 1) * E0], ALU.add))
            link(v.tensor_scalar(tiles_i[:, 0, :], cum[:, NSEQ, :], float(P - 1), None, ALU.add))
            link(v.tensor_scalar(tiles_i[:, 1, :], tiles_i[:, 0, :], 7, None, ALU.arith_shift_right))
            link(v.tensor_copy(tiles_f[:, 0, :], tiles_i[:, 1, :]))
            link(v.tensor_tensor(route["rest"][:, :, :], c("below").rearrange("p (a b) -> p a b", b=E0),
                                 tiles_f[:, 0, :].unsqueeze(1).broadcast_to([P, E0, E0]), ALU.mult))
            link(v.tensor_reduce(tiles_f[:, 1, :], route["rest"][:, :, :], AX.X, ALU.add))
            link(v.tensor_tensor(tiles_f[:, 2, :], tiles_f[:, 1, :], tiles_f[:, 0, :], ALU.add))
            link(v.tensor_scalar(tiles_f[:, 3, :], tiles_f[:, 1, :], float(P), None, ALU.mult))
            link(v.tensor_tensor(route["slot"][:, :, :].rearrange("p a b -> p (a b)"),
                                 cum[:, 0:NSEQ, :].rearrange("p a b -> p (a b)"), b[:, 0:64], ALU.add))
            link(v.tensor_tensor(route["slot"][:, :, :], route["slot"][:, :, :],
                                 tiles_f[:, 3, :].unsqueeze(1).broadcast_to([P, NSEQ, E0]), ALU.add))
            for i in range(2):
                link(v.tensor_tensor(route["rest"][:, :, :], route["one%d" % (i + 1)][:, :, :], route["slot"][:, :, :], ALU.mult))
                link(v.tensor_reduce(slots_f[:, i, :], route["rest"][:, :, :], AX.X, ALU.add))
            v.tensor_copy(slots_i[:, :, :], slots_f[:, :, :]).then_inc(slots_ready, 1)
            link(v.tensor_tensor(tile_cmp[:, :].rearrange("p (a b) -> p a b", b=E0),
                                 c("tile_no")[0:1, :].rearrange("p (a b) -> p a b", b=E0),
                                 tiles_f[0:1, 2, :].unsqueeze(1).broadcast_to([1, TILES0, E0]), ALU.is_ge))
            link(v.tensor_reduce(tile_ef[:, :], tile_cmp[:, :].rearrange("p (a b) -> p a b", b=E0), AX.X, ALU.add))
            v.tensor_scalar(tile_e[:, :], tile_ef[:, :], float(E0 - 1), None, ALU.min).then_inc(tile_e_ready, 1)
            dve.wait_ge(exp_ready, 1)
            top2_probs(NSEQ, link)
            dve.wait_ge(slots_ready, 1)
            nc.vector.memset(carrier[0:1, 0:1], 0.0).then_inc(free_sem(B, "rank"), 1)

        def B_pe():
            pe, te = nc.tensor, nc.tensor
            pe.wait_ge(ones_ready, 1)
            b = claim(B, 0, "rank")
            m = route["eq"][:, :, :].rearrange("p a b -> p (a b)")
            te.matmul(b[:, 0:64], c("before"), m, start=True, stop=True)
            te.matmul(b[:, 64:128], c("ones"), m, start=True, stop=True).then_inc(full_sem(B, "rank"), 1)

        def B_act():
            act = nc.scalar
            act.wait_ge(route_step, 12)
            nc.scalar.activation(pexp[:, 1, :], pexp[:, 0, :], ACT.Exp).then_inc(exp_ready, 1)

        def B_pool():
            pool = nc.gpsimd
            pool.wait_ge(slots_ready, 1)
            pool.wait_ge(x2_all_ready, 1)
            pool.wait_ge(zero_filled, 48)
            for b in range(NSEQ):
                for i in range(2):
                    nc.gpsimd.indirect_dma_start(
                        out=xs_d, out_offset=bass.IndirectOffsetOnAxis(ap=slots_i[:, i, b:b + 1], axis=0),
                        in_=x2_all[:, b, :], in_offset=None).then_inc(scattered, 16)

        kvl = sb("kv_lens", [P, NSEQ], i32)
        pos = sb("positions", [P, 2 * NSEQ], i32)
        slot = sb("block_slots", [P, 2 * NSEQ], i32)
        off = sb("block_offsets", [P, 2 * NSEQ], i32)
        off_f = sb("block_offsets_float", [P, 2 * NSEQ])
        cache_f = sb("cache_rows_float", [P, NSEQ])
        table_at = sb("table_rows", [P, 2 * NSEQ], i32)
        block_no = sb("blocks", [P, 2 * NSEQ], i32)
        place = sb("places", [P, 24])
        winner = sb("last_writers", [P, 24])
        winner_i = sb("last_writers_int", [P, 2 * NSEQ], i32)
        winner_f = sb("last_writers_index", [P, 2 * NSEQ])
        cache_at = sb("cache_rows", [P, G1, NSEQ], i32)
        early = sb("positions_below_zero", [P, NSEQ])
        cs_all = sb("rope_rows", [P, NSEQ, 2 * BLOCK])
        written = kv_new[:, 0:4, :].rearrange("p a b -> p (a b)")
        row_no = kv_new[:, 4:8, :].rearrange("p a b -> p (a b)")
        winner_tmp = swapped[:, :, :].rearrange("p a b -> p (a b)")
        kvl_loaded = sem("kv_lens_loaded")
        place_step = sem("places_step")
        table_at_ready = sem("table_rows_ready")
        table_read = sem("table_read")
        pool_step = sem("pool_places_step")
        place_ready = sem("places_ready")
        written_out = sem("places_in_dram")
        written_in = sem("places_of_all_loaded")
        cache_read = sem("cache_read")
        winner_step = sem("winner_compared")
        winner_ready = sem("winner_ready")
        rope_loaded = sem("rope_rows_loaded")

        def places_dve():
            dve, v = nc.vector, nc.vector
            steps = [0]

            def link(ins):
                steps[0] += 1
                ins.then_inc(place_step, 1)
                dve.wait_ge(place_step, steps[0])

            v.memset(kv_old[:, :, :], 0.0).then_inc(zero_ready, 1)
            v.memset(place[:, :], 0.0)
            dve.wait_ge(kvl_loaded, 16)
            v.tensor_scalar(early[:, :], kvl[:, :], -1.0, float(P), ALU.mult, ALU.add)
            v.tensor_scalar(pos[:, 0:NSEQ], kvl[:, :], c("row"), None, ALU.add)
            link(v.tensor_scalar(pos[:, NSEQ:], kvl[:, :], c("row"), -float(P), ALU.add, ALU.add))
            link(v.tensor_scalar(pos[:, NSEQ:], pos[:, NSEQ:], 0.0, None, ALU.max))
            v.tensor_scalar(off[:, :], pos[:, :], BLOCK - 1, None, ALU.bitwise_and)
            link(v.tensor_scalar(slot[:, :], pos[:, :], 4, None, ALU.arith_shift_right))
            v.tensor_copy(off_f[:, :], off[:, :])
            v.scalar_tensor_tensor(table_at[:, :], slot[:, :], float(NBLK - 1), c("seq_base"), ALU.min, ALU.add)\
                .then_inc(table_at_ready, 1)

        def places_pool():
            pool, g = nc.gpsimd, nc.gpsimd
            pool.wait_ge(table_at_ready, 1)
            for n in range(2 * NSEQ):
                g.indirect_dma_start(out=block_no[:, n:n + 1], out_offset=None, in_=t["table"],
                                     in_offset=bass.IndirectOffsetOnAxis(ap=table_at[:, n:n + 1], axis=0)).then_inc(table_read, 16)
            pool.wait_ge(table_read, 16 * 2 * NSEQ)
            n = [0]

            def link(ins):
                n[0] += 1
                ins.then_inc(pool_step, 1)
                pool.wait_ge(pool_step, n[0])

            link(g.tensor_scalar(place[:, 0:16], block_no[:, :], float(BLOCK), None, ALU.mult))
            link(g.tensor_tensor(place[:, 0:16], place[:, 0:16], off_f[:, :], ALU.add))
            g.dma_start(wl_d.rearrange("(b p) -> p b", p=P), place[:, 0:NSEQ], allow_slow_non_contiguous=True).then_inc(written_out, 16)
            link(g.tensor_scalar(cache_f[:, :], block_no[:, NSEQ:], float(BLOCK * G1), None, ALU.mult))
            link(g.tensor_tensor(cache_f[:, :], cache_f[:, :], off_f[:, NSEQ:], ALU.add))
            for i in range(G1):
                link(g.tensor_scalar(cache_at[:, i, :], cache_f[:, :], float(BLOCK * i), None, ALU.add))

        def cache_pool():
            for name, at in (("k_blocks", 0), ("v_blocks", P)):
                rows = t[name].rearrange("n g o d -> (n g o) d")
                for b in range(NSEQ):
                    for i in range(G1):
                        nc.gpsimd.indirect_dma_start(
                            out=kv_old[:, b, at + i * HD1:at + (i + 1) * HD1], out_offset=None, in_=rows,
                            in_offset=bass.IndirectOffsetOnAxis(ap=cache_at[:, i, b:b + 1], axis=0)).then_inc(cache_read, 16)

        C = TileBanks(B.after, TILES0)
        rows_in = x_in
        rowsT = xT[:, :, :].rearrange("p a (r b) -> p r a b", r=2)
        silu = masked
        hid = probs
        hidT = probsT[:, :, :].rearrange("p r (a b) -> p r a b", b=P)
        rows_out = o_sb
        row_loaded = [sem("row_loaded0"), sem("row_loaded1")]
        row_stored = [sem("row_stored0"), sem("row_stored1")]

        STEPS = (TILES0 - 1) // 2

        def C_pe_step(j, k, more=True):
            pe, te = nc.tensor, nc.tensor
            i = j * 2 + k
            e = pe.value_load(tile_e[0:1, bass.ds(i, 1)], min_val=0, max_val=E0 - 1)
            drained(pe, C, j, ("xT", k))

            def half(use, w):
                b = claim(C, j, (use, k))
                for q in range(KC):
                    last = te.matmul(b[:, :], rowsT[:, k % 2, q, :], w13[:, w, bass.ds(e, 1), q, :],
                                     start=(q == 0), stop=(q == KC - 1))
                last.then_inc(full_sem(C, (use, k)), 1)

            half("up", 0)
            if k > 0 or not isinstance(j, int) or j > 0:
                C_transpose_hidden(j, k - 1)
            half("gate", 1)
            if more:
                C_transpose_rows(j, k + 1)
            if k > 0 or not isinstance(j, int) or j > 0:
                C_down(j, k - 1)

        def C_transpose_rows(j, k):
            pe, te = nc.tensor, nc.tensor
            wait(pe, row_loaded[k % 2], (j + (k // 2 + 1)) * 16)
            b = claim(C, j, ("xT", k))
            for q in range(KC):
                last = te.transpose(b[:, q * P:(q + 1) * P], rows_in[:, k % 2, q * P:(q + 1) * P], ident)
            last.then_inc(full_sem(C, ("xT", k)), 1)

        def C_transpose_hidden(j, k):
            pe, te = nc.tensor, nc.tensor
            drained(pe, C, j, ("gate", k))
            b = claim(C, j, ("hT", k))
            for q in range(F0 // P):
                last = te.transpose(b[:, q * P:(q + 1) * P], hid[:, k % 2, q * P:(q + 1) * P], ident)
            last.then_inc(full_sem(C, ("hT", k)), 1)

        def C_down(j, k):
            pe, te = nc.tensor, nc.tensor
            e = pe.value_load(tile_e[0:1, bass.ds(j * 2 + k, 1)], min_val=0, max_val=E0 - 1)
            drained(pe, C, j, ("hT", k))
            b = claim(C, j, ("down", k))
            for q in range(F0 // P):
                last = te.matmul(b[:, 0:256], hidT[:, k % 2, q, :], w2e[:, bass.ds(e, 1), q, :],
                                 start=(q == 0), stop=(q == F0 // P - 1))
            last.then_inc(full_sem(C, ("down", k)), 1)

        def C_rowsT_copy(j, k):
            b = filled(nc.vector, C, j, ("xT", k))
            for q in range(KC):
                last = nc.vector.tensor_scalar(rowsT[:, k % 2, q, :], b[:, q * P:(q + 1) * P], norm2[:, q:q + 1], None, ALU.mult)
            last.then_inc(free_sem(C, ("xT", k)), 1)

        def last_writer(j, k):
            v = nc.vector
            col = bass.ds(j * 2 + (k - 1), 1)
            n = j * 4 + 2 * (k - 1)
            wait(v, winner_step, n)
            v.scalar_tensor_tensor(winner_tmp, written, place[:, col], row_no, ALU.is_equal, ALU.mult).then_inc(winner_step, 1)
            v.wait_ge(winner_step, n + 1)
            v.tensor_reduce(winner[:, col], winner_tmp, AX.X, ALU.max).then_inc(winner_step, 1)

        def C_hidT_copy(j, k):
            b = filled(nc.vector, C, j, ("hT", k))
            nc.vector.tensor_copy(hidT[:, k % 2, :, :].rearrange("p a b -> p (a b)"), b[:, :]).then_inc(free_sem(C, ("hT", k)), 1)

        def C_dve_step(j, k, more=True):
            dve, v = nc.vector, nc.vector
            if k > 0 or not isinstance(j, int) or j > 0:
                C_hidT_copy(j, k - 1)
            b = filled(dve, C, j, ("gate", k))
            drained(dve, C, j, ("up", k))
            v.tensor_tensor(hid[:, k % 2, :], silu[:, k % 2, :], b[:, :], ALU.mult).then_inc(free_sem(C, ("gate", k)), 1)
            if more:
                C_rowsT_copy(j, k + 1)
            if 0 < k and more:
                last_writer(j, k)

        def C_act_down(j, k):
            act = nc.scalar
            b = filled(act, C, j, ("down", k))
            if k >= 2 or not isinstance(j, int) or j > 0:
                wait(act, row_stored[k % 2], (j + k // 2) * 16)
            nc.scalar.activation(rows_out[:, k % 2, :], b[:, 0:256], ACT.Copy).then_inc(free_sem(C, ("down", k)), 1)

        def C_act_step(j, k):
            act = nc.scalar
            b = filled(act, C, j, ("up", k))
            if k >= 2 or not isinstance(j, int) or j > 0:
                drained(act, C, j, ("gate", k - 2))
            nc.scalar.activation(silu[:, k % 2, :], b[:, :], ACT.Silu).then_inc(free_sem(C, ("up", k)), 1)
            if k > 0 or not isinstance(j, int) or j > 0:
                C_act_down(j, k - 1)

        def C_load(j, k):
            sp = nc.sync
            if k >= 2 or not isinstance(j, int) or j > 0:
                filled(sp, C, j, ("xT", k - 2))
            sp.dma_start(rows_in[:, k % 2, :], xs_d[bass.ds((j * 2 + k) * P, P), :]).then_inc(row_loaded[k % 2], 16)

        def C_store(j, k):
            sp = nc.sync
            drained(sp, C, j, ("down", k))
            sp.dma_start(ys_d[bass.ds((j * 2 + k) * P, P), :], rows_out[:, k % 2, :]).then_inc(row_stored[k % 2], 16)

        def C_run(eng, first, step, last):
            first()
            step(0, 1)
            step(0, 2)
            with eng.Fori(1, STEPS - 1) as j:
                step(j, 1)
                step(j, 2)
            step(STEPS - 1, 1)
            last()

        Dp = Banks([("x1T", 0), (("qkv", 0), 1), (("qkv", 1), 2), (("qT", 0), 3), (("qT", 1), 4)], C.after, PAIRS)
        w13f = w13[:, :, :, :, :].rearrange("p a e c f -> p (a e c f)")
        y_rows = [w13f[:, i * 2048:(i + 1) * 2048].rearrange("p (b d) -> p b d", b=NSEQ) for i in range(2)]
        x1_s = y_sb
        x1T = xT
        sq_rows = masked
        qn = probs
        qn_sin = oT[:, :, :].rearrange("p a b -> p (a b)")
        qkv_rows = swapped
        norm_w = cqT[:, :, :].rearrange("p a b -> p (a b)")
        w_qkv = fv[:, :, :].rearrange("p s n -> p (s n)").rearrange("p (c n) -> p c n", c=KC)
        w1_1 = w_c[:, :, :, :].rearrange("p a b c -> p (a b c)").rearrange("p (e c n) -> p e c n", e=E1, c=KC)
        w2_1 = w_kv[:, :, :, :].rearrange("p a b c -> p (a b c)").rearrange("p (e n) -> p e n", e=E1)
        sw1 = fkT[:, 0:2, :]
        sw2 = fkT[:, 2:4, :]
        wo_1 = foT[:, 0, :].rearrange("p (c n) -> p c n", c=C1)
        small = foT[:, 1, :]
        b1_s = small[:, 0:8]
        sb1_s = small[:, 8:10]
        gate1 = small[:, 16:32].rearrange("p (c n) -> p c n", c=KC)
        b2_s = small[0:9, 64:320]
        qT_all = fqT[:, :, :, :].rearrange("p a b c -> p (a b c)").rearrange("p (c b q) -> p c b q", c=C1, b=NSEQ)
        NQK = 12
        ssq = sb("qk_sum_squares", [P, 2, 16])
        rqk = sb("qk_rstd", [P, 2, 16])

        y_gathered = sem("expert_rows_gathered")
        x1_step = sem("x1_step")
        x1_ready = sem("x1_rows_ready")
        x1_kept = sem("x1_rows_kept")
        x_again = sem("x_loaded_again")
        sq_ready = sem("qk_squares_ready")
        ms_step = sem("qk_mean_squares_step")
        ms_ready = sem("qk_mean_squares_ready")
        rqk_ready = sem("qk_rstd_ready")
        qn_step = sem("qk_norm_step")
        qn_ready = sem("qk_normed")
        qsin_ready = sem("qk_sine_part_ready")
        v_copied = sem("new_v_copied")
        rows_ready = sem("qkv_rows_ready")
        kv_stored = sem("new_kv_stored")
        norm_w_ready = sem("qk_norm_weights_ready")

        def D_gather():
            pool = nc.gpsimd
            for i in range(2):
                tiles = (TILES0 + 1 - i) // 2
                pool.wait_ge(row_stored[i], 16 * tiles)
            for b in range(NSEQ):
                for i in range(2):
                    nc.gpsimd.indirect_dma_start(
                        out=y_rows[i][:, b, :], out_offset=None, in_=ys_d,
                        in_offset=bass.IndirectOffsetOnAxis(ap=slots_i[:, i, b:b + 1], axis=0)).then_inc(y_gathered, 16)

        def D_pe(it):
            pe, te = nc.tensor, nc.tensor
            pe.wait_ge(x1_ready, it * 2 + 2)
            b = claim(Dp, it, "x1T")
            for k in range(KC):
                for s in range(2):
                    last = te.transpose(b[:, (k * 2 + s) * P:(k * 2 + s + 1) * P], x1_s[:, s, k * P:(k + 1) * P], ident)
            last.then_inc(full_sem(Dp, "x1T"), 1)
            drained(pe, Dp, it, "x1T")
            for s in range(2):
                b = claim(Dp, it, ("qkv", s))
                for k in range(KC):
                    last = te.matmul(b[:, :], x1T[:, k, s * P:(s + 1) * P], w_qkv[:, k, :], start=(k == 0), stop=(k == KC - 1))
                last.then_inc(full_sem(Dp, ("qkv", s)), 1)
            for s in range(2):
                pe.wait_ge(rows_ready, it * 2 + (s + 1))
                b = claim(Dp, it, ("qT", s))
                for k in range(C1):
                    last = te.transpose(b[:, k * P:(k + 1) * P], qkv_rows[:, s, k * P:(k + 1) * P], ident)
                last.then_inc(full_sem(Dp, ("qT", s)), 1)

        def D_dve(it):
            dve, v = nc.vector, nc.vector
            dve.wait_ge(x_again, it * 16 + 16)
            if not isinstance(it, int) or it > 0:
                dve.wait_ge(x1_kept, it)
            for s in range(2):
                n = it * 6 + 3 * s
                v.tensor_tensor(x1_s[:, s, :], x_in[:, s, :], h_all[:, bass.ds(it * 2 + s, 1), :].rearrange("p a b -> p (a b)"),
                                ALU.add).then_inc(x1_step, 1)
                for i in range(2):
                    dve.wait_ge(x1_step, n + (i + 1))
                    v.scalar_tensor_tensor(x1_s[:, s, :], y_rows[i][:, bass.ds(it * 2 + s, 1), :].rearrange("p a b -> p (a b)"),
                                           p12[:, i, bass.ds(it * 2 + s, 1)], x1_s[:, s, :], ALU.mult, ALU.add)\
                        .then_inc(x1_step if i == 0 else x1_ready, 1)
                    if i == 1:
                        v.memset(carrier[0:1, 0:1], 0.0).then_inc(x1_step, 1)
            b = filled(dve, Dp, it, "x1T")
            v.tensor_copy(x1T[:, :, :].rearrange("p a b -> p (a b)"), b[:, :]).then_inc(free_sem(Dp, "x1T"), 1)
            for s in range(2):
                dve.wait_ge(sq_ready, it * 2 + (s + 1))
                v.tensor_reduce(ssq[:, s, 0:NQK], sq_rows[:, s, 0:NQK * HD1].rearrange("p (h d) -> p h d", d=HD1), AX.X, ALU.add)\
                    .then_inc(ms_step, 1)
                dve.wait_ge(ms_step, it * 2 + (s + 1))
                v.tensor_scalar(ssq[:, s, 0:NQK], ssq[:, s, 0:NQK], 1.0 / HD1, 1e-6, ALU.mult, ALU.add).then_inc(ms_ready, 1)
            for s in range(2):
                dve.wait_ge(rqk_ready, it * 2 + (s + 1))
                b = filled(dve, Dp, it, ("qkv", s))
                dve.wait_ge(v_copied, it * 2 + (s + 1))
                q = qn[:, s, 0:NQK * HD1]
                v.tensor_tensor(q.rearrange("p (h d) -> p h d", d=HD1), b[:, 0:NQK * HD1].rearrange("p (h d) -> p h d", d=HD1),
                                rqk[:, s, 0:NQK].unsqueeze(2).broadcast_to([P, NQK, HD1]), ALU.mult).then_inc(free_sem(Dp, ("qkv", s)), 1)
                drained(dve, Dp, it, ("qkv", s))
                v.tensor_tensor(q, q, norm_w[:, 0:NQK * HD1], ALU.mult).then_inc(qn_ready, 1)
                dve.wait_ge(qn_ready, it * 2 + (s + 1))
                if not isinstance(it, int) or it > 0:
                    dve.wait_ge(kv_stored, (it * 2 + (s - 1)) * 16 if s == 1 else it * 32)
                q4 = q.rearrange("p (h a d) -> p h a d", a=2, d=HD1 // 2)
                cs = cs_all[:, bass.ds(it * 2 + s, 1), :].rearrange("p a b -> p (a b)")
                sq4 = sq_rows[:, s, 0:NQK * HD1].rearrange("p (h a d) -> p h a d", a=2, d=HD1 // 2)
                for a in range(2):
                    last = v.tensor_tensor(sq4[:, :, a, :], q4[:, :, a, :],
                                           cs[:, 0:HD1 // 2].unsqueeze(1).broadcast_to([P, NQK, HD1 // 2]), ALU.mult)
                last.then_inc(qn_step, 1)
                dve.wait_ge(qn_step, it * 2 + (s + 1))
                dve.wait_ge(qsin_ready, it * 2 + (s + 1))
                r4 = qkv_rows[:, s, 0:NQK * HD1].rearrange("p (h a d) -> p h a d", a=2, d=HD1 // 2)
                n4 = qn_sin4(s)
                v.tensor_tensor(r4[:, :, 0, :], sq4[:, :, 0, :], n4[:, :, 1, :], ALU.subtract)
                v.tensor_tensor(r4[:, :, 1, :], sq4[:, :, 1, :], n4[:, :, 0, :], ALU.add).then_inc(rows_ready, 1)
            for s in range(2):
                b = filled(dve, Dp, it, ("qT", s))
                v.tensor_copy(qT_all[:, :, bass.ds(it * 2 + s, 1), :].rearrange("p c b q -> p c (b q)"),
                              b[:, 0:256].rearrange("p (c q) -> p c q", c=C1)).then_inc(free_sem(Dp, ("qT", s)), 1)

        def qn_sin4(s):
            return w13f[:, 4096 + 512 * s:4096 + 512 * s + NQK * HD1].rearrange("p (h a d) -> p h a d", a=2, d=HD1 // 2)

        def D_act(it):
            act, a = nc.scalar, nc.scalar
            act.wait_ge(x1_ready, it * 2 + 2)
            a.activation(h_all[:, bass.ds(it * 2, 2), :].rearrange("p a b -> p (a b)"),
                         x1_s[:, :, :].rearrange("p a b -> p (a b)"), ACT.Copy).then_inc(x1_kept, 1)
            for s in range(2):
                b = filled(act, Dp, it, ("qkv", s))
                if s == 0:
                    wait(act, rows_ready, it * 2)
                wait(act, kv_stored, it * 32)
                a.activation(sq_rows[:, s, 0:NQK * HD1], b[:, 0:NQK * HD1], ACT.Square).then_inc(sq_ready, 1)
                a.activation(qkv_rows[:, s, NQK * HD1:], b[:, NQK * HD1:], ACT.Copy).then_inc(v_copied, 1)

        def D_pool(it):
            pool, g = nc.gpsimd, nc.gpsimd
            for s in range(2):
                pool.wait_ge(ms_ready, it * 2 + (s + 1))
                g.tensor_tensor(rqk[:, s, 0:NQK], ssq[:, s, 0:NQK], neg_half[:, 0:NQK], ALU.pow).then_inc(rqk_ready, 1)
            for s in range(2):
                pool.wait_ge(qn_ready, it * 2 + (s + 1))
                q4 = qn[:, s, 0:NQK * HD1].rearrange("p (h a d) -> p h a d", a=2, d=HD1 // 2)
                cs = cs_all[:, bass.ds(it * 2 + s, 1), :].rearrange("p a b -> p (a b)")
                for a in range(2):
                    last = g.tensor_tensor(qn_sin4(s)[:, :, a, :], q4[:, :, a, :],
                                           cs[:, HD1 // 2:].unsqueeze(1).broadcast_to([P, NQK, HD1 // 2]), ALU.mult)
                last.then_inc(qsin_ready, 1)

        def D_store(it):
            sp = nc.sync
            if not isinstance(it, int) or it < PAIRS - 1:
                sp.wait_ge(x1_ready, it * 2 + 2)
                sp.dma_start(x_in[:, :, :], t["x"][bass.ds((it + 1) * 2, 2), :, :].rearrange("s p d -> p s d")).then_inc(x_again, 16)
            for s in range(2):
                sp.wait_ge(rows_ready, it * 2 + (s + 1))
                sp.wait_ge(v_copied, it * 2 + (s + 1))
                sp.dma_start(kv_d[bass.ds((it * 2 + s) * P, P), :], qkv_rows[:, s, 256:512]).then_inc(kv_stored, 16)

        E = Banks([(("kT", p), p) for p in range(PAIRS)], Dp.after, 1)
        kT_all = w_qo[:, 0:2048].rearrange("p (b k) -> p b k", b=NSEQ)
        kv_gathered = [sem("kv_gathered%d" % b) for b in range(NSEQ)]

        def E_pool():
            pool = nc.gpsimd
            pool.wait_ge(winner_ready, 1)
            pool.wait_ge(cache_read, 16 * 2 * NSEQ * G1)
            pool.wait_ge(kv_stored, 16 * NSEQ)
            for b in range(NSEQ):
                for dst, col in ((kv_old, NSEQ + b), (kv_new, b)):
                    nc.gpsimd.indirect_dma_start(
                        out=dst[:, b, :], out_offset=None, in_=kv_d,
                        in_offset=bass.IndirectOffsetOnAxis(ap=winner_i[:, col:col + 1], axis=0),
                        bounds_check=NSEQ * P - 1, oob_is_err=False).then_inc(kv_gathered[b], 16)

        def winners_dve():
            dve, v = nc.vector, nc.vector
            n = 2 * (2 * (STEPS - 1) + 1)
            dve.wait_ge(winner_step, n)
            v.tensor_scalar(winner_f[:, :], winner[:, 0:16], 0.0, 4096.0, ALU.is_equal, ALU.mult).then_inc(winner_step, 1)
            dve.wait_ge(winner_step, n + 1)
            v.scalar_tensor_tensor(winner_i[:, :], winner[:, 0:16], -1.0, winner_f[:, :], ALU.add, ALU.add).then_inc(winner_ready, 1)

        def E_pe():
            pe, te = nc.tensor, nc.tensor
            for p in range(PAIRS):
                b = claim(E, 0, ("kT", p))
                for s in range(2):
                    pe.wait_ge(kv_gathered[2 * p + s], 32)
                    for i, src in enumerate((kv_old, kv_new)):
                        last = te.transpose(b[:, (2 * s + i) * P:(2 * s + i + 1) * P], src[:, 2 * p + s, 0:P], ident)
                last.then_inc(full_sem(E, ("kT", p)), 1)

        def E_dve():
            for p in range(PAIRS):
                b = filled(nc.vector, E, 0, ("kT", p))
                nc.vector.tensor_copy(kT_all[:, 2 * p:2 * p + 2, :].rearrange("p a b -> p (a b)"), b[:, :])\
                    .then_inc(free_sem(E, ("kT", p)), 1)

        NL = 8
        uses = []
        for n in range(NL + 3):
            if n < NL:
                uses.append((("S", n), n % 4))
            if 0 <= n - 2 < NL:
                uses.append((("T", n - 2), 4 + n % 2))
            if 0 <= n - 3 and (n - 3) % 4 == 3:
                uses.append((("O", (n - 3) // 4), 6 + (n - 3) // 4))
            if n == 8:
                uses.append((("OT", 0), 0))
            if n == 9:
                uses.append((("Y", 0), 6))
        uses += [(("OT", 1), 1), (("XT", 0), 2), (("Y", 1), 7), (("XT", 1), 3), ("logit", 4), (("H", 0), 5), (("H", 1), 0),
                 ("gatesT", 1), (("H", 2), 2), (("H", 3), 3), ("SH", 4), ("SY", 6)]
        uses += [(("E", e), (5, 7, 0, 1)[e % 4]) for e in range(E1)]
        Fp = Banks(uses, E.after, PAIRS)

        def wf(at, n):
            return w13f[:, 8192 + at:8192 + at + n]

        q_s = wf(0, 512).rearrange("p (c s q) -> p c s q", c=C1, s=2)
        k_s = wf(512, 512).rearrange("p (s k) -> p s k", s=2)
        v_s = wf(1024, 512).rearrange("p (s i d) -> p s i d", s=2, i=2)
        mask_s = wf(1536, 512).rearrange("p (s k) -> p s k", s=2)
        hT = wf(2048, 2048).rearrange("p (e n) -> p e n", e=E1)
        shT = wf(4096, 512).rearrange("p (c n) -> p c n", c=2)
        acc = wf(4608, 512).rearrange("p (s d) -> p s d", s=2)
        gates = wf(5120, 32).rearrange("p (s e) -> p s e", s=2)
        gatesT = wf(5152, 256).rearrange("p (s q) -> p s q", s=2)[0:9, :, :]
        lg1 = wf(5408, 16).rearrange("p (s e) -> p s e", s=2)
        gtmp = wf(5424, 16).rearrange("p (s e) -> p s e", s=2)
        out_s = wf(5440, 512).rearrange("p (s d) -> p s d", s=2)

        l1_max = sem("l1_max_ready")
        l1_probs = sem("l1_probs_ready")
        l1_pv = sem("l1_pv_done")
        l1_inv = sem("l1_inverse_sums_ready")
        kvq_copied = sem("q_k_v_copied")
        mask_step = sem("l1_mask_step")
        mask_ready = sem("l1_mask_ready")
        gate_step = sem("l1_gate_step")
        gate_exp = sem("l1_gate_exp_ready")
        gates_ready = sem("l1_gates_ready")
        acc_step = sem("l1_sum_step")
        out_ready = sem("out_rows_ready")
        out_stored = sem("out_stored")
        GATE_STEPS = 17

        def F_pool(it):
            pool, g = nc.gpsimd, nc.gpsimd
            if not isinstance(it, int) or it > 0:
                filled(pool, Fp, it - 1, ("O", 1))
            two = bass.ds(it * 2, 2)
            g.tensor_copy(q_s, qT_all[:, :, two, :])
            g.tensor_copy(k_s, kT_all[:, two, :])
            g.tensor_copy(v_s[:, :, 0, :], kv_old[:, two, P:])
            g.tensor_copy(v_s[:, :, 1, :], kv_new[:, two, P:]).then_inc(kvq_copied, 1)

        def F_pe(it):
            pe, te = nc.tensor, nc.tensor
            pe.wait_ge(kvq_copied, it + 1)

            def scores(n):
                s, g = n // 4, n % 4
                b = claim(Fp, it, ("S", n))
                for cc in range(C1):
                    last = te.matmul(b[:, cc * 256:(cc + 1) * 256], q_s[32 * g:32 * g + 32, cc, s, :],
                                     k_s[32 * g:32 * g + 32, s, :], start=True, stop=True)
                last.then_inc(full_sem(Fp, ("S", n)), 1)

            def transpose_probs(n):
                pe.wait_ge(l1_probs, it * NL + (n + 1))
                b = claim(Fp, it, ("T", n))
                for i in range(4):
                    last = te.transpose(b[:, i * P:(i + 1) * P], probs[:, n % 3, i * P:(i + 1) * P], ident)
                last.then_inc(full_sem(Fp, ("T", n)), 1)

            def values(n):
                s, g = n // 4, n % 4
                drained(pe, Fp, it, ("T", n))
                b = claim(Fp, it, ("O", s)) if g == 0 else bank[6 + s]
                for cc in range(C1):
                    for i in range(2):
                        last = te.matmul(b[:, cc * P + g * HD1:cc * P + (g + 1) * HD1],
                                         probsT[:, n % 2, (2 * cc + i) * P:(2 * cc + i + 1) * P],
                                         v_s[:, s, i, g * HD1:(g + 1) * HD1], start=(i == 0), stop=(i == 1))
                last.then_inc(l1_pv if g < 3 else full_sem(Fp, ("O", s)), 1)

            def transpose_rows(use, s, src):
                b = claim(Fp, it, (use, s))
                for k in range(KC):
                    last = te.transpose(b[:, k * P:(k + 1) * P], src[:, s, k * P:(k + 1) * P], ident)
                last.then_inc(full_sem(Fp, (use, s)), 1)

            def out_proj(s):
                drained(pe, Fp, it, ("OT", s))
                b = claim(Fp, it, ("Y", s))
                for k in range(KC):
                    last = te.matmul(b[:, 0:256], oT[:, k, s * P:(s + 1) * P], wo_1[:, k, :], start=(k == 0), stop=(k == KC - 1))
                last.then_inc(full_sem(Fp, ("Y", s)), 1)

            for n in range(NL + 3):
                if n < NL:
                    scores(n)
                if 0 <= n - 2 < NL:
                    transpose_probs(n - 2)
                if 0 <= n - 3:
                    values(n - 3)
                if n == 8:
                    drained(pe, Fp, it, ("O", 0))
                    transpose_rows("OT", 0, o_sb)
                if n == 9:
                    out_proj(0)
            drained(pe, Fp, it, ("O", 1))
            transpose_rows("OT", 1, o_sb)
            drained(pe, Fp, it, ("Y", 0))
            transpose_rows("XT", 0, y_sb)
            out_proj(1)
            drained(pe, Fp, it, ("Y", 1))
            transpose_rows("XT", 1, y_sb)
            drained(pe, Fp, it, ("XT", 0))
            drained(pe, Fp, it, ("XT", 1))
            b = claim(Fp, it, "logit")
            for s in range(2):
                for k in range(KC):
                    last = te.matmul(b[:, s * E1:(s + 1) * E1], xnT[:, k, s * P:(s + 1) * P], gate1[:, k, :],
                                     start=(k == 0), stop=(k == KC - 1))
            last.then_inc(full_sem(Fp, "logit"), 1)

            def up(hp):
                b = claim(Fp, it, ("H", hp))
                for i in range(2):
                    for k in range(KC):
                        last = te.matmul(b[:, i * 256:(i + 1) * 256], w1_1[:, 2 * hp + i, k, :], xnT[:, k, :],
                                         start=(k == 0), stop=(k == KC - 1))
                last.then_inc(full_sem(Fp, ("H", hp)), 1)

            up(0)
            up(1)
            pe.wait_ge(gates_ready, it + 1)
            b = claim(Fp, it, "gatesT")
            for s in range(2):
                last = te.transpose(b[0:9, s * P:(s + 1) * P], gates[:, s, 0:9], ident)
            last.then_inc(full_sem(Fp, "gatesT"), 1)
            up(2)
            up(3)
            b = claim(Fp, it, "SH")
            for i in range(2):
                for k in range(KC):
                    last = te.matmul(b[:, i * 256:(i + 1) * 256], sw1[:, k, i * P:(i + 1) * P], xnT[:, k, :],
                                     start=(k == 0), stop=(k == KC - 1))
            last.then_inc(full_sem(Fp, "SH"), 1)

            def down(e):
                drained(pe, Fp, it, ("H", e // 2))
                b = claim(Fp, it, ("E", e))
                for s in range(2):
                    last = te.matmul(b[:, s * 256:(s + 1) * 256], hT[:, e, s * P:(s + 1) * P], w2_1[:, e, :], start=True, stop=True)
                last.then_inc(full_sem(Fp, ("E", e)), 1)

            drained(pe, Fp, it, "gatesT")
            drained(pe, Fp, it, "SH")
            b = claim(Fp, it, "SY")
            for s in range(2):
                for k in range(2):
                    te.matmul(b[:, s * 256:(s + 1) * 256], shT[:, k, s * P:(s + 1) * P], sw2[:, k, :], start=(k == 0), stop=False)
                last = te.matmul(b[:, s * 256:(s + 1) * 256], gatesT[:, s, :], b2_s, start=False, stop=True)
            last.then_inc(full_sem(Fp, "SY"), 1)
            for e in range(E1):
                down(e)

        def F_dve(it):
            dve, v = nc.vector, nc.vector
            if not isinstance(it, int) or it > 0:
                drained(dve, Fp, it - 1, ("S", NL - 1))
            for s in range(2):
                v.tensor_scalar(mask_s[:, s, 0:P], c("key_row"), early[:, bass.ds(it * 2 + s, 1)], NEG, ALU.is_lt, ALU.mult)\
                    .then_inc(mask_step, 1)
                v.tensor_copy(mask_s[:, s, P:], c("causal"))
                dve.wait_ge(mask_step, it * 2 + (s + 1))
                v.tensor_tensor(mask_s[:, s, 0:P], mask_s[:, s, 0:P], c("older"), ALU.add).then_inc(mask_ready, 1)
            dve.wait_ge(mask_ready, it * 2 + 2)

            def mask_max(n):
                s = n // 4
                b, cnt = Fp.count(it, ("S", n))
                dve.wait_ge(bank_full[b], cnt + 1)
                wait(dve, l1_probs, it * NL + (n - 1))
                carry_waits(v)
                for cc in range(C1):
                    last = v.tensor_tensor_reduce(out=masked[:, n % 2, cc * 256:(cc + 1) * 256], in0=bank[b][:, cc * 256:(cc + 1) * 256],
                                                  in1=mask_s[:, s, :], scale=1.0, scalar=-3.0e38, op0=ALU.add, op1=ALU.max,
                                                  accum_out=row_max[:, n % 2, cc:cc + 1])
                last.then_inc(bank_free[b], 1)
                dve.wait_ge(bank_free[b], cnt + 1)
                v.tensor_scalar(neg_max[:, n % 3, 0:C1], row_max[:, n % 2, 0:C1], -(256.0 ** -0.5), None, ALU.mult).then_inc(l1_max, 1)

            def probsT_copy(n):
                b = filled(dve, Fp, it, ("T", n))
                if n >= 2:
                    s, g = (n - 2) // 4, (n - 2) % 4
                    if g < 3:
                        dve.wait_ge(l1_pv, it * 6 + (3 * s + g + 1))
                    else:
                        filled(dve, Fp, it, ("O", s))
                v.tensor_copy(probsT[:, n % 2, :], b[:, :]).then_inc(free_sem(Fp, ("T", n)), 1)

            def norm(s):
                dve.wait_ge(l1_probs, it * NL + (4 * s + 4))
                v.reciprocal(row_inv[:, s, 0:8], row_sum[:, s, 0:8]).then_inc(l1_inv, 1)
                dve.wait_ge(l1_inv, it * 2 + (s + 1))
                b = filled(dve, Fp, it, ("O", s))
                v.tensor_tensor(o_sb[:, s, :].rearrange("p (h d) -> p h d", h=8), b[:, 0:256].rearrange("p (h d) -> p h d", h=8),
                                row_inv[:, s, 0:8].unsqueeze(2).broadcast_to([P, 8, HD1]), ALU.mult).then_inc(free_sem(Fp, ("O", s)), 1)

            def halves_copy(use, s, dst):
                b = filled(dve, Fp, it, (use, s))
                v.tensor_copy(dst[:, :, s * P:(s + 1) * P], b[:, 0:256].rearrange("p (a b) -> p a b", a=2))\
                    .then_inc(free_sem(Fp, (use, s)), 1)

            for n in range(NL + 2):
                if n < NL:
                    mask_max(n)
                if 0 <= n - 2:
                    probsT_copy(n - 2)
                if n == 7:
                    norm(0)
                if n == 9:
                    halves_copy("OT", 0, oT)
            norm(1)
            halves_copy("OT", 1, oT)
            halves_copy("XT", 0, xnT)
            halves_copy("XT", 1, xnT)
            steps = [0]

            def link(ins):
                steps[0] += 1
                ins.then_inc(gate_step, 1)
                dve.wait_ge(gate_step, it * GATE_STEPS + steps[0])

            b = filled(dve, Fp, it, "logit")
            v.tensor_copy(lg1, b[:, 0:16].rearrange("p (s e) -> p s e", s=2)).then_inc(free_sem(Fp, "logit"), 1)
            drained(dve, Fp, it, "logit")
            top2(lg1, 2, link)
            dve.wait_ge(gate_exp, it + 1)
            top2_probs(2, link)
            link(v.tensor_tensor(gtmp, route["one1"][:, 0:2, :], p12[:, 0, 0:2].unsqueeze(2).broadcast_to([P, 2, E1]), ALU.mult))
            link(v.tensor_tensor(gates[:, :, 0:E1], route["one2"][:, 0:2, :], p12[:, 1, 0:2].unsqueeze(2).broadcast_to([P, 2, E1]), ALU.mult))
            v.memset(gates[:, :, E1:E1 + 1], 1.0)
            v.tensor_tensor(gates[:, :, 0:E1], gates[:, :, 0:E1], gtmp, ALU.add).then_inc(gates_ready, 1)
            assert steps[0] == GATE_STEPS
            b = filled(dve, Fp, it, "gatesT")
            v.tensor_copy(gatesT, b[0:9, 0:256].rearrange("p (s q) -> p s q", s=2)).then_inc(free_sem(Fp, "gatesT"), 1)
            b = filled(dve, Fp, it, "SY")
            v.tensor_tensor(acc[:, :, :], b[:, :].rearrange("p (s d) -> p s d", s=2), h_all[:, bass.ds(it * 2, 2), :], ALU.add)\
                .then_inc(free_sem(Fp, "SY"), 1)
            drained(dve, Fp, it, "SY")
            dve.wait_ge(gates_ready, it + 1)
            for e in range(E1):
                b = filled(dve, Fp, it, ("E", e))
                if e > 0:
                    drained(dve, Fp, it, ("E", e - 1))
                if e == E1 - 1:
                    wait(dve, out_stored, it * 16)
                for s in range(2):
                    last = v.scalar_tensor_tensor((acc if e < E1 - 1 else out_s)[:, s, :], b[:, s * 256:(s + 1) * 256],
                                                  gates[:, s, e:e + 1], acc[:, s, :], ALU.mult, ALU.add)
                last.then_inc(free_sem(Fp, ("E", e)), 1)

        def F_act(it):
            act, a = nc.scalar, nc.scalar
            for n in range(NL):
                act.wait_ge(l1_max, it * NL + (n + 1))
                if n >= 3:
                    filled(act, Fp, it, ("T", n - 3))
                for cc in range(C1):
                    h = cc * G1 + n % 4
                    last = a.activation(probs[:, n % 3, cc * 256:(cc + 1) * 256], masked[:, n % 2, cc * 256:(cc + 1) * 256],
                                        ACT.Exp, bias=neg_max[:, n % 3, cc:cc + 1], scale=256.0 ** -0.5,
                                        accum_out=row_sum[:, n // 4, h:h + 1])
                last.then_inc(l1_probs, 1)
            for s in range(2):
                b = filled(act, Fp, it, ("Y", s))
                a.activation(y_sb[:, s, :], b[:, 0:256], ACT.Copy).then_inc(free_sem(Fp, ("Y", s)), 1)
            act.wait_ge(gate_step, it * GATE_STEPS + 12)
            a.activation(pexp[:, 1, 0:2], pexp[:, 0, 0:2], ACT.Exp).then_inc(gate_exp, 1)
            for hp in range(4):
                b = filled(act, Fp, it, ("H", hp))
                for i in range(2):
                    e = 2 * hp + i
                    last = a.activation(hT[:, e, :], b[:, i * 256:(i + 1) * 256], ACT.Gelu, bias=b1_s[:, e:e + 1])
                last.then_inc(free_sem(Fp, ("H", hp)), 1)
            b = filled(act, Fp, it, "SH")
            for i in range(2):
                last = a.activation(shT[:, i, :], b[:, i * 256:(i + 1) * 256], ACT.Gelu, bias=sb1_s[:, i:i + 1])
            last.then_inc(free_sem(Fp, "SH"), 1)

        def F_store(it):
            sp = nc.sync
            drained(sp, Fp, it, ("E", E1 - 1))
            sp.dma_start(out[bass.ds(it * 2, 2), :, :].rearrange("s p d -> p s d"), out_s[:, :, :]).then_inc(out_stored, 16)

        def loop(eng, body, n):
            body(0)
            with eng.Fori(1, n) as it:
                body(it)

        block = ctx.enter_context(nc.Block())

        @block.sync
        def _(sp):
            sp.dma_start(const[:, :], t["const"]).then_inc(consts_loaded, 16)
            sp.dma_start(kvl[:, :], t["kv_lens"].rearrange("(o n) -> o n", o=1).broadcast_to([P, NSEQ])).then_inc(kvl_loaded, 16)
            sp.dma_start(x_in[:, :, :], t["x"][0:2, :, :].rearrange("s p d -> p s d")).then_inc(x_loaded, 16)
            for i, n in enumerate(("cWq", "cWk", "cWv", "cWo")):
                sp.dma_start(w_c[:, i, :, :], t[n].rearrange("(c p) n -> p c n", p=P)).then_inc(cond_w_loaded, 16)
            sp.dma_start(beta[:, :], t["cond_1"].rearrange("b o -> o b").broadcast_to([P, NSEQ])).then_inc(cond_w_loaded, 16)
            sp.dma_start(norm1[:, :], t["norm1"].rearrange("(c p) -> p c", p=P), allow_slow_non_contiguous=True).then_inc(cond_w_loaded, 16)
            sp.dma_start(norm2[:, :], t["norm2"].rearrange("(c p) -> p c", p=P), allow_slow_non_contiguous=True).then_inc(cond_w_loaded, 16)
            sp.dma_start(gate0[:, :, :], t["gate0"].rearrange("(c p) n -> p c n", p=P)).then_inc(cond_w_loaded, 16)
            sp.dma_start(w_kv[:, 1, :, :], t["wv"].rearrange("(c p) n -> p c n", p=P)).then_inc(attn_w_loaded, 16)
            sp.dma_start(w_kv[:, 0, :, :], t["wk"].rearrange("(c p) n -> p c n", p=P)).then_inc(attn_w_loaded, 16)
            sp.dma_start(wq, t["wq"].rearrange("(c p) n -> p c n", p=P)).then_inc(attn_w_loaded, 16)
            sp.dma_start(wo, t["wo"].rearrange("(h p) n -> p h n", p=P)).then_inc(attn_w_loaded, 16)
            sp.wait_ge(zero_ready, 1)
            zero_rows = xs_d.rearrange("(i p) d -> p i d", p=P)
            for a in range(0, TILES0, NSEQ):
                z = min(a + NSEQ, TILES0)
                sp.dma_start(zero_rows[:, a:z, :], kv_old[:, 0:z - a, :]).then_inc(zero_filled, 16)
            sp.wait_ge(kvl_loaded, 16)
            for b in range(NSEQ):
                n = sp.value_load(kvl[0:1, b:b + 1], min_val=0, max_val=NBLK * BLOCK - P)
                sp.dma_start(cs_all[:, b, :], t["rope"][bass.ds(n, P), :]).then_inc(rope_loaded, 16)

            def next_x(it):
                filled(sp, Ac, it, "xT")
                sp.dma_start(x_in[:, :, :], t["x"][bass.ds((it + 1) * 2, 2), :, :].rearrange("s p d -> p s d"))\
                    .then_inc(x_loaded, 16)

            next_x(0)
            for w, n in enumerate(("w1", "w3")):
                for e in range(E0):
                    sp.dma_start(w13[:, w, e, :, :], t[n][e, :, :].rearrange("(c p) n -> p c n", p=P)).then_inc(expert_w_loaded, 16)
            with sp.Fori(1, PAIRS - 1) as it:
                next_x(it)
            drained(sp, Af, PAIRS - 1, "logit")
            for e in range(E0):
                sp.dma_start(w2e[:, e, :, :], t["w2"][e, :, :].rearrange("(c p) n -> p c n", p=P)).then_inc(w2_loaded, 16)
            sp.wait_ge(scattered, 16 * 2 * NSEQ)
            C_load(0, 0)
            C_load(0, 1)
            C_load(0, 2)

            def step(j, k):
                C_load(j, k + 2)
                C_store(j, k - 1)

            step(0, 1)
            sp.dma_start(w_qkv, t["Wqkv1"].rearrange("(c p) n -> p c n", p=P)).then_inc(l1_loaded, 16)
            sp.dma_start(norm_w[:, 0:NQK * HD1], t["qk_scale"].rearrange("(o n) -> o n", o=1).broadcast_to([P, NQK * HD1])).then_inc(l1_loaded, 16)
            sp.dma_start(w1_1, t["l1w1"].rearrange("e (c p) n -> p e c n", p=P)).then_inc(l1_loaded, 16)
            sp.dma_start(w2_1, t["l1w2"].rearrange("e p n -> p e n")).then_inc(l1_loaded, 16)
            sp.dma_start(sw1, t["sw1"].rearrange("(c p) n -> p c n", p=P)).then_inc(l1_loaded, 16)
            sp.dma_start(sw2, t["sw2"].rearrange("(c p) n -> p c n", p=P)).then_inc(l1_loaded, 16)
            sp.dma_start(wo_1, t["Wo1"].rearrange("(c p) n -> p c n", p=P)).then_inc(l1_loaded, 16)
            sp.dma_start(gate1, t["gate1"].rearrange("(c p) n -> p c n", p=P)).then_inc(l1_loaded, 16)
            sp.dma_start(b1_s, t["b1"].rearrange("e p -> p e"), allow_slow_non_contiguous=True).then_inc(l1_loaded, 16)
            sp.dma_start(sb1_s, t["sb1"].rearrange("(c p) -> p c", p=P), allow_slow_non_contiguous=True).then_inc(l1_loaded, 16)
            sp.dma_start(b2_s[0:8, :], t["b2"]).then_inc(l1_loaded, 16)
            sp.dma_start(b2_s[8:9, :], t["sb2"].rearrange("(o n) -> o n", o=1)).then_inc(l1_loaded, 16)
            step(0, 2)
            with sp.Fori(1, STEPS - 1) as j:
                step(j, 1)
                step(j, 2)
            C_store(STEPS - 1, 0)
            C_store(STEPS - 1, 1)
            C_store(STEPS - 1, 2)
            sp.dma_start(x_in[:, :, :], t["x"][0:2, :, :].rearrange("s p d -> p s d")).then_inc(x_again, 16)
            D_store(0)
            with sp.Fori(1, PAIRS - 1) as it:
                D_store(it)
            D_store(PAIRS - 1)
            loop(sp, F_store, PAIRS)
            for i in range(2):
                sp.wait_ge(row_stored[i], 16 * ((TILES0 + 1 - i) // 2))
            sp.wait_ge(kv_stored, 16 * NSEQ)
            sp.wait_ge(zero_filled, 48)
            sp.wait_ge(scattered, 16 * 2 * NSEQ)
            sp.wait_ge(written_out, 16)
            sp.wait_ge(out_stored, 16 * PAIRS)

        @block.gpsimd
        def _(pool):
            nc.gpsimd.memset(neg_half[:, :], -0.5).then_inc(neg_half_ready, 1)
            pool.wait_ge(neg_half_ready, 1)
            pool.wait_ge(consts_loaded, 16)
            A_run(pool, A_pool)
            pool.wait_ge(slots_ready, 1)
            pool.wait_ge(written_out, 16)
            nc.gpsimd.dma_start(written, wl_d.rearrange("(o n) -> o n", o=1).broadcast_to([P, NSEQ * P])).then_inc(written_in, 16)
            nc.gpsimd.dma_start(row_no, t["row_no"].rearrange("(o n) -> o n", o=1).broadcast_to([P, NSEQ * P])).then_inc(written_in, 16)
            B_pool()
            cache_pool()
            D_gather()
            pool.wait_ge(rope_loaded, 16 * NSEQ)
            loop(pool, D_pool, PAIRS)
            E_pool()
            for b in range(NSEQ):
                pool.wait_ge(kv_gathered[b], 32)
            drained(pool, E, 0, ("kT", PAIRS - 1))
            loop(pool, F_pool, PAIRS)

        @block.scalar
        def _(act):
            act.wait_ge(beta_ready, 1)
            A_run(act, A_act)
            B_act()

            def first():
                C_act_step(0, 0)

            C_run(act, first, C_act_step, lambda: (C_act_step(STEPS - 1, 2), C_act_down(STEPS - 1, 2)))
            loop(act, D_act, PAIRS)
            act.wait_ge(l1_loaded, 16 * 12)
            loop(act, F_act, PAIRS)

        @block.vector
        def _(dve):
            dve.wait_ge(consts_loaded, 16)
            places_dve()
            dve.wait_ge(cond_w_loaded, 128)
            nc.vector.tensor_scalar(beta[:, :], beta[:, :], 4.0, CHD ** -0.5, ALU.min, ALU.mult).then_inc(beta_ready, 1)
            dve.wait_ge(zero_filled, 48)
            A_run(dve, A_dve)
            B_dve()
            dve.wait_ge(written_in, 32)

            def first():
                C_rowsT_copy(0, 0)
                C_dve_step(0, 0)

            C_run(dve, first, C_dve_step, lambda: (C_dve_step(STEPS - 1, 2, more=False), C_hidT_copy(STEPS - 1, 2)))
            winners_dve()
            dve.wait_ge(l1_loaded, 16 * 12)
            dve.wait_ge(rope_loaded, 16 * NSEQ)
            nc.vector.tensor_scalar(norm_w[:, 0:NQK * HD1], norm_w[:, 0:NQK * HD1], 1.0, None, ALU.add).then_inc(norm_w_ready, 1)
            dve.wait_ge(norm_w_ready, 1)
            dve.wait_ge(y_gathered, 16 * 2 * NSEQ)
            loop(dve, D_dve, PAIRS)
            E_dve()
            loop(dve, F_dve, PAIRS)

        @block.tensor
        def _(pe):
            pe.wait_ge(consts_loaded, 16)
            pe.wait_ge(cond_w_loaded, 128)
            A_run(pe, A_pe)
            B_pe()
            pe.wait_ge(expert_w_loaded, 16 * 2 * E0)
            pe.wait_ge(tile_e_ready, 1)

            def first():
                C_transpose_rows(0, 0)
                C_pe_step(0, 0)
                pe.wait_ge(w2_loaded, 16 * E0)

            C_run(pe, first, C_pe_step, lambda: (C_pe_step(STEPS - 1, 2, more=False), C_transpose_hidden(STEPS - 1, 2),
                                                 C_down(STEPS - 1, 2)))
            pe.wait_ge(l1_loaded, 16 * 12)
            loop(pe, D_pe, PAIRS)
            E_pe()
            loop(pe, F_pe, PAIRS)


def constants(np):
    a = {k: np.zeros((P, w), np.float32) for k, w in CONST_COLS.items()}
    i = np.arange(P)
    a["ident"][:] = np.eye(P)
    a["causal"][:] = np.where(i[None, :] <= i[:, None], 0.0, NEG)
    a["older"][:] = np.where(i[None, :] > i[:, None], 0.0, NEG)
    inv = (1.0 / np.float32(1000000.0) ** (np.arange(0, FHD, 2, dtype=np.float32) / np.float32(FHD))).astype(np.float32)
    ang = i.astype(np.float32)[None, :] * inv[:, None]
    a["cos"][:] = np.concatenate([np.cos(ang), np.cos(ang)])
    a["sin"][:] = np.concatenate([-np.sin(ang), np.sin(ang)])
    a["ones"][:] = 1.0
    a["before"][:] = i[:, None] < i[None, :]
    a["key_row"][:] = i[None, :]
    a["expert"][:] = np.tile(np.arange(8), 8)[None, :]
    a["expert8"][:] = np.tile(np.arange(8) + 8, 8)[None, :]
    a["below"][:] = np.tril(np.ones((8, 8)), -1).reshape(1, 64)
    a["tile_no"][:] = np.repeat(np.arange(TILES0), E0)[None, :]
    a["even"][:, 0] = (i // CHD) % 2 == 0
    a["odd"][:, 0] = (i // CHD) % 2 == 1
    a["row"][:, 0] = i
    a["seq_base"][:] = np.tile(np.arange(NSEQ) * NBLK, 2)[None, :]
    return np.ascontiguousarray(np.concatenate([a[k] for k in CONST_COLS], axis=1))


def kernel(**inputs):
    import numpy as np
    import concourse.bacc as bacc
    from concourse import mybir as mb
    from concourse.bass_utils import run_bass_kernel_spmd

    nc = bacc.Bacc("TRN2", target_bir_lowering=False, num_devices=1)
    g = {k: np.asarray(v) for k, v in inputs.items()}
    arrays = {"const": constants(np), "x": g["x"], "cond_1": g["cond_1"]}
    for n in ("Wq", "Wk", "Wv", "Wo"):
        arrays["c" + n] = np.ascontiguousarray(g["L0_cond_" + n].T)
    for n, k in (("norm1", "norm1_w"), ("norm2", "norm2_w"), ("wq", "wq"), ("wk", "wk"), ("wv", "wv"), ("wo", "wo"),
                 ("gate0", "gate_w"), ("w1", "w1"), ("w3", "w3"), ("w2", "w2")):
        arrays[n] = np.ascontiguousarray(g["L0_ffn_" + k])
    wq1 = g["L1_cond_Wq"].reshape(G1, C1, HD1, D).transpose(1, 0, 2, 3).reshape(D, D)
    arrays["Wqkv1"] = np.ascontiguousarray(np.concatenate([wq1, g["L1_cond_Wk"], g["L1_cond_Wv"]], axis=0).T)
    arrays["Wo1"] = np.ascontiguousarray(g["L1_cond_Wo"].reshape(D, G1, C1, HD1).transpose(2, 1, 3, 0).reshape(D, D))
    arrays["qk_scale"] = np.concatenate([np.tile(g["L1_cond_q_norm_scale"], 8), np.tile(g["L1_cond_k_norm_scale"], G1)])
    arrays["k_blocks"], arrays["v_blocks"] = g["L1_cond_k_blocks"], g["L1_cond_v_blocks"]
    arrays["table"] = g["itok_Bx257_0_4111"].reshape(NSEQ * NBLK, 1)
    arrays["kv_lens"] = g["itok_B_37_3939"]
    for n, k in (("gate1", "gate_w"), ("l1w1", "w1"), ("b1", "b1"), ("l1w2", "w2"), ("b2", "b2"), ("sw1", "shared_w1"),
                 ("sb1", "shared_b1"), ("sw2", "shared_w2"), ("sb2", "shared_b2")):
        arrays[n] = np.ascontiguousarray(g["L1_ffn_" + k])
    inv = (1.0 / np.float32(10000.0) ** (np.arange(HD1 // 2, dtype=np.float32) / np.float32(HD1 // 2))).astype(np.float32)
    ang = np.arange(NBLK * BLOCK, dtype=np.float32)[:, None] * inv[None, :]
    arrays["rope"] = np.concatenate([np.cos(ang), np.sin(ang)], axis=1).astype(np.float32)
    arrays["row_no"] = np.arange(1, NSEQ * P + 1, dtype=np.float32)
    t = {n: nc.dram_tensor("in_" + n, a.shape, mb.dt.from_np(a.dtype), kind="ExternalInput").ap() for n, a in arrays.items()}
    out = nc.dram_tensor("out", (NSEQ, P, D), mb.dt.float32, kind="ExternalOutput").ap()
    program(nc, t, out)
    r = run_bass_kernel_spmd(nc, [{"in_" + n: a for n, a in arrays.items()}], core_ids=[0])
    return r.results[0]["out"]
```

```python
import concourse.bass as bass
from concourse import mybir
from concourse.alu_op_type import AluOpType as ALU
from contextlib import ExitStack

P = 128
NSEQ, D = 8, 256
KC = D // P
PAIRS = NSEQ // 2
CH, CHD = 16, 16
FH, FKV, FHD = 16, 4, 128
E0, F0 = 8, 512
TILES0 = (2 * NSEQ * P + E0 * (P - 1)) // P
G1, HD1 = 4, 32
C1 = 2
NBLK, BLOCK = 257, 16
E1, H1 = 8, 128
SH1 = 2 * H1
ZERO_TILES = 4
ZERO_FILLS = -(-TILES0 // ZERO_TILES)
NEG = -1.0e30

CONST_COLS = dict(ident=P, causal=P, older=P, cos=P, sin=P, ones=P, before=P, key_row=P, expert=64,
                  expert8=64, below=64, tile_no=TILES0 * E0, even=1, odd=1, row=1, seq_base=16)
CONST_AT, _n = {}, 0
for _k, _w in CONST_COLS.items():
    CONST_AT[_k] = (_n, _w)
    _n += _w
CONST_N = _n


class Banks:

    def __init__(self, uses, before, times):
        self.base = list(before)
        self.per = [0] * 8
        self.at = {}
        for use, bank in uses:
            self.at[use] = (bank, self.per[bank])
            self.per[bank] += 1
        self.after = [b + times * p for b, p in zip(before, self.per)]

    def count(self, it, use):
        bank, k = self.at[use]
        return bank, it * self.per[bank] + (self.base[bank] + k)


class TileBanks:

    RINGS = dict(up=(0, 2), gate=(2, 2), hT=(4, 1), xT=(5, 1), down=(6, 2))

    def __init__(self, before, tiles):
        self.base = list(before)
        self.after = list(before)
        for first, ring in self.RINGS.values():
            for i in range(tiles):
                self.after[first + i % ring] += 1

    def count(self, j, use):
        name, c = use
        first, ring = self.RINGS[name]
        b = first + c % ring
        return b, (j + (self.base[b] + c // 2) if ring == 2 else j * 2 + (self.base[b] + c))


def program(nc, t, out):
    fp32, i32 = mybir.dt.float32, mybir.dt.int32
    ACT = mybir.ActivationFunctionType
    AX = mybir.AxisListType
    ctx = ExitStack()
    with ctx:
        def sb(name, shape, dt=fp32):
            return ctx.enter_context(nc.sbuf_tensor(name, shape, dt))

        def sem(name):
            return ctx.enter_context(nc.semaphore(name))

        bank = [ctx.enter_context(nc.psum_tensor(f"bank{i}", [P, 512], fp32)) for i in range(8)]
        bank_full = [sem(f"bank_full{i}") for i in range(8)]
        bank_free = [sem(f"bank_free{i}") for i in range(8)]

        xs_d = nc.dram_tensor("routed_rows", [TILES0 * P, D], fp32, kind="Internal").ap()
        ys_d = nc.dram_tensor("expert_rows", [TILES0 * P, D], fp32, kind="Internal").ap()
        kv_d = nc.dram_tensor("new_kv_rows", [NSEQ * P, D], fp32, kind="Internal").ap()
        wl_d = nc.dram_tensor("written_places", [NSEQ * P], fp32, kind="Internal").ap()

        const = sb("const", [P, CONST_N])

        def c(name):
            a, w = CONST_AT[name]
            return const[:, a:a + w]

        ident = c("ident")
        w_c = sb("cond_weights", [P, 4, KC, D])
        w_kv = sb("ffn_wk_wv", [P, 2, KC, FKV * FHD])
        w_qo = sb("ffn_wq_wo", [P, 8192])
        wq = w_qo[:, 0:4096].rearrange("p (c n) -> p c n", c=KC)
        wo = w_qo[:, 4096:8192].rearrange("p (h n) -> p h n", h=FH)
        w2e = w_qo[:, :].rearrange("p (e c n) -> p e c n", e=E0, c=F0 // P)
        w13 = sb("experts_w1_w3", [P, 2, E0, KC, F0])
        gate0 = sb("gate0", [P, KC, E0])
        norm1 = sb("norm1", [P, KC])
        norm2 = sb("norm2", [P, KC])
        beta = sb("beta", [P, NSEQ])
        x_in = sb("x_in", [P, 2, D])
        xT = sb("xT", [P, KC, 2 * P])
        cqT = sb("cond_qT", [P, KC, 2 * P])
        ckT = sb("cond_kT_masked", [P, KC, 2, 2 * P])
        cv = sb("cond_v_masked", [P, 2, 2, D])
        masked = sb("masked_scores", [P, 2, 512])
        probs = sb("probs", [P, 3, 512])
        probsT = sb("probsT", [P, 2, 512])
        oT = sb("attn_rowsT", [P, KC, 2 * P])
        y_sb = sb("cond_out", [P, 2, D])
        xn = sb("normed", [P, 2, D])
        xnT = sb("normedT", [P, KC, 2 * P])
        fqT = sb("ffn_qT", [P, 2, 4, 2 * P])
        fkT = sb("ffn_kT", [P, FKV, 2 * P])
        fv = sb("ffn_v", [P, 2, 512])
        swapped = sb("swapped", [P, 2, 512])
        foT = sb("ffn_oT", [P, 2, 512])
        junk = swapped[:, 0, 0:D]
        h_all = sb("h_all", [P, NSEQ, D])
        logits = sb("logits", [P, NSEQ, E0])
        row_max = sb("row_max", [P, 2, 4])
        neg_max = sb("neg_max", [P, 3, 4])
        fsum = sb("ffn_row_sum", [P, 3, 4])
        finv = sb("ffn_row_inv", [P, 3, 4])
        sq = sb("sum_squares", [P, 4])
        ms = sb("mean_squares", [P, 4])
        rstd = sb("rstd", [P, 4])
        rstd2 = sb("rstd2_all", [P, NSEQ])
        neg_half = sb("neg_half", [P, 16])
        carrier = sb("carrier", [1, 1])
        cos_b = c("cos")
        sin_b = c("sin")
        kv_old = sb("kv_old", [P, NSEQ, D])
        kv_new = sb("kv_new", [P, NSEQ, D])

        consts_loaded = sem("consts_loaded")
        neg_half_ready = sem("neg_half_ready")
        beta_ready = sem("beta_ready")
        cond_w_loaded = sem("cond_w_loaded")
        attn_w_loaded = sem("attn_w_loaded")
        expert_w_loaded = sem("expert_w_loaded")
        x_loaded = sem("x_loaded")

        def wait(eng, s, value):
            if not isinstance(value, int) or value > 0:
                eng.wait_ge(s, value)

        def carry_waits(v):
            v.memset(carrier[0:1, 0:1], 0.0)

        def claim(ph, it, use):
            b, n = ph.count(it, use)
            wait(nc.tensor, bank_free[b], n)
            return bank[b]

        def filled(eng, ph, it, use):
            b, n = ph.count(it, use)
            eng.wait_ge(bank_full[b], n + 1)
            return bank[b]

        def drained(eng, ph, it, use):
            b, n = ph.count(it, use)
            wait(eng, bank_free[b], n + 1)

        def full_sem(ph, use):
            return bank_full[ph.count(0, use)[0]]

        def free_sem(ph, use):
            return bank_free[ph.count(0, use)[0]]

        NU = 8
        STEPS_A = NU + 5

        def cond_unit(t):
            return t - 1

        def ffn_unit(t):
            return t - 3

        def ropes_of(t):
            return (2 * t - 2, 2 * t - 1) if t in (1, 2) else (t + 1,) if 3 <= t <= 8 else ()

        NR = 10
        uses = []
        for t_ in range(STEPS_A):
            v_ = cond_unit(t_)
            if t_ == 0:
                uses += [("xT", 2), ("cq", 0), ("ck", 2), ("cv", 3)]
            if 0 <= v_ < NU:
                uses.append((("cS", v_), 0))
            if 0 <= v_ - 1 < NU:
                uses.append((("cT", v_ - 1), 2))
            if v_ - 2 in (0, 4):
                uses.append((("cO", (v_ - 2) // 4), 3))
            uses += {7: [(("cY", 0), 2)], 10: [(("xn", 0), 2)], 11: [(("cY", 1), 2)], 12: [(("xn", 1), 2)]}.get(t_, [])
        Ac = Banks(uses, [0] * 8, PAIRS)
        uses = [(("fv", 0), 5), (("fv", 1), 1)]
        for t_ in range(STEPS_A):
            u_ = ffn_unit(t_)
            if 0 <= u_ < NU:
                uses.append((("fS", u_), 4))
            uses += [(("rope", r), (5, 1)[r % 2]) for r in ropes_of(t_)]
            if 0 <= u_ - 1 < NU:
                uses += [(("fT", u_ - 1), 6), (("fO", u_ - 1), 6)]
        uses += [("wo", 7), ("x2", 7), ("logit", 7)]
        Af = Banks(uses, [0] * 8, PAIRS)
        after_A = [a + b for a, b in zip(Ac.after, Af.after)]

        cprobs = kv_new[:, 0:6, :].rearrange("p (r a) d -> p r (a d)", r=3)
        y_keep = kv_new[:, 6:8, :]
        cprobsT = masked
        xn2 = kv_old[:, 0:2, :]
        x2T = kv_old[:, 2:4, :]
        junk = kv_old[:, 5, :]
        crow_max = kv_old[:, 4, 0:12].rearrange("p (r h) -> p r h", r=3)
        cneg_max = kv_old[:, 4, 16:28].rearrange("p (r h) -> p r h", r=3)
        frow_max = kv_old[:, 4, 32:44].rearrange("p (r h) -> p r h", r=3)
        csum = kv_old[:, 4, 48:60].rearrange("p (r h) -> p r h", r=3)
        cinv = kv_old[:, 4, 64:76].rearrange("p (r h) -> p r h", r=3)

        cond_max = sem("cond_max_ready")
        cond_probs = sem("cond_probs_ready")
        cond_pv = sem("cond_pv_done")
        cond_inv = sem("cond_inverse_sums_ready")
        cond_scaled = sem("cond_probs_scaled")
        cv_zero = sem("cond_v_zeroed")
        y_copied = sem("cond_out_copied")
        y_squares = sem("cond_out_squares_ready")
        y_kept = sem("cond_out_kept")
        y_rstd = sem("cond_out_rstd_ready")
        xn_ready = sem("normed_rows_ready")
        swap_ready = sem("rope_halves_swapped")
        sin_ready = sem("rope_sine_part_ready")
        rope_done = sem("rope_done")
        ffn_max = sem("ffn_max_ready")
        ffn_probs = sem("ffn_probs_ready")
        ffn_inv = sem("ffn_inverse_sums_ready")
        ffn_scaled = sem("ffn_probs_scaled")
        wo_done = sem("wo_step_done")
        h_squares = sem("h_squares_ready")
        h_mean = sem("h_mean_squares_ready")
        h_rstd = sem("h_rstd_ready")
        x2_ready = sem("x2_rows_ready")
        rstd2_ready = sem("rstd2_ready")

        def pe_transpose_probs(ph, it, use, n, ready, src):
            pe, te = nc.tensor, nc.tensor
            pe.wait_ge(ready, it * NU + (n + 1))
            b = claim(ph, it, (use, n))
            for i in range(4):
                last = te.transpose(b[:, i * P:(i + 1) * P], src[:, n % 3, i * P:(i + 1) * P], ident)
            last.then_inc(full_sem(ph, (use, n)), 1)

        def pe_transpose_rows(ph, it, use, s, src):
            b = claim(ph, it, (use, s))
            for k in range(KC):
                last = nc.tensor.transpose(b[:, k * P:(k + 1) * P], src[:, s, k * P:(k + 1) * P], ident)
            last.then_inc(full_sem(ph, (use, s)), 1)

        def pe_cond_start(i):
            pe, te = nc.tensor, nc.tensor
            pe.wait_ge(x_loaded, i * 16 + 16)
            b = claim(Ac, i, "xT")
            for k in range(KC):
                for s in range(2):
                    last = te.transpose(b[:, (k * 2 + s) * P:(k * 2 + s + 1) * P], x_in[:, s, k * P:(k + 1) * P], ident)
            last.then_inc(full_sem(Ac, "xT"), 1)

        def pe_cond_proj(i):
            pe, te = nc.tensor, nc.tensor
            drained(pe, Ac, i, "xT")
            for use, w in (("cq", 0), ("ck", 1)):
                b = claim(Ac, i, use)
                for fc in range(KC):
                    for k in range(KC):
                        last = te.matmul(b[:, fc * 256:(fc + 1) * 256], w_c[:, w, k, fc * P:(fc + 1) * P], xT[:, k, :],
                                         start=(k == 0), stop=(k == KC - 1))
                last.then_inc(full_sem(Ac, use), 1)
            b = claim(Ac, i, "cv")
            for s in range(2):
                for k in range(KC):
                    last = te.matmul(b[:, s * 256:(s + 1) * 256], xT[:, k, s * P:(s + 1) * P], w_c[:, 2, k, :],
                                     start=(k == 0), stop=(k == KC - 1))
            last.then_inc(full_sem(Ac, "cv"), 1)

        def pe_cond_scores(i, n):
            pe, te = nc.tensor, nc.tensor
            s, j = n // 4, n % 4
            if n == 0:
                drained(pe, Ac, i, "cq")
                drained(pe, Ac, i, "ck")
            b = claim(Ac, i, ("cS", n))
            for fc in range(2):
                last = te.matmul(b[:, fc * 256:(fc + 1) * 256], cqT[32 * j:32 * j + 32, fc, s * P:(s + 1) * P],
                                 ckT[32 * j:32 * j + 32, fc, :, s * P:(s + 1) * P], start=True, stop=True)
            last.then_inc(full_sem(Ac, ("cS", n)), 1)

        def pe_cond_values(i, n):
            pe, te = nc.tensor, nc.tensor
            s, j = n // 4, n % 4
            if n == 0:
                drained(pe, Ac, i, "cv")
            drained(pe, Ac, i, ("cT", n))
            b = claim(Ac, i, ("cO", s)) if j == 0 else bank[3]
            for fc in range(2):
                f = fc * P + j * 32
                for par in range(2):
                    q = 2 * fc + par
                    last = te.matmul(b[32 * j:32 * j + 32, fc * P:(fc + 1) * P], cv[:, par, s, f:f + 32],
                                     cprobsT[:, n % 2, q * P:(q + 1) * P], start=(par == 0), stop=(par == 1))
            last.then_inc(cond_pv if j < 3 else full_sem(Ac, ("cO", s)), 1)

        def pe_cond_late(i, t_):
            pe, te = nc.tensor, nc.tensor
            if t_ in (7, 11):
                s = (t_ - 7) // 4
                drained(pe, Ac, i, ("cO", s))
                b = claim(Ac, i, ("cY", s))
                for k in range(KC):
                    last = te.matmul(b[:, 0:256], oT[:, k, s * P:(s + 1) * P], w_c[:, 3, k, :],
                                     start=(k == 0), stop=(k == KC - 1))
                last.then_inc(full_sem(Ac, ("cY", s)), 1)
            if t_ in (10, 12):
                s = (t_ - 10) // 2
                pe.wait_ge(xn_ready, i * 2 + (s + 1))
                pe_transpose_rows(Ac, i, "xn", s, xn)

        def pe_values_proj(it, s):
            drained(nc.tensor, Ac, it, ("xn", s))
            b = claim(Af, it, ("fv", s))
            for k in range(KC):
                last = nc.tensor.matmul(b[:, :], xnT[:, k, s * P:(s + 1) * P], w_kv[:, 1, k, :],
                                        start=(k == 0), stop=(k == KC - 1))
            last.then_inc(full_sem(Af, ("fv", s)), 1)

        def pe_rope_proj(it, r):
            b = claim(Af, it, ("rope", r))
            for i in range(2):
                for k in range(KC):
                    f = (2 * r + i) * FHD if r < 2 else (2 * (r - 2) + i) * FHD
                    w = w_kv[:, 0, k, f:f + FHD] if r < 2 else wq[:, k, f:f + FHD]
                    last = nc.tensor.matmul(b[:, i * 256:(i + 1) * 256], w, xnT[:, k, :],
                                            start=(k == 0), stop=(k == KC - 1))
            last.then_inc(full_sem(Af, ("rope", r)), 1)

        def pe_ffn_scores(it, n):
            pe, te = nc.tensor, nc.tensor
            g, s = n // 2, n % 2
            if s == 0:
                pe.wait_ge(rope_done, it * NR + (2 * g + 4))
            b = claim(Af, it, ("fS", n))
            for i in range(4):
                last = te.matmul(b[:, i * P:(i + 1) * P], fqT[:, g % 2, i, s * P:(s + 1) * P],
                                 fkT[:, g, s * P:(s + 1) * P], start=True, stop=True)
            last.then_inc(full_sem(Af, ("fS", n)), 1)

        def pe_ffn_values(it, n):
            pe, te = nc.tensor, nc.tensor
            g, s = n // 2, n % 2
            if n < 2:
                drained(pe, Af, it, ("fv", n))
            drained(pe, Af, it, ("fT", n))
            b = claim(Af, it, ("fO", n))
            te.matmul(b[:, :], fv[:, s, g * FHD:(g + 1) * FHD], probsT[:, n % 2, :],
                      start=True, stop=True).then_inc(full_sem(Af, ("fO", n)), 1)

        def pe_ffn_out(it, n):
            pe, te = nc.tensor, nc.tensor
            g, s = n // 2, n % 2
            if n == 0:
                claim(Af, it, "wo")
            drained(pe, Af, it, ("fO", n))
            for i in range(4):
                last = te.matmul(bank[7][:, s * 256:(s + 1) * 256], foT[:, n % 2, i * P:(i + 1) * P],
                                 wo[:, 4 * g + i, :], start=(n == 0 and i == 0), stop=(g == 3 and i == 3),
                                 skip_group_check=True)
            if n == NU - 1:
                last.then_inc(full_sem(Af, "wo"), 1)

        def pe_tail(i, t_):
            pe, te = nc.tensor, nc.tensor
            if t_ == 2:
                pe.wait_ge(x2_ready, i * 2 + 2)
                b = claim(Af, i, "x2")
                for k in range(KC):
                    for s in range(2):
                        last = te.transpose(b[:, (k * 2 + s) * P:(k * 2 + s + 1) * P], xn2[:, s, k * P:(k + 1) * P], ident)
                last.then_inc(full_sem(Af, "x2"), 1)
            if t_ == 3:
                drained(pe, Af, i, "x2")
                b = claim(Af, i, "logit")
                for s in range(2):
                    for k in range(KC):
                        last = te.matmul(b[:, s * E0:(s + 1) * E0], x2T[:, k, s * P:(s + 1) * P], gate0[:, k, :],
                                         start=(k == 0), stop=(k == KC - 1))
                last.then_inc(full_sem(Af, "logit"), 1)

        def lag_of(ffn):
            return 0 if ffn else 1

        def A_pe(it, ffn, cond, tail):
            lag = lag_of(ffn)
            for t_ in range(STEPS_A + lag):
                u, v = ffn_unit(t_), cond_unit(t_)
                if t_ == 0 and cond:
                    pe_cond_start(it + 1)
                if t_ == 0 and ffn:
                    pe_values_proj(it, 0)
                    pe_values_proj(it, 1)
                if t_ == 0 and cond:
                    pe_cond_proj(it + 1)
                if cond and 0 <= v < NU:
                    pe_cond_scores(it + 1, v)
                if ffn:
                    for r in ropes_of(t_):
                        pe_rope_proj(it, r)
                if ffn and 0 <= u < NU:
                    pe_ffn_scores(it, u)
                if ffn and 0 <= u - 1 < NU:
                    pe_transpose_probs(Af, it, "fT", u - 1, ffn_scaled, probs)
                if cond and 0 <= v - 1 - lag < NU:
                    pe_transpose_probs(Ac, it + 1, "cT", v - 1 - lag, cond_scaled, cprobs)
                if tail:
                    pe_tail(it - 1, t_)
                if ffn and 0 <= u - 2 < NU:
                    pe_ffn_out(it, u - 2)
                if ffn and 0 <= u - 1 < NU:
                    pe_ffn_values(it, u - 1)
                if cond and 0 <= v - 2 - lag < NU:
                    pe_cond_values(it + 1, v - 2 - lag)
                if cond:
                    pe_cond_late(it + 1, t_ - lag)

        def dve_mask_max(ph, it, use, n, buf, rmax, nmax, scale, ready):
            dve, v = nc.vector, nc.vector
            b = filled(dve, ph, it, (use, n))
            carry_waits(v)
            for i in range(4):
                last = v.tensor_tensor_reduce(out=buf[:, n % 3, i * P:(i + 1) * P], in0=b[:, i * P:(i + 1) * P],
                                              in1=c("causal"), scale=1.0, scalar=-3.0e38, op0=ALU.add, op1=ALU.max,
                                              accum_out=rmax[:, n % 3, i:i + 1])
            last.then_inc(free_sem(ph, (use, n)), 1)
            drained(dve, ph, it, (use, n))
            v.tensor_scalar(nmax[:, n % 3, :], rmax[:, n % 3, :], -scale, None, ALU.mult).then_inc(ready, 1)

        def dve_copy(ph, it, use, dst, src=lambda b: b[:, :]):
            b = filled(nc.vector, ph, it, use)
            nc.vector.tensor_copy(dst, src(b)).then_inc(free_sem(ph, use), 1)

        def halves(b):
            return b[:, 0:256].rearrange("p (a b) -> p a b", a=2)

        def dve_cond_start(i):
            v = nc.vector
            dve_copy(Ac, i, "xT", xT[:, :, :].rearrange("p a b -> p (a b)"))

        def dve_cond_keys(i):
            v = nc.vector
            b = filled(v, Ac, i, "ck")
            bk = b[:, :].rearrange("p (a b) -> p a b", a=2)
            v.tensor_scalar(ckT[:, :, 0, :], bk, c("even"), None, ALU.mult)
            v.tensor_scalar(ckT[:, :, 1, :], bk, c("odd"), None, ALU.mult).then_inc(free_sem(Ac, "ck"), 1)

        def dve_cond_late(i, t_):
            dve, v = nc.vector, nc.vector
            if t_ in (7, 11):
                s = (t_ - 7) // 4
                dve_copy(Ac, i, ("cO", s), oT[:, :, s * P:(s + 1) * P], halves)
            if t_ in (9, 12):
                s = (t_ - 9) // 3
                dve.wait_ge(y_rstd, i * 2 + (s + 1))
                dve.wait_ge(y_copied, i * 2 + (s + 1))
                v.tensor_scalar(xn[:, s, :], y_sb[:, s, :], rstd[:, s:s + 1], None, ALU.mult).then_inc(xn_ready, 1)

        def dve_xnT(i, s):
            b = filled(nc.vector, Ac, i, ("xn", s))
            for k in range(KC):
                last = nc.vector.tensor_scalar(xnT[:, k, s * P:(s + 1) * P], b[:, k * P:(k + 1) * P], norm1[:, k:k + 1],
                                               None, ALU.mult)
            last.then_inc(free_sem(Ac, ("xn", s)), 1)

        def rope_dst(r):
            if r < 2:
                return fkT[:, 2 * r:2 * r + 2, :].rearrange("p a b -> p (a b)")
            g, i = (r - 2) // 2, (r - 2) % 2
            return fqT[:, g % 2, 2 * i:2 * i + 2, :].rearrange("p a b -> p (a b)")

        def dve_rope_cos(it, r):
            dve, v = nc.vector, nc.vector
            b = filled(dve, Af, it, ("rope", r))
            dve.wait_ge(swap_ready, it * NR + (r + 1))
            v.tensor_tensor(rope_dst(r).rearrange("p (a b) -> p a b", a=4), b[:, :].rearrange("p (a b) -> p a b", a=4),
                            cos_b.unsqueeze(1).broadcast_to([P, 4, P]), ALU.mult).then_inc(free_sem(Af, ("rope", r)), 1)

        def dve_rope_add(it, r):
            dve, v = nc.vector, nc.vector
            drained(dve, Af, it, ("rope", r))
            dve.wait_ge(sin_ready, it * NR + (r + 1))
            v.tensor_tensor(rope_dst(r), rope_dst(r), swapped[:, r % 2, :], ALU.add).then_inc(rope_done, 1)

        def dve_scale_probs(it, n):
            dve, v = nc.vector, nc.vector
            dve.wait_ge(ffn_probs, it * NU + (n + 1))
            v.reciprocal(finv[:, n % 3, :], fsum[:, n % 3, :]).then_inc(ffn_inv, 1)
            dve.wait_ge(ffn_inv, it * NU + (n + 1))
            pr = probs[:, n % 3, :].rearrange("p (a b) -> p a b", a=4)
            v.tensor_tensor(pr, pr, finv[:, n % 3, :].unsqueeze(2).broadcast_to([P, 4, P]), ALU.mult)\
                .then_inc(ffn_scaled, 1)

        def dve_tail(i, t_):
            dve, v = nc.vector, nc.vector
            if t_ == 0:
                b = filled(dve, Af, i, "wo")
                dve.wait_ge(y_kept, i + 1)
                v.tensor_tensor(h_all[:, bass.ds(i * 2, 2), :], b[:, :].rearrange("p (a b) -> p a b", a=2), y_keep,
                                ALU.add).then_inc(free_sem(Af, "wo"), 1)
            if t_ == 1:
                for s in range(2):
                    dve.wait_ge(h_rstd, i * 2 + (s + 1))
                    v.tensor_scalar(xn2[:, s, :], h_all[:, bass.ds(i * 2 + s, 1), :].rearrange("p a b -> p (a b)"),
                                    rstd[:, 2 + s:3 + s], None, ALU.mult).then_inc(x2_ready, 1)
                v.tensor_copy(rstd2[:, bass.ds(i * 2, 2)], rstd[:, 2:4]).then_inc(rstd2_ready, 1)
            if t_ == 2:
                b = filled(dve, Af, i, "x2")
                for k in range(KC):
                    last = v.tensor_scalar(x2T[:, k, :], b[:, k * 256:(k + 1) * 256], norm2[:, k:k + 1], None, ALU.mult)
                last.then_inc(free_sem(Af, "x2"), 1)
            if t_ == 4:
                dve_copy(Af, i, "logit", logits[:, bass.ds(i * 2, 2), :],
                         lambda b: b[:, 0:2 * E0].rearrange("p (a b) -> p a b", a=2))

        def A_dve(it, ffn, cond, tail):
            lag = lag_of(ffn)
            for t_ in range(STEPS_A + lag):
                u, v = ffn_unit(t_), cond_unit(t_)
                if tail and t_ == 0:
                    dve_tail(it - 1, t_)
                if cond and t_ == 0:
                    dve_cond_start(it + 1)
                if cond:
                    dve_cond_late(it + 1, t_ - lag)
                if cond and t_ - lag == 11:
                    dve_xnT(it + 1, 0)
                if cond and t_ == 0:
                    dve_cond_keys(it + 1)
                if cond and 0 <= v < NU:
                    dve_mask_max(Ac, it + 1, "cS", v, cprobs, crow_max, cneg_max, 1.0, cond_max)
                if tail and t_ > 0:
                    dve_tail(it - 1, t_)
                if ffn:
                    for r in ropes_of(t_):
                        dve_rope_cos(it, r)
                if ffn and 0 <= u < NU:
                    dve_mask_max(Af, it, "fS", u, probs, frow_max, neg_max, FHD ** -0.5, ffn_max)
                if ffn and 0 <= u - 1 < NU:
                    dve_copy(Af, it, ("fT", u - 1), probsT[:, (u - 1) % 2, :])
                if cond and 0 <= v - 1 - lag < NU:
                    dve_copy(Ac, it + 1, ("cT", v - 1 - lag), cprobsT[:, (v - 1 - lag) % 2, :])
                if ffn:
                    for r in ropes_of(t_):
                        dve_rope_add(it, r)
                if cond and 0 <= v - lag < NU:
                    n = v - lag
                    nc.vector.wait_ge(cond_probs, (it + 1) * NU + (n + 1))
                    nc.vector.reciprocal(cinv[:, n % 3, :], csum[:, n % 3, :]).then_inc(cond_inv, 1)
                if ffn and 0 <= u < NU:
                    dve_scale_probs(it, u)
            if cond:
                dve_xnT(it + 1, 1)

        def act_exps(it, n, m_ready, buf, nmax, scale, p_ready, sums):
            act, a = nc.scalar, nc.scalar
            act.wait_ge(m_ready, it * NU + (n + 1))
            for i in range(4):
                x = buf[:, n % 3, i * P:(i + 1) * P]
                last = a.activation(x, x, ACT.Exp, bias=nmax[:, n % 3, i:i + 1], scale=scale, accum_out=sums(n, i))
            last.then_inc(p_ready, 1)

        def act_cond_start(i):
            act, a = nc.scalar, nc.scalar
            b = filled(act, Ac, i, "cq")
            for s in range(2):
                last = a.activation(cqT[:, :, s * P:(s + 1) * P],
                                    b[:, :].rearrange("p (f t) -> p f t", f=2)[:, :, s * P:(s + 1) * P],
                                    ACT.Copy, scale=beta[:, bass.ds(i * 2 + s, 1)])
            last.then_inc(free_sem(Ac, "cq"), 1)
            b = filled(act, Ac, i, "cv")
            for par in range(2):
                dst = cv[:, par, :, :].rearrange("p s (h a d) -> p (s h) a d", a=2, d=CHD)[:, :, par, :]
                src = b[:, :].rearrange("p (h a d) -> p h a d", a=2, d=CHD)[:, :, par, :]
                last = a.activation(dst, src, ACT.Copy)
            last.then_inc(free_sem(Ac, "cv"), 1)

        def act_cond_rows(i, s):
            act, a = nc.scalar, nc.scalar
            b = filled(act, Ac, i, ("cY", s))
            wait(act, y_kept, i)
            a.activation(y_sb[:, s, :], b[:, 0:256], ACT.Copy).then_inc(y_copied, 1)
            a.activation(junk, b[:, 0:256], ACT.Square, accum_out=sq[:, s:s + 1]).then_inc(y_squares, 1)
            act.wait_ge(y_squares, i * 2 + (s + 1))
            a.activation(ms[:, s:s + 1], sq[:, s:s + 1], ACT.Copy, scale=1.0 / D, bias=1e-5).then_inc(free_sem(Ac, ("cY", s)), 1)

        def act_swap(it, r):
            act, a = nc.scalar, nc.scalar
            b = filled(act, Af, it, ("rope", r))
            wait(act, rope_done, it * NR + (r - 1))
            a.activation(swapped[0:64, r % 2, :], b[64:128, :], ACT.Copy)
            a.activation(swapped[64:128, r % 2, :], b[0:64, :], ACT.Copy).then_inc(swap_ready, 1)

        def act_tail(i):
            act, a = nc.scalar, nc.scalar
            drained(act, Af, i, "wo")
            for s in range(2):
                a.activation(junk, h_all[:, bass.ds(i * 2 + s, 1), :].rearrange("p a b -> p (a b)"), ACT.Square,
                             accum_out=sq[:, 2 + s:3 + s]).then_inc(h_squares, 1)
                act.wait_ge(h_squares, i * 2 + (s + 1))
                a.activation(ms[:, 2 + s:3 + s], sq[:, 2 + s:3 + s], ACT.Copy, scale=1.0 / D, bias=1e-5).then_inc(h_mean, 1)

        def A_act(it, ffn, cond, tail):
            act, a = nc.scalar, nc.scalar
            lag = lag_of(ffn)
            for t_ in range(STEPS_A + lag):
                u, v = ffn_unit(t_), cond_unit(t_)
                if tail and t_ == 0:
                    act_tail(it - 1)
                if ffn and t_ == 0:
                    if tail:
                        drained(act, Af, it - 1, "wo")
                    act.wait_ge(y_copied, it * 2 + 2)
                    a.activation(y_keep, y_sb[:, :, :], ACT.Copy).then_inc(y_kept, 1)
                    for s in range(2):
                        b = filled(act, Af, it, ("fv", s))
                        a.activation(fv[:, s, :], b[:, :], ACT.Copy).then_inc(free_sem(Af, ("fv", s)), 1)
                if cond and t_ == 0:
                    act_cond_start(it + 1)
                if cond and t_ - lag in (8, 12):
                    act_cond_rows(it + 1, (t_ - lag - 8) // 4)
                if ffn:
                    for r in ropes_of(t_):
                        act_swap(it, r)
                if cond and 0 <= v < NU:
                    act_exps(it + 1, v, cond_max, cprobs, cneg_max, 1.0, cond_probs,
                             lambda n, i: csum[:, n % 3, i:i + 1])
                if ffn and 0 <= u < NU:
                    act_exps(it, u, ffn_max, probs, neg_max, FHD ** -0.5, ffn_probs, lambda n, i: fsum[:, n % 3, i:i + 1])
                if ffn and 0 <= u - 1 < NU:
                    b = filled(act, Af, it, ("fO", u - 1))
                    a.activation(foT[:, (u - 1) % 2, :], b[:, :], ACT.Copy).then_inc(free_sem(Af, ("fO", u - 1)), 1)

        def A_pool(it, ffn, cond, tail):
            pool, g = nc.gpsimd, nc.gpsimd
            for t_ in range(STEPS_A):
                if tail and t_ == 0:
                    for s in range(2):
                        pool.wait_ge(h_mean, (it - 1) * 2 + (s + 1))
                        g.tensor_tensor(rstd[:, 2 + s:3 + s], ms[:, 2 + s:3 + s], neg_half[:, 0:1], ALU.pow).then_inc(h_rstd, 1)
                if ffn:
                    for r in ropes_of(t_):
                        pool.wait_ge(swap_ready, it * NR + (r + 1))
                        sw = swapped[:, r % 2, :].rearrange("p (a b) -> p a b", a=4)
                        g.tensor_tensor(sw, sw, sin_b.unsqueeze(1).broadcast_to([P, 4, P]), ALU.mult).then_inc(sin_ready, 1)
                if cond and 0 <= cond_unit(t_) < NU:
                    n = cond_unit(t_)
                    pool.wait_ge(cond_inv, (it + 1) * NU + (n + 1))
                    pr = cprobs[:, n % 3, :].rearrange("p (a b) -> p a b", a=4)
                    g.tensor_tensor(pr, pr, cinv[:, n % 3, :].unsqueeze(2).broadcast_to([P, 4, P]), ALU.mult)\
                        .then_inc(cond_scaled, 1)
                    if isinstance(it, int) and it == 0:
                        places_gather(2 * n)
                        places_gather(2 * n + 1)
                if cond and t_ in (8, 12):
                    s = (t_ - 8) // 4
                    drained(pool, Ac, it + 1, ("cY", s))
                    g.tensor_tensor(rstd[:, s:s + 1], ms[:, s:s + 1], neg_half[:, 0:1], ALU.pow).then_inc(y_rstd, 1)

        def A_run(eng, body):
            body(-1, ffn=False, cond=True, tail=False)
            if eng is nc.tensor:
                eng.wait_ge(attn_w_loaded, 64)
            body(0, ffn=True, cond=True, tail=False)
            if eng is nc.gpsimd:
                places_pool()
            if eng is nc.vector:
                eng.wait_ge(zero_filled, ZERO_FILLS * 16)
            with eng.Fori(1, PAIRS - 1) as it:
                body(it, ffn=True, cond=True, tail=True)
            body(PAIRS - 1, ffn=True, cond=False, tail=True)
            body(PAIRS, ffn=False, cond=False, tail=True)

        B = Banks([("rank", 0)], after_A, 1)
        route = {n: sb("route_" + n, [P, NSEQ, E0]) for n in ("eq", "one1", "one2", "rest", "slot")}
        rmax = sb("route_max", [P, 2, NSEQ])
        rcand = sb("route_first", [P, NSEQ])
        p12 = sb("route_probs", [P, 2, NSEQ])
        pexp = sb("route_exp", [P, 2, NSEQ])
        cum = sb("rows_before", [P, NSEQ + 1, E0])
        tiles_f = sb("tiles_of_expert", [P, 4, E0])
        tiles_i = sb("tiles_of_expert_int", [P, 2, E0], i32)
        slots_i = sb("slots", [P, 2, NSEQ], i32)
        slots_f = sb("slots_float", [P, 2, NSEQ])
        tile_e = sb("expert_of_tile", [1, TILES0], i32)
        tile_ef = sb("expert_of_tile_float", [1, TILES0])
        tile_cmp = sb("tile_compare", [1, TILES0 * E0])
        x2_all = fqT[:, :, :, :].rearrange("p a b c -> p (a b c)").rearrange("p (b d) -> p b d", b=NSEQ)

        route_step = sem("routing_step")
        exp_ready = sem("route_exp_ready")
        ones_ready = sem("route_counts_ready")
        x2_all_ready = sem("x2_all_ready")
        slots_ready = sem("slots_ready")
        tile_e_ready = sem("expert_of_tile_ready")
        zero_filled = sem("routed_rows_zero_filled")
        zero_ready = sem("zero_tile_ready")
        scattered = sem("rows_scattered")
        w2_loaded = sem("w2_loaded")
        l1_loaded = sem("layer1_weights_loaded")

        def top2(lg, n, link):
            v = nc.vector
            one, rest, eq = (route["one1"], route["one2"]), route["rest"], route["eq"]
            src = lg
            for i in range(2):
                link(v.tensor_reduce(rmax[:, i, 0:n], src, AX.X, ALU.max))
                link(v.tensor_tensor(eq[:, 0:n, :], src, rmax[:, i, 0:n].unsqueeze(2).broadcast_to([P, n, E0]), ALU.is_equal))
                link(v.scalar_tensor_tensor(eq[:, 0:n, :], eq[:, 0:n, :], -8.0,
                                            c("expert8").rearrange("p (a b) -> p a b", b=E0)[:, 0:n, :], ALU.mult, ALU.add))
                link(v.tensor_reduce(rcand[:, 0:n], eq[:, 0:n, :], AX.X, ALU.min))
                link(v.tensor_tensor(one[i][:, 0:n, :], c("expert").rearrange("p (a b) -> p a b", b=E0)[:, 0:n, :],
                                     rcand[:, 0:n].unsqueeze(2).broadcast_to([P, n, E0]), ALU.is_equal))
                if i == 0:
                    link(v.scalar_tensor_tensor(rest[:, 0:n, :], one[0][:, 0:n, :], NEG, lg, ALU.mult, ALU.add))
                    src = rest[:, 0:n, :]
            link(v.tensor_tensor(pexp[:, 0, 0:n], rmax[:, 1, 0:n], rmax[:, 0, 0:n], ALU.subtract))

        def top2_probs(n, link):
            v = nc.vector
            link(v.tensor_scalar(p12[:, 1, 0:n], pexp[:, 1, 0:n], 1.0, None, ALU.add))
            link(v.reciprocal(p12[:, 0, 0:n], p12[:, 1, 0:n]))
            link(v.tensor_tensor(p12[:, 1, 0:n], pexp[:, 1, 0:n], p12[:, 0, 0:n], ALU.mult))

        def B_dve():
            dve, v = nc.vector, nc.vector
            steps = [0]

            def link(ins):
                steps[0] += 1
                ins.then_inc(route_step, 1)
                dve.wait_ge(route_step, steps[0])

            drained(dve, Af, PAIRS - 1, "logit")
            top2(logits[:, :, :], NSEQ, link)
            v.tensor_tensor(route["eq"][:, :, :], route["one1"][:, :, :], route["one2"][:, :, :], ALU.add)\
                .then_inc(ones_ready, 1)
            link(v.memset(cum[:, 0, :], 0.0))
            b = filled(dve, B, 0, "rank")
            for i in range(NSEQ):
                link(v.tensor_tensor(cum[:, i + 1, :], cum[:, i, :], b[:, 64 + i * E0:64 + (i + 1) * E0], ALU.add))
            link(v.tensor_scalar(tiles_i[:, 0, :], cum[:, NSEQ, :], float(P - 1), None, ALU.add))
            link(v.tensor_scalar(tiles_i[:, 1, :], tiles_i[:, 0, :], 7, None, ALU.arith_shift_right))
            link(v.tensor_copy(tiles_f[:, 0, :], tiles_i[:, 1, :]))
            link(v.tensor_tensor(route["rest"][:, :, :], c("below").rearrange("p (a b) -> p a b", b=E0),
                                 tiles_f[:, 0, :].unsqueeze(1).broadcast_to([P, E0, E0]), ALU.mult))
            link(v.tensor_reduce(tiles_f[:, 1, :], route["rest"][:, :, :], AX.X, ALU.add))
            link(v.tensor_tensor(tiles_f[:, 2, :], tiles_f[:, 1, :], tiles_f[:, 0, :], ALU.add))
            link(v.tensor_scalar(tiles_f[:, 3, :], tiles_f[:, 1, :], float(P), None, ALU.mult))
            link(v.tensor_tensor(route["slot"][:, :, :].rearrange("p a b -> p (a b)"),
                                 cum[:, 0:NSEQ, :].rearrange("p a b -> p (a b)"), b[:, 0:64], ALU.add))
            link(v.tensor_tensor(route["slot"][:, :, :], route["slot"][:, :, :],
                                 tiles_f[:, 3, :].unsqueeze(1).broadcast_to([P, NSEQ, E0]), ALU.add))
            for i in range(2):
                link(v.tensor_tensor(route["rest"][:, :, :], route["one%d" % (i + 1)][:, :, :], route["slot"][:, :, :], ALU.mult))
                link(v.tensor_reduce(slots_f[:, i, :], route["rest"][:, :, :], AX.X, ALU.add))
            v.tensor_copy(slots_i[:, :, :], slots_f[:, :, :]).then_inc(slots_ready, 1)
            link(v.tensor_tensor(tile_cmp[:, :].rearrange("p (a b) -> p a b", b=E0),
                                 c("tile_no")[0:1, :].rearrange("p (a b) -> p a b", b=E0),
                                 tiles_f[0:1, 2, :].unsqueeze(1).broadcast_to([1, TILES0, E0]), ALU.is_ge))
            link(v.tensor_reduce(tile_ef[:, :], tile_cmp[:, :].rearrange("p (a b) -> p a b", b=E0), AX.X, ALU.add))
            v.tensor_scalar(tile_e[:, :], tile_ef[:, :], float(E0 - 1), None, ALU.min).then_inc(tile_e_ready, 1)
            dve.wait_ge(exp_ready, 1)
            top2_probs(NSEQ, link)
            dve.wait_ge(slots_ready, 1)
            nc.vector.memset(carrier[0:1, 0:1], 0.0).then_inc(free_sem(B, "rank"), 1)

        def B_pe():
            pe, te = nc.tensor, nc.tensor
            pe.wait_ge(ones_ready, 1)
            b = claim(B, 0, "rank")
            m = route["eq"][:, :, :].rearrange("p a b -> p (a b)")
            te.matmul(b[:, 0:64], c("before"), m, start=True, stop=True)
            te.matmul(b[:, 64:128], c("ones"), m, start=True, stop=True).then_inc(full_sem(B, "rank"), 1)

        def B_act():
            act = nc.scalar
            filled(act, Af, PAIRS - 1, ("fS", NU - 1))
            act.wait_ge(x2_ready, 2 * PAIRS)
            act.wait_ge(rstd2_ready, PAIRS)
            for b in range(NSEQ):
                last = nc.scalar.activation(x2_all[:, b, :], h_all[:, b, :], ACT.Copy, scale=rstd2[:, b:b + 1])
            last.then_inc(x2_all_ready, 1)
            act.wait_ge(route_step, 12)
            nc.scalar.activation(pexp[:, 1, :], pexp[:, 0, :], ACT.Exp).then_inc(exp_ready, 1)

        def B_pool():
            pool = nc.gpsimd
            pool.wait_ge(slots_ready, 1)
            pool.wait_ge(x2_all_ready, 1)
            pool.wait_ge(zero_filled, ZERO_FILLS * 16)
            for b in range(NSEQ):
                for i in range(2):
                    nc.gpsimd.indirect_dma_start(
                        out=xs_d, out_offset=bass.IndirectOffsetOnAxis(ap=slots_i[:, i, b:b + 1], axis=0),
                        in_=x2_all[:, b, :], in_offset=None).then_inc(scattered, 16)

        kvl = sb("kv_lens", [P, NSEQ], i32)
        pos = sb("positions", [P, 2 * NSEQ], i32)
        slot = sb("block_slots", [P, 2 * NSEQ], i32)
        off = sb("block_offsets", [P, 2 * NSEQ], i32)
        off_f = sb("block_offsets_float", [P, 2 * NSEQ])
        cache_f = sb("cache_rows_float", [P, NSEQ])
        table_at = sb("table_rows", [P, 2 * NSEQ], i32)
        block_no = sb("blocks", [P, 2 * NSEQ], i32)
        place = sb("places", [P, 24])
        winner = sb("last_writers", [P, 24])
        winner_i = sb("last_writers_int", [P, 2 * NSEQ], i32)
        winner_f = sb("last_writers_index", [P, 2 * NSEQ])
        cache_at = sb("cache_rows", [P, G1, NSEQ], i32)
        early = sb("positions_below_zero", [P, NSEQ])
        cs_all = sb("rope_rows", [P, NSEQ, 2 * BLOCK])
        written = kv_new[:, 0:4, :].rearrange("p a b -> p (a b)")
        row_no = kv_new[:, 4:8, :].rearrange("p a b -> p (a b)")
        winner_tmp = swapped[:, :, :].rearrange("p a b -> p (a b)")
        kvl_loaded = sem("kv_lens_loaded")
        place_step = sem("places_step")
        table_at_ready = sem("table_rows_ready")
        table_read = sem("table_read")
        pool_step = sem("pool_places_step")
        place_ready = sem("places_ready")
        written_out = sem("places_in_dram")
        written_in = sem("places_of_all_loaded")
        cache_read = sem("cache_read")
        winner_step = sem("winner_compared")
        winner_ready = sem("winner_ready")
        rope_loaded = sem("rope_rows_loaded")

        def places_dve():
            dve, v = nc.vector, nc.vector
            steps = [0]

            def link(ins):
                steps[0] += 1
                ins.then_inc(place_step, 1)
                dve.wait_ge(place_step, steps[0])

            v.memset(cv[:, :, :, :], 0.0).then_inc(cv_zero, 1)
            v.memset(kv_old[:, 0:ZERO_TILES, :], 0.0).then_inc(zero_ready, 1)
            v.memset(place[:, :], 0.0)
            dve.wait_ge(kvl_loaded, 16)
            v.tensor_scalar(early[:, :], kvl[:, :], -1.0, float(P), ALU.mult, ALU.add)
            v.tensor_scalar(pos[:, 0:NSEQ], kvl[:, :], c("row"), None, ALU.add)
            link(v.tensor_scalar(pos[:, NSEQ:], kvl[:, :], c("row"), -float(P), ALU.add, ALU.add))
            link(v.tensor_scalar(pos[:, NSEQ:], pos[:, NSEQ:], 0.0, None, ALU.max))
            v.tensor_scalar(off[:, :], pos[:, :], BLOCK - 1, None, ALU.bitwise_and)
            link(v.tensor_scalar(slot[:, :], pos[:, :], 4, None, ALU.arith_shift_right))
            v.tensor_copy(off_f[:, :], off[:, :])
            v.scalar_tensor_tensor(table_at[:, :], slot[:, :], float(NBLK - 1), c("seq_base"), ALU.min, ALU.add)\
                .then_inc(table_at_ready, 1)

        def places_gather(n):
            nc.gpsimd.indirect_dma_start(out=block_no[:, n:n + 1], out_offset=None, in_=t["table"],
                                         in_offset=bass.IndirectOffsetOnAxis(ap=table_at[:, n:n + 1], axis=0)).then_inc(table_read, 16)

        def places_pool():
            pool, g = nc.gpsimd, nc.gpsimd
            pool.wait_ge(table_read, 16 * 2 * NSEQ)
            n = [0]

            def link(ins):
                n[0] += 1
                ins.then_inc(pool_step, 1)
                pool.wait_ge(pool_step, n[0])

            link(g.tensor_scalar(place[:, 0:16], block_no[:, :], float(BLOCK), None, ALU.mult))
            link(g.tensor_tensor(place[:, 0:16], place[:, 0:16], off_f[:, :], ALU.add))
            g.dma_start(wl_d.rearrange("(b p) -> p b", p=P), place[:, 0:NSEQ], allow_slow_non_contiguous=True).then_inc(written_out, 16)
            link(g.tensor_scalar(cache_f[:, :], block_no[:, NSEQ:], float(BLOCK * G1), None, ALU.mult))
            link(g.tensor_tensor(cache_f[:, :], cache_f[:, :], off_f[:, NSEQ:], ALU.add))
            for i in range(G1):
                link(g.tensor_scalar(cache_at[:, i, :], cache_f[:, :], float(BLOCK * i), None, ALU.add))

        def cache_pool():
            for name, at in (("k_blocks", 0), ("v_blocks", P)):
                rows = t[name].rearrange("n g o d -> (n g o) d")
                for b in range(NSEQ):
                    for i in range(G1):
                        nc.gpsimd.indirect_dma_start(
                            out=kv_old[:, b, at + i * HD1:at + (i + 1) * HD1], out_offset=None, in_=rows,
                            in_offset=bass.IndirectOffsetOnAxis(ap=cache_at[:, i, b:b + 1], axis=0)).then_inc(cache_read, 16)

        C = TileBanks(B.after, TILES0)
        rows_in = x_in
        rowsT = xT[:, :, :].rearrange("p a (r b) -> p r a b", r=2)
        silu = masked
        hid = probs
        hidT = probsT[:, :, :].rearrange("p r (a b) -> p r a b", b=P)
        rows_out = cv[:, 0, :, :]
        row_loaded = [sem("row_loaded0"), sem("row_loaded1")]
        row_stored = [sem("row_stored0"), sem("row_stored1")]

        STEPS = (TILES0 - 1) // 2

        def C_pe_step(j, k, more=True):
            pe, te = nc.tensor, nc.tensor
            i = j * 2 + k
            e = pe.value_load(tile_e[0:1, bass.ds(i, 1)], min_val=0, max_val=E0 - 1)
            drained(pe, C, j, ("xT", k))

            def half(use, w):
                b = claim(C, j, (use, k))
                for q in range(KC):
                    last = te.matmul(b[:, :], rowsT[:, k % 2, q, :], w13[:, w, bass.ds(e, 1), q, :],
                                     start=(q == 0), stop=(q == KC - 1))
                last.then_inc(full_sem(C, (use, k)), 1)

            half("up", 0)
            if k > 0 or not isinstance(j, int) or j > 0:
                C_transpose_hidden(j, k - 1)
            half("gate", 1)
            if more:
                C_transpose_rows(j, k + 1)
            if k > 0 or not isinstance(j, int) or j > 0:
                C_down(j, k - 1)

        def C_transpose_rows(j, k):
            pe, te = nc.tensor, nc.tensor
            wait(pe, row_loaded[k % 2], (j + (k // 2 + 1)) * 16)
            b = claim(C, j, ("xT", k))
            for q in range(KC):
                last = te.transpose(b[:, q * P:(q + 1) * P], rows_in[:, k % 2, q * P:(q + 1) * P], ident)
            last.then_inc(full_sem(C, ("xT", k)), 1)

        def C_transpose_hidden(j, k):
            pe, te = nc.tensor, nc.tensor
            drained(pe, C, j, ("gate", k))
            b = claim(C, j, ("hT", k))
            for q in range(F0 // P):
                last = te.transpose(b[:, q * P:(q + 1) * P], hid[:, k % 2, q * P:(q + 1) * P], ident)
            last.then_inc(full_sem(C, ("hT", k)), 1)

        def C_down(j, k):
            pe, te = nc.tensor, nc.tensor
            e = pe.value_load(tile_e[0:1, bass.ds(j * 2 + k, 1)], min_val=0, max_val=E0 - 1)
            drained(pe, C, j, ("hT", k))
            b = claim(C, j, ("down", k))
            for q in range(F0 // P):
                last = te.matmul(b[:, 0:256], hidT[:, k % 2, q, :], w2e[:, bass.ds(e, 1), q, :],
                                 start=(q == 0), stop=(q == F0 // P - 1))
            last.then_inc(full_sem(C, ("down", k)), 1)

        def C_rowsT_copy(j, k):
            b = filled(nc.vector, C, j, ("xT", k))
            for q in range(KC):
                last = nc.vector.tensor_scalar(rowsT[:, k % 2, q, :], b[:, q * P:(q + 1) * P], norm2[:, q:q + 1], None, ALU.mult)
            last.then_inc(free_sem(C, ("xT", k)), 1)

        def last_writer(j, k):
            v = nc.vector
            col = bass.ds(j * 2 + (k - 1), 1)
            n = j * 4 + 2 * (k - 1)
            wait(v, winner_step, n)
            v.scalar_tensor_tensor(winner_tmp, written, place[:, col], row_no, ALU.is_equal, ALU.mult).then_inc(winner_step, 1)
            v.wait_ge(winner_step, n + 1)
            v.tensor_reduce(winner[:, col], winner_tmp, AX.X, ALU.max).then_inc(winner_step, 1)

        def C_hidT_copy(j, k):
            b = filled(nc.vector, C, j, ("hT", k))
            nc.vector.tensor_copy(hidT[:, k % 2, :, :].rearrange("p a b -> p (a b)"), b[:, :]).then_inc(free_sem(C, ("hT", k)), 1)

        def C_dve_step(j, k, more=True):
            dve, v = nc.vector, nc.vector
            if k > 0 or not isinstance(j, int) or j > 0:
                C_hidT_copy(j, k - 1)
            b = filled(dve, C, j, ("gate", k))
            drained(dve, C, j, ("up", k))
            v.tensor_tensor(hid[:, k % 2, :], silu[:, k % 2, :], b[:, :], ALU.mult).then_inc(free_sem(C, ("gate", k)), 1)
            if more:
                C_rowsT_copy(j, k + 1)
            if 0 < k and more:
                last_writer(j, k)

        def C_act_down(j, k):
            act = nc.scalar
            b = filled(act, C, j, ("down", k))
            if k >= 2 or not isinstance(j, int) or j > 0:
                wait(act, row_stored[k % 2], (j + k // 2) * 16)
            nc.scalar.activation(rows_out[:, k % 2, :], b[:, 0:256], ACT.Copy).then_inc(free_sem(C, ("down", k)), 1)

        def C_act_step(j, k):
            act = nc.scalar
            b = filled(act, C, j, ("up", k))
            if k >= 2 or not isinstance(j, int) or j > 0:
                drained(act, C, j, ("gate", k - 2))
            nc.scalar.activation(silu[:, k % 2, :], b[:, :], ACT.Silu).then_inc(free_sem(C, ("up", k)), 1)
            if k > 0 or not isinstance(j, int) or j > 0:
                C_act_down(j, k - 1)

        def C_load(j, k):
            sp = nc.sync
            if k >= 2 or not isinstance(j, int) or j > 0:
                filled(sp, C, j, ("xT", k - 2))
            sp.dma_start(rows_in[:, k % 2, :], xs_d[bass.ds((j * 2 + k) * P, P), :]).then_inc(row_loaded[k % 2], 16)

        def C_store(j, k):
            sp = nc.sync
            drained(sp, C, j, ("down", k))
            sp.dma_start(ys_d[bass.ds((j * 2 + k) * P, P), :], rows_out[:, k % 2, :]).then_inc(row_stored[k % 2], 16)

        def C_run(eng, first, step, last):
            first()
            step(0, 1)
            step(0, 2)
            with eng.Fori(1, STEPS - 1) as j:
                step(j, 1)
                step(j, 2)
            step(STEPS - 1, 1)
            last()

        uses = []
        for s_ in range(2):
            uses += [(("x1T", s_), (0, 5)[s_]), (("qkv", s_), 1 + s_)]
        Da = Banks(uses, C.after, PAIRS)
        Db = Banks([(("qT", 0), 3), (("qT", 1), 4)], C.after, PAIRS)
        after_D = [max(a, b) for a, b in zip(Da.after, Db.after)]
        w13f = w13[:, :, :, :, :].rearrange("p a e c f -> p (a e c f)")
        y_rows = [w13f[:, i * 2048:(i + 1) * 2048].rearrange("p (b d) -> p b d", b=NSEQ) for i in range(2)]
        x1_s = y_sb
        x1T = xT
        x_all = x2_all
        sq_rows = masked
        qn = probs
        qn_sin = oT[:, :, :].rearrange("p a b -> p (a b)")
        qkv_rows = swapped
        norm_w = cqT[:, :, :].rearrange("p a b -> p (a b)")
        w_qkv = fv[:, :, :].rearrange("p s n -> p (s n)").rearrange("p (c n) -> p c n", c=KC)
        w1_1 = w_c[:, :, :, :].rearrange("p a b c -> p (a b c)").rearrange("p (e c n) -> p e c n", e=E1, c=KC)
        w2_1 = w_kv[:, :, :, :].rearrange("p a b c -> p (a b c)").rearrange("p (e n) -> p e n", e=E1)
        sw1 = fkT[:, 0:2, :]
        sw2 = fkT[:, 2:4, :]
        wo_1 = foT[:, 0, :].rearrange("p (c n) -> p c n", c=C1)
        small = foT[:, 1, :]
        b1_s = small[:, 0:8]
        sb1_s = small[:, 8:10]
        gate1 = small[:, 16:32].rearrange("p (c n) -> p c n", c=KC)
        b2_s = small[0:9, 64:320]
        qT_all = fqT[:, :, :, :].rearrange("p a b c -> p (a b c)").rearrange("p (c b q) -> p c b q", c=C1, b=NSEQ)
        NQK = 12
        ssq = sb("qk_sum_squares", [P, 2, 16])
        rqk = sb("qk_rstd", [P, 2, 16])

        y_gathered = [sem("expert_rows_gathered%d" % p) for p in range(PAIRS)]
        x_added = sem("x_added")
        x1_step = sem("x1_step")
        x1_ready = sem("x1_rows_ready")
        x1_kept = sem("x1_rows_kept")
        x_again = sem("x_loaded_again")
        sq_ready = sem("qk_squares_ready")
        ms_step = sem("qk_mean_squares_step")
        ms_ready = sem("qk_mean_squares_ready")
        rqk_ready = sem("qk_rstd_ready")
        qn_step = sem("qk_norm_step")
        qn_ready = sem("qk_normed")
        qsin_ready = sem("qk_sine_part_ready")
        v_copied = sem("new_v_copied")
        rows_ready = sem("qkv_rows_ready")
        kv_stored = [sem("new_kv_stored%d" % i) for i in range(2)]
        norm_w_ready = sem("qk_norm_weights_ready")

        def D_add_x():
            pool, g = nc.gpsimd, nc.gpsimd
            pool.wait_ge(x_again, 16)
            pool.wait_ge(x2_all_ready, 1)
            g.tensor_tensor(h_all[:, :, :], h_all[:, :, :], x_all[:, :, :], ALU.add).then_inc(x_added, 1)

        def D_gather(n):
            b, i = n // 2, n % 2
            nc.gpsimd.indirect_dma_start(
                out=y_rows[i][:, b, :], out_offset=None, in_=ys_d,
                in_offset=bass.IndirectOffsetOnAxis(ap=slots_i[:, i, b:b + 1], axis=0)).then_inc(y_gathered[b // 2], 16)

        def pe_qT(i, s):
            pe, te = nc.tensor, nc.tensor
            pe.wait_ge(rows_ready, i * 2 + (s + 1))
            b = claim(Db, i, ("qT", s))
            for k in range(C1):
                last = te.transpose(b[:, k * P:(k + 1) * P], qkv_rows[:, s, k * P:(k + 1) * P], ident)
            last.then_inc(full_sem(Db, ("qT", s)), 1)

        def D_pe(it, qkv, rot, late):
            pe, te = nc.tensor, nc.tensor
            for s in range(2):
                i = it + 1
                if qkv:
                    pe.wait_ge(x1_ready, i * 2 + (s + 1))
                    b = claim(Da, i, ("x1T", s))
                    for k in range(KC):
                        last = te.transpose(b[:, k * P:(k + 1) * P], x1_s[:, s, k * P:(k + 1) * P], ident)
                    last.then_inc(full_sem(Da, ("x1T", s)), 1)
                if s == 0 and late:
                    pe_qT(it - 1, 1)
                if s == 1 and rot:
                    pe_qT(it, 0)
                if qkv:
                    drained(pe, Da, i, ("x1T", s))
                    b = claim(Da, i, ("qkv", s))
                    for k in range(KC):
                        last = te.matmul(b[:, :], x1T[:, k, s * P:(s + 1) * P], w_qkv[:, k, :], start=(k == 0), stop=(k == KC - 1))
                    last.then_inc(full_sem(Da, ("qkv", s)), 1)

        def D_dve(it, qkv, rot, late):
            dve, v = nc.vector, nc.vector

            def x1(i, s):
                if isinstance(i, int):
                    dve.wait_ge(y_gathered[i], 64)
                if not isinstance(i, int) or i > 0:
                    dve.wait_ge(x1_kept, i * 2 + (s - 1))
                    drained(dve, Da, i - 1, ("x1T", s))
                seq = bass.ds(i * 2 + s, 1)
                rows = x1_s[:, s, :]
                v.scalar_tensor_tensor(rows, y_rows[0][:, seq, :].rearrange("p a b -> p (a b)"), p12[:, 0, seq],
                                       h_all[:, seq, :].rearrange("p a b -> p (a b)"), ALU.mult, ALU.add).then_inc(x1_step, 1)
                dve.wait_ge(x1_step, i * 2 + (s + 1))
                v.scalar_tensor_tensor(rows, y_rows[1][:, seq, :].rearrange("p a b -> p (a b)"), p12[:, 1, seq], rows,
                                       ALU.mult, ALU.add).then_inc(x1_ready, 1)

            def mean_squares(i, s):
                n = i * 2 + (s + 1)
                dve.wait_ge(sq_ready, n)
                v.tensor_reduce(ssq[:, s, 0:NQK], sq_rows[:, s, 0:NQK * HD1].rearrange("p (h d) -> p h d", d=HD1), AX.X, ALU.add)\
                    .then_inc(ms_step, 1)
                dve.wait_ge(ms_step, n)
                v.tensor_scalar(ssq[:, s, 0:NQK], ssq[:, s, 0:NQK], 1.0 / HD1, 1e-6, ALU.mult, ALU.add).then_inc(ms_ready, 1)

            def normed(s):
                n = it * 2 + (s + 1)
                dve.wait_ge(rqk_ready, n)
                b = filled(dve, Da, it, ("qkv", s))
                dve.wait_ge(v_copied, n)
                q = qn[:, s, 0:NQK * HD1]
                v.tensor_tensor(q.rearrange("p (h d) -> p h d", d=HD1), b[:, 0:NQK * HD1].rearrange("p (h d) -> p h d", d=HD1),
                                rqk[:, s, 0:NQK].unsqueeze(2).broadcast_to([P, NQK, HD1]), ALU.mult).then_inc(free_sem(Da, ("qkv", s)), 1)
                drained(dve, Da, it, ("qkv", s))
                v.tensor_tensor(q, q, norm_w[:, 0:NQK * HD1], ALU.mult).then_inc(qn_ready, 1)
                dve.wait_ge(qn_ready, n)
                q4 = q.rearrange("p (h a d) -> p h a d", a=2, d=HD1 // 2)
                cs = cs_all[:, bass.ds(it * 2 + s, 1), :].rearrange("p a b -> p (a b)")
                for a in range(2):
                    last = v.tensor_tensor(cos4(s)[:, :, a, :], q4[:, :, a, :],
                                           cs[:, 0:HD1 // 2].unsqueeze(1).broadcast_to([P, NQK, HD1 // 2]), ALU.mult)
                last.then_inc(qn_step, 1)

            def rotated(s):
                n = it * 2 + (s + 1)
                dve.wait_ge(qn_step, n)
                dve.wait_ge(qsin_ready, n)
                if not isinstance(it, int) or it > 0:
                    dve.wait_ge(kv_stored[s], it * 16)
                    drained(dve, Db, it - 1, ("qT", s))
                r4 = qkv_rows[:, s, 0:NQK * HD1].rearrange("p (h a d) -> p h a d", a=2, d=HD1 // 2)
                v.tensor_tensor(r4[:, :, 0, :], cos4(s)[:, :, 0, :], sin4(s)[:, :, 1, :], ALU.subtract)
                v.tensor_tensor(r4[:, :, 1, :], cos4(s)[:, :, 1, :], sin4(s)[:, :, 0, :], ALU.add).then_inc(rows_ready, 1)

            if qkv:
                x1(it + 1, 0)
            if rot:
                mean_squares(it, 1)
                normed(0)
            if qkv:
                x1(it + 1, 1)
            if rot:
                rotated(0)
                normed(1)
            if qkv:
                mean_squares(it + 1, 0)
            if rot:
                rotated(1)

        def cos4(s):
            return w13f[:, 5120 + 512 * s:5120 + 512 * s + NQK * HD1].rearrange("p (h a d) -> p h a d", a=2, d=HD1 // 2)

        def sin4(s):
            return w13f[:, 4096 + 512 * s:4096 + 512 * s + NQK * HD1].rearrange("p (h a d) -> p h a d", a=2, d=HD1 // 2)

        def D_act(it, qkv, rot, late):
            act, a = nc.scalar, nc.scalar
            i = it + 1

            def x1T_copy(s):
                b = filled(act, Da, i, ("x1T", s))
                a.activation(x1T[:, :, s * P:(s + 1) * P], b[:, 0:256].rearrange("p (k t) -> p k t", k=KC), ACT.Copy)\
                    .then_inc(free_sem(Da, ("x1T", s)), 1)

            def keep(s):
                act.wait_ge(x1_ready, i * 2 + (s + 1))
                a.activation(h_all[:, bass.ds(i * 2 + s, 1), :].rearrange("p a b -> p (a b)"), x1_s[:, s, :], ACT.Copy)\
                    .then_inc(x1_kept, 1)

            def squares(s):
                b = filled(act, Da, i, ("qkv", s))
                if not isinstance(i, int) or i > 0:
                    act.wait_ge(ms_step, i * 2 + (s - 1))
                a.activation(sq_rows[:, s, 0:NQK * HD1], b[:, 0:NQK * HD1], ACT.Square).then_inc(sq_ready, 1)

            def v_copy(p, s):
                b = filled(act, Da, p, ("qkv", s))
                if not isinstance(p, int) or p > 0:
                    act.wait_ge(kv_stored[s], p * 16)
                a.activation(qkv_rows[:, s, NQK * HD1:], b[:, NQK * HD1:], ACT.Copy).then_inc(v_copied, 1)

            def qT_copy(p, s):
                b = filled(act, Db, p, ("qT", s))
                a.activation(qT_all[:, :, bass.ds(p * 2 + s, 1), :].rearrange("p c b q -> p c (b q)"),
                             b[:, 0:256].rearrange("p (c q) -> p c q", c=C1), ACT.Copy).then_inc(free_sem(Db, ("qT", s)), 1)

            if qkv:
                x1T_copy(0)
            if rot:
                v_copy(it, 1)
            if qkv:
                keep(0)
            if late:
                qT_copy(it - 1, 1)
            if qkv:
                squares(0)
                x1T_copy(1)
                v_copy(i, 0)
                keep(1)
            if rot:
                qT_copy(it, 0)
            if qkv:
                squares(1)

        def D_pool(it, qkv, rot, late):
            pool, g = nc.gpsimd, nc.gpsimd

            def rstds(i, s):
                pool.wait_ge(ms_ready, i * 2 + (s + 1))
                g.tensor_tensor(rqk[:, s, 0:NQK], ssq[:, s, 0:NQK], neg_half[:, 0:NQK], ALU.pow).then_inc(rqk_ready, 1)

            def sines(s):
                pool.wait_ge(qn_ready, it * 2 + (s + 1))
                q4 = qn[:, s, 0:NQK * HD1].rearrange("p (h a d) -> p h a d", a=2, d=HD1 // 2)
                cs = cs_all[:, bass.ds(it * 2 + s, 1), :].rearrange("p a b -> p (a b)")
                for a in range(2):
                    last = g.tensor_tensor(sin4(s)[:, :, a, :], q4[:, :, a, :],
                                           cs[:, HD1 // 2:].unsqueeze(1).broadcast_to([P, NQK, HD1 // 2]), ALU.mult)
                last.then_inc(qsin_ready, 1)

            first = isinstance(it, int) and it == 0
            if rot:
                rstds(it, 1)
                if first:
                    D_gather(14)
                sines(0)
                if first:
                    D_gather(15)
                sines(1)
            if qkv:
                rstds(it + 1, 0)

        def D_store(it, qkv, rot, late):
            sp = nc.sync
            for s in range(2 if rot else 0):
                sp.wait_ge(rows_ready, it * 2 + (s + 1))
                sp.wait_ge(v_copied, it * 2 + (s + 1))
                sp.dma_start(kv_d[bass.ds((it * 2 + s) * P, P), :], qkv_rows[:, s, 256:512]).then_inc(kv_stored[s], 16)

        def D_run(eng, body):
            if eng is nc.gpsimd:
                for i in range(2):
                    eng.wait_ge(row_stored[i], 16 * ((TILES0 + 1 - i) // 2))
                for n in range(14):
                    D_gather(n)
            body(-1, qkv=True, rot=False, late=False)
            body(0, qkv=True, rot=True, late=False)
            if eng is nc.vector:
                for p in range(2, PAIRS):
                    eng.wait_ge(y_gathered[p], 64)
            with eng.Fori(1, PAIRS - 1) as it:
                body(it, qkv=True, rot=True, late=True)
            body(PAIRS - 1, qkv=False, rot=True, late=True)
            body(PAIRS, qkv=False, rot=False, late=True)

        E = Banks([(("kT", p), (0, 5, 6, 7)[p]) for p in range(PAIRS)], after_D, 1)
        kT_all = w_qo[:, 0:2048].rearrange("p (b k) -> p b k", b=NSEQ)
        kv_gathered = [sem("kv_gathered%d" % b) for b in range(NSEQ)]

        def E_gather(b):
            if b < NSEQ:
                for dst, col in ((kv_old, NSEQ + b), (kv_new, b)):
                    nc.gpsimd.indirect_dma_start(
                        out=dst[:, b, :], out_offset=None, in_=kv_d,
                        in_offset=bass.IndirectOffsetOnAxis(ap=winner_i[:, col:col + 1], axis=0),
                        bounds_check=NSEQ * P - 1, oob_is_err=False).then_inc(kv_gathered[b], 16)

        def E_pool(p):
            E_gather(0)
            E_gather(1)
            drained(nc.gpsimd, Db, PAIRS - 1, ("qT", 1))
            nc.gpsimd.tensor_copy(q_s, qT_all[:, :, 0:2, :]).then_inc(qk_copied, 1)

        def winners_dve():
            dve, v = nc.vector, nc.vector
            n = 2 * (2 * (STEPS - 1) + 1)
            dve.wait_ge(winner_step, n)
            v.tensor_scalar(winner_f[:, :], winner[:, 0:16], 0.0, 4096.0, ALU.is_equal, ALU.mult).then_inc(winner_step, 1)
            dve.wait_ge(winner_step, n + 1)
            v.scalar_tensor_tensor(winner_i[:, :], winner[:, 0:16], -1.0, winner_f[:, :], ALU.add, ALU.add).then_inc(winner_ready, 1)

        def E_pe(p):
            pe, te = nc.tensor, nc.tensor
            b = claim(E, 0, ("kT", p))
            for s in range(2):
                pe.wait_ge(kv_gathered[2 * p + s], 32)
                for i, src in enumerate((kv_old, kv_new)):
                    last = te.transpose(b[:, (2 * s + i) * P:(2 * s + i + 1) * P], src[:, 2 * p + s, 0:P], ident)
            last.then_inc(full_sem(E, ("kT", p)), 1)

        def E_dve(p):
            b = filled(nc.vector, E, 0, ("kT", p))
            dst = k_s if p == 0 else kT_all[:, 2 * p:2 * p + 2, :]
            nc.vector.tensor_copy(dst.rearrange("p a b -> p (a b)"), b[:, :])\
                .then_inc(free_sem(E, ("kT", p)), 1)

        NL = 8
        STEPS_F = NL + 6
        DOWNS = {4: 0, 6: 1, 8: 2, 9: 3, 10: 4, 11: 5, 12: 6, 13: 7}
        uses = []
        for n in range(STEPS_F):
            if n < NL:
                uses.append((("S", n), n % 2))
            if 0 <= n - 2 < NL:
                uses.append((("T", n - 2), 3))
            if n - 3 in (0, 4):
                uses.append((("O", (n - 3) // 4), (2, 4)[(n - 3) // 4]))
            uses += {8: [(("Y", 0), 2)], 9: [(("XT", 0), 2)], 11: [(("Y", 1), 4)], 12: [(("XT", 1), 4)],
                     13: [("logit", 3)]}.get(n, [])
        Fa = Banks(uses, E.after, PAIRS)
        uses = [(("H", 0), 5), (("H", 1), 6), (("H", 2), 7), (("H", 3), 5), ("SH", 6), ("gatesT", 7), ("SY", 5)]
        uses += [(("E", e), (6, 7, 5)[e % 3]) for e in range(E1)]
        Fm = Banks(uses, E.after, PAIRS)

        def wf(at, n):
            return w13f[:, 8192 + at:8192 + at + n]

        q_s = wf(0, 512).rearrange("p (c s q) -> p c s q", c=C1, s=2)
        k_s = wf(512, 512).rearrange("p (s k) -> p s k", s=2)
        v_s = wf(1024, 512).rearrange("p (s i d) -> p s i d", s=2, i=2)
        mask_s = wf(1536, 512).rearrange("p (s k) -> p s k", s=2)
        hT = wf(2048, 2048).rearrange("p (e n) -> p e n", e=E1)
        shT = wf(4096, 512).rearrange("p (c n) -> p c n", c=2)
        acc = wf(4608, 512).rearrange("p (s d) -> p s d", s=2)
        gates = wf(5120, 32).rearrange("p (s e) -> p s e", s=2)
        gatesT = wf(5152, 256).rearrange("p (s q) -> p s q", s=2)[0:9, :, :]
        lg1 = wf(5408, 16).rearrange("p (s e) -> p s e", s=2)
        gtmp = wf(5424, 16).rearrange("p (s e) -> p s e", s=2)
        out_s = wf(5440, 512).rearrange("p (s d) -> p s d", s=2)

        l1_max = sem("l1_max_ready")
        l1_probs = sem("l1_probs_ready")
        l1_pv = sem("l1_pv_done")
        l1_inv = sem("l1_inverse_sums_ready")
        l1_scaled = sem("l1_probs_scaled")
        qk_copied = sem("q_k_copied")
        values_copied = sem("cached_values_copied")
        mask_step = sem("l1_mask_step")
        mask_ready = sem("l1_mask_ready")
        gate_step = sem("l1_gate_step")
        gate_exp = sem("l1_gate_exp_ready")
        gates_ready = sem("l1_gates_ready")
        out_stored = sem("out_stored")
        GATE_STEPS = 17

        def l1_scale(engine, n):
            pr = probs[:, n % 3, :].rearrange("p (c k) -> p c k", c=C1)
            engine.tensor_tensor(pr, pr, finv[:, n % 3, 0:C1].unsqueeze(2).broadcast_to([P, C1, 256]), ALU.mult)\
                .then_inc(l1_scaled, 1)

        def F_pool(it, att, moe):
            if not att:
                return
            pool, g, i = nc.gpsimd, nc.gpsimd, it + 1
            later = not isinstance(i, int) or i > 0
            two = bass.ds(i * 2, 2)
            if later:
                filled(pool, Fa, i - 1, ("S", NL - 1))
                if isinstance(i, int):
                    drained(pool, E, 0, ("kT", i))
                g.tensor_copy(q_s, qT_all[:, :, two, :])
                g.tensor_copy(k_s, kT_all[:, two, :]).then_inc(qk_copied, 1)
            if isinstance(i, int):
                for s in range(2):
                    pool.wait_ge(kv_gathered[2 * i + s], 32)
            if later:
                filled(pool, Fa, i - 1, ("O", 1))
            g.tensor_copy(v_s[:, :, 0, :], kv_old[:, two, P:])
            g.tensor_copy(v_s[:, :, 1, :], kv_new[:, two, P:]).then_inc(values_copied, 1)
            for n in range(NL):
                if isinstance(i, int) and i == 0:
                    E_gather(n + 2)
                else:
                    pool.wait_ge(l1_inv, i * NL + (n + 1))
                    l1_scale(g, n)

        def pe_l1_scores(i, n):
            s, g = n // 4, n % 4
            if n == 0:
                nc.tensor.wait_ge(qk_copied, i + 1)
                if isinstance(i, int) and i == 0:
                    drained(nc.tensor, E, 0, ("kT", 0))
            b = claim(Fa, i, ("S", n))
            for cc in range(C1):
                last = nc.tensor.matmul(b[:, cc * 256:(cc + 1) * 256], q_s[32 * g:32 * g + 32, cc, s, :],
                                        k_s[32 * g:32 * g + 32, s, :], start=True, stop=True)
            last.then_inc(full_sem(Fa, ("S", n)), 1)

        def pe_l1_transpose(i, n):
            pe, te = nc.tensor, nc.tensor
            pe.wait_ge(l1_scaled, i * NL + (n + 1))
            b = claim(Fa, i, ("T", n))
            for q in range(4):
                last = te.transpose(b[:, q * P:(q + 1) * P], probs[:, n % 3, q * P:(q + 1) * P], ident)
            last.then_inc(full_sem(Fa, ("T", n)), 1)

        def pe_l1_values(i, n):
            pe, te = nc.tensor, nc.tensor
            s, g = n // 4, n % 4
            if n == 0:
                pe.wait_ge(values_copied, i + 1)
            drained(pe, Fa, i, ("T", n))
            b = claim(Fa, i, ("O", s)) if g == 0 else bank[(2, 4)[s]]
            pT = probsT[:, n % 2, :].rearrange("p (c k q) -> p c k q", c=C1, k=2)
            for q in range(2):
                last = te.matmul(b[g * HD1:(g + 1) * HD1, 0:256], v_s[:, s, q, g * HD1:(g + 1) * HD1], pT[:, :, q, :],
                                 start=(q == 0), stop=(q == 1))
            last.then_inc(l1_pv if g < 3 else full_sem(Fa, ("O", s)), 1)

        def pe_attention(i, n):
            pe, te = nc.tensor, nc.tensor

            def transpose_rows(use, s, src):
                b = claim(Fa, i, (use, s))
                for k in range(KC):
                    last = te.transpose(b[:, k * P:(k + 1) * P], src[:, s, k * P:(k + 1) * P], ident)
                last.then_inc(full_sem(Fa, (use, s)), 1)

            if n < NL:
                pe_l1_scores(i, n)
            if 0 <= n - 2 < NL:
                pe_l1_transpose(i, n - 2)
            if 0 <= n - 3 < NL:
                pe_l1_values(i, n - 3)
            s = (n - 8) // 3
            if n in (8, 11):
                drained(pe, Fa, i, ("O", s))
                b = claim(Fa, i, ("Y", s))
                for k in range(KC):
                    last = te.matmul(b[:, 0:256], oT[:, k, s * P:(s + 1) * P], wo_1[:, k, :], start=(k == 0), stop=(k == KC - 1))
                last.then_inc(full_sem(Fa, ("Y", s)), 1)
            if n in (9, 12):
                drained(pe, Fa, i, ("Y", s))
                transpose_rows("XT", s, y_sb)
            if n == 13:
                drained(pe, Fa, i, ("XT", 0))
                drained(pe, Fa, i, ("XT", 1))
                b = claim(Fa, i, "logit")
                for s in range(2):
                    for k in range(KC):
                        last = te.matmul(b[:, s * E1:(s + 1) * E1], xnT[:, k, s * P:(s + 1) * P], gate1[:, k, :],
                                         start=(k == 0), stop=(k == KC - 1))
                last.then_inc(full_sem(Fa, "logit"), 1)

        def pe_experts(it, n):
            pe, te = nc.tensor, nc.tensor
            if n == 1:
                for hp in range(4):
                    b = claim(Fm, it, ("H", hp))
                    for i in range(2):
                        for k in range(KC):
                            last = te.matmul(b[:, i * 256:(i + 1) * 256], w1_1[:, 2 * hp + i, k, :], xnT[:, k, :],
                                             start=(k == 0), stop=(k == KC - 1))
                    last.then_inc(full_sem(Fm, ("H", hp)), 1)
                b = claim(Fm, it, "SH")
                for i in range(2):
                    for k in range(KC):
                        last = te.matmul(b[:, i * 256:(i + 1) * 256], sw1[:, k, i * P:(i + 1) * P], xnT[:, k, :],
                                         start=(k == 0), stop=(k == KC - 1))
                last.then_inc(full_sem(Fm, "SH"), 1)
            if n == 2:
                pe.wait_ge(gates_ready, it + 1)
                b = claim(Fm, it, "gatesT")
                for s in range(2):
                    last = te.transpose(b[0:9, s * P:(s + 1) * P], gates[:, s, 0:9], ident)
                last.then_inc(full_sem(Fm, "gatesT"), 1)
            if n == 3:
                drained(pe, Fm, it, "gatesT")
                drained(pe, Fm, it, "SH")
                b = claim(Fm, it, "SY")
                for s in range(2):
                    for k in range(2):
                        te.matmul(b[:, s * 256:(s + 1) * 256], shT[:, k, s * P:(s + 1) * P], sw2[:, k, :], start=(k == 0), stop=False)
                    last = te.matmul(b[:, s * 256:(s + 1) * 256], gatesT[:, s, :], b2_s, start=False, stop=True)
                last.then_inc(full_sem(Fm, "SY"), 1)
            if n in DOWNS:
                e = DOWNS[n]
                drained(pe, Fm, it, ("H", e // 2))
                b = claim(Fm, it, ("E", e))
                for s in range(2):
                    last = te.matmul(b[:, s * 256:(s + 1) * 256], hT[:, e, s * P:(s + 1) * P], w2_1[:, e, :], start=True, stop=True)
                last.then_inc(full_sem(Fm, ("E", e)), 1)

        def F_pe(it, att, moe):
            for n in range(STEPS_F):
                if att:
                    pe_attention(it + 1, n)
                if not moe and 9 <= n < 9 + PAIRS - 1:
                    E_pe(n - 8)
                if moe:
                    pe_experts(it, n)

        def dve_masks(i):
            dve, v = nc.vector, nc.vector
            if not isinstance(i, int) or i > 0:
                drained(dve, Fa, i - 1, ("S", NL - 1))
            for s in range(2):
                v.tensor_scalar(mask_s[:, s, 0:P], c("key_row"), early[:, bass.ds(i * 2 + s, 1)], NEG, ALU.is_lt, ALU.mult)\
                    .then_inc(mask_step, 1)
                v.tensor_copy(mask_s[:, s, P:], c("causal"))
                dve.wait_ge(mask_step, i * 2 + (s + 1))
                v.tensor_tensor(mask_s[:, s, 0:P], mask_s[:, s, 0:P], c("older"), ALU.add).then_inc(mask_ready, 1)
            dve.wait_ge(mask_ready, i * 2 + 2)

        def dve_l1_max(i, n):
            dve, v = nc.vector, nc.vector
            s = n // 4
            b = filled(dve, Fa, i, ("S", n))
            wait(dve, l1_probs, i * NL + (n - 1))
            carry_waits(v)
            for cc in range(C1):
                last = v.tensor_tensor_reduce(out=masked[:, n % 2, cc * 256:(cc + 1) * 256], in0=b[:, cc * 256:(cc + 1) * 256],
                                              in1=mask_s[:, s, :], scale=1.0, scalar=-3.0e38, op0=ALU.add, op1=ALU.max,
                                              accum_out=row_max[:, n % 2, cc:cc + 1])
            last.then_inc(free_sem(Fa, ("S", n)), 1)
            drained(dve, Fa, i, ("S", n))
            v.tensor_scalar(neg_max[:, n % 3, 0:C1], row_max[:, n % 2, 0:C1], -(256.0 ** -0.5), None, ALU.mult).then_inc(l1_max, 1)

        def dve_l1_probsT(i, n):
            dve, v = nc.vector, nc.vector
            b = filled(dve, Fa, i, ("T", n))
            if n >= 2:
                s, g = (n - 2) // 4, (n - 2) % 4
                if g < 3:
                    dve.wait_ge(l1_pv, i * 6 + (3 * s + g + 1))
                else:
                    filled(dve, Fa, i, ("O", s))
            v.tensor_copy(probsT[:, n % 2, :], b[:, :]).then_inc(free_sem(Fa, ("T", n)), 1)

        def dve_attention(i, n):
            dve, v = nc.vector, nc.vector

            def halves_copy(use, s, dst):
                b = filled(dve, Fa, i, (use, s))
                v.tensor_copy(dst[:, :, s * P:(s + 1) * P], b[:, 0:256].rearrange("p (a b) -> p a b", a=2))\
                    .then_inc(free_sem(Fa, (use, s)), 1)

            if n == 0:
                dve_masks(i)
            if n < NL:
                dve_l1_max(i, n)
            if 0 <= n - 2 < NL:
                dve_l1_probsT(i, n - 2)
            if 0 <= n - 1 < NL:
                dve.wait_ge(l1_probs, i * NL + n)
                v.reciprocal(finv[:, (n - 1) % 3, 0:C1], fsum[:, (n - 1) % 3, 0:C1]).then_inc(l1_inv, 1)
                if isinstance(i, int) and i == 0:
                    dve.wait_ge(l1_inv, n)
                    l1_scale(v, n - 1)
            if n in (7, 10):
                halves_copy("O", (n - 7) // 3, oT)
            if n in (9, 12):
                s = (n - 9) // 3
                if s == 0 and (not isinstance(i, int) or i > 0):
                    filled(dve, Fm, i - 1, "SH")
                halves_copy("XT", s, xnT)

        def dve_gates(it):
            dve, v = nc.vector, nc.vector
            steps = [0]

            def link(ins):
                steps[0] += 1
                ins.then_inc(gate_step, 1)
                dve.wait_ge(gate_step, it * GATE_STEPS + steps[0])

            b = filled(dve, Fa, it, "logit")
            v.tensor_copy(lg1, b[:, 0:16].rearrange("p (s e) -> p s e", s=2)).then_inc(free_sem(Fa, "logit"), 1)
            drained(dve, Fa, it, "logit")
            top2(lg1, 2, link)
            dve.wait_ge(gate_exp, it + 1)
            top2_probs(2, link)
            link(v.tensor_tensor(gtmp, route["one1"][:, 0:2, :], p12[:, 0, 0:2].unsqueeze(2).broadcast_to([P, 2, E1]), ALU.mult))
            link(v.tensor_tensor(gates[:, :, 0:E1], route["one2"][:, 0:2, :], p12[:, 1, 0:2].unsqueeze(2).broadcast_to([P, 2, E1]), ALU.mult))
            v.memset(gates[:, :, E1:E1 + 1], 1.0)
            v.tensor_tensor(gates[:, :, 0:E1], gates[:, :, 0:E1], gtmp, ALU.add).then_inc(gates_ready, 1)
            assert steps[0] == GATE_STEPS

        def dve_experts(it, n):
            dve, v = nc.vector, nc.vector
            if n == 0:
                dve_gates(it)
            if n == 2:
                b = filled(dve, Fm, it, "gatesT")
                v.tensor_copy(gatesT, b[0:9, 0:256].rearrange("p (s q) -> p s q", s=2)).then_inc(free_sem(Fm, "gatesT"), 1)
            if n == 4:
                b = filled(dve, Fm, it, "SY")
                v.tensor_tensor(acc[:, :, :], b[:, :].rearrange("p (s d) -> p s d", s=2), h_all[:, bass.ds(it * 2, 2), :], ALU.add)\
                    .then_inc(free_sem(Fm, "SY"), 1)
                drained(dve, Fm, it, "SY")
                dve.wait_ge(gates_ready, it + 1)
            if n in DOWNS:
                e = DOWNS[n]
                b = filled(dve, Fm, it, ("E", e))
                if e > 0:
                    drained(dve, Fm, it, ("E", e - 1))
                if e == E1 - 1:
                    wait(dve, out_stored, it * 16)
                for s in range(2):
                    last = v.scalar_tensor_tensor((acc if e < E1 - 1 else out_s)[:, s, :], b[:, s * 256:(s + 1) * 256],
                                                  gates[:, s, e:e + 1], acc[:, s, :], ALU.mult, ALU.add)
                last.then_inc(free_sem(Fm, ("E", e)), 1)

        def F_dve(it, att, moe):
            for n in range(STEPS_F):
                if att:
                    dve_attention(it + 1, n)
                if not moe and 9 <= n < 9 + PAIRS - 1:
                    E_dve(n - 8)
                if moe:
                    dve_experts(it, n)

        def act_attention(i, n):
            act, a = nc.scalar, nc.scalar
            if n < NL:
                act.wait_ge(l1_max, i * NL + (n + 1))
                if n >= 3:
                    filled(act, Fa, i, ("T", n - 3))
                for cc in range(C1):
                    last = a.activation(probs[:, n % 3, cc * 256:(cc + 1) * 256], masked[:, n % 2, cc * 256:(cc + 1) * 256],
                                        ACT.Exp, bias=neg_max[:, n % 3, cc:cc + 1], scale=256.0 ** -0.5,
                                        accum_out=fsum[:, n % 3, cc:cc + 1])
                last.then_inc(l1_probs, 1)
            if n in (8, 11):
                s = (n - 8) // 3
                b = filled(act, Fa, i, ("Y", s))
                a.activation(y_sb[:, s, :], b[:, 0:256], ACT.Copy).then_inc(free_sem(Fa, ("Y", s)), 1)

        def act_experts(it):
            act, a = nc.scalar, nc.scalar
            act.wait_ge(gate_step, it * GATE_STEPS + 12)
            a.activation(pexp[:, 1, 0:2], pexp[:, 0, 0:2], ACT.Exp).then_inc(gate_exp, 1)
            for hp in range(4):
                b = filled(act, Fm, it, ("H", hp))
                for i in range(2):
                    e = 2 * hp + i
                    last = a.activation(hT[:, e, :], b[:, i * 256:(i + 1) * 256], ACT.Gelu, bias=b1_s[:, e:e + 1])
                last.then_inc(free_sem(Fm, ("H", hp)), 1)
            b = filled(act, Fm, it, "SH")
            for i in range(2):
                last = a.activation(shT[:, i, :], b[:, i * 256:(i + 1) * 256], ACT.Gelu, bias=sb1_s[:, i:i + 1])
            last.then_inc(free_sem(Fm, "SH"), 1)

        def F_act(it, att, moe):
            for n in range(STEPS_F):
                if att:
                    act_attention(it + 1, n)
                if moe and n == 0:
                    act_experts(it)

        def F_store(it):
            sp = nc.sync
            drained(sp, Fm, it, ("E", E1 - 1))
            sp.dma_start(out[bass.ds(it * 2, 2), :, :].rearrange("s p d -> p s d"), out_s[:, :, :]).then_inc(out_stored, 16)

        def F_run(eng, keys, body):
            keys(0)
            body(-1, att=True, moe=False)
            body(0, att=True, moe=True)
            if eng is nc.gpsimd:
                for p in range(2, PAIRS):
                    drained(eng, E, 0, ("kT", p))
                    for s in range(2):
                        eng.wait_ge(kv_gathered[2 * p + s], 32)
            with eng.Fori(1, PAIRS - 1) as it:
                body(it, att=True, moe=True)
            body(PAIRS - 1, att=False, moe=True)

        def loop(eng, body, n):
            body(0)
            with eng.Fori(1, n) as it:
                body(it)

        block = ctx.enter_context(nc.Block())

        @block.sync
        def _(sp):
            sp.dma_start(const[:, :], t["const"]).then_inc(consts_loaded, 16)
            sp.dma_start(kvl[:, :], t["kv_lens"].rearrange("(o n) -> o n", o=1).broadcast_to([P, NSEQ])).then_inc(kvl_loaded, 16)
            sp.dma_start(x_in[:, :, :], t["x"][0:2, :, :].rearrange("s p d -> p s d")).then_inc(x_loaded, 16)
            for i, n in enumerate(("cWq", "cWk", "cWv", "cWo")):
                sp.dma_start(w_c[:, i, :, :], t[n].rearrange("(c p) n -> p c n", p=P)).then_inc(cond_w_loaded, 16)
            sp.dma_start(beta[:, :], t["cond_1"].rearrange("b o -> o b").broadcast_to([P, NSEQ])).then_inc(cond_w_loaded, 16)
            sp.dma_start(norm1[:, :], t["norm1"].rearrange("(c p) -> p c", p=P), allow_slow_non_contiguous=True).then_inc(cond_w_loaded, 16)
            sp.dma_start(norm2[:, :], t["norm2"].rearrange("(c p) -> p c", p=P), allow_slow_non_contiguous=True).then_inc(cond_w_loaded, 16)
            sp.dma_start(gate0[:, :, :], t["gate0"].rearrange("(c p) n -> p c n", p=P)).then_inc(cond_w_loaded, 16)
            sp.dma_start(w_kv[:, 1, :, :], t["wv"].rearrange("(c p) n -> p c n", p=P)).then_inc(attn_w_loaded, 16)
            sp.dma_start(w_kv[:, 0, :, :], t["wk"].rearrange("(c p) n -> p c n", p=P)).then_inc(attn_w_loaded, 16)
            sp.dma_start(wq, t["wq"].rearrange("(c p) n -> p c n", p=P)).then_inc(attn_w_loaded, 16)
            sp.dma_start(wo, t["wo"].rearrange("(h p) n -> p h n", p=P)).then_inc(attn_w_loaded, 16)
            sp.wait_ge(zero_ready, 1)
            zero_rows = xs_d.rearrange("(i p) d -> p i d", p=P)
            for a in range(0, TILES0, ZERO_TILES):
                z = min(a + ZERO_TILES, TILES0)
                sp.dma_start(zero_rows[:, a:z, :], kv_old[:, 0:z - a, :]).then_inc(zero_filled, 16)
            sp.wait_ge(kvl_loaded, 16)
            for b in range(NSEQ):
                n = sp.value_load(kvl[0:1, b:b + 1], min_val=0, max_val=NBLK * BLOCK - P)
                sp.dma_start(cs_all[:, b, :], t["rope"][bass.ds(n, P), :]).then_inc(rope_loaded, 16)

            def next_x(it):
                filled(sp, Ac, it, "xT")
                sp.dma_start(x_in[:, :, :], t["x"][bass.ds((it + 1) * 2, 2), :, :].rearrange("s p d -> p s d"))\
                    .then_inc(x_loaded, 16)

            next_x(0)
            for w, n in enumerate(("w1", "w3")):
                for e in range(E0):
                    sp.dma_start(w13[:, w, e, :, :], t[n][e, :, :].rearrange("(c p) n -> p c n", p=P)).then_inc(expert_w_loaded, 16)
            with sp.Fori(1, PAIRS - 1) as it:
                next_x(it)
            filled(sp, Ac, PAIRS - 1, ("cY", 1))
            sp.dma_start(w1_1, t["l1w1"].rearrange("e (c p) n -> p e c n", p=P)).then_inc(l1_loaded, 16)
            sp.dma_start(norm_w[:, 0:NQK * HD1], t["qk_scale"].rearrange("(o n) -> o n", o=1).broadcast_to([P, NQK * HD1])).then_inc(l1_loaded, 16)
            filled(sp, Af, PAIRS - 1, ("rope", NR - 1))
            for e in range(0, E0 // 2):
                sp.dma_start(w2e[:, e, :, :], t["w2"][e, :, :].rearrange("(c p) n -> p c n", p=P)).then_inc(w2_loaded, 16)
            sp.dma_start(w2_1, t["l1w2"].rearrange("e p n -> p e n")).then_inc(l1_loaded, 16)
            filled(sp, Af, PAIRS - 1, "wo")
            for e in range(E0 // 2, E0):
                sp.dma_start(w2e[:, e, :, :], t["w2"][e, :, :].rearrange("(c p) n -> p c n", p=P)).then_inc(w2_loaded, 16)
            sp.dma_start(w_qkv, t["Wqkv1"].rearrange("(c p) n -> p c n", p=P)).then_inc(l1_loaded, 16)
            sp.dma_start(sw1, t["sw1"].rearrange("(c p) n -> p c n", p=P)).then_inc(l1_loaded, 16)
            sp.dma_start(sw2, t["sw2"].rearrange("(c p) n -> p c n", p=P)).then_inc(l1_loaded, 16)
            sp.dma_start(wo_1, t["Wo1"].rearrange("(c p) n -> p c n", p=P)).then_inc(l1_loaded, 16)
            sp.dma_start(gate1, t["gate1"].rearrange("(c p) n -> p c n", p=P)).then_inc(l1_loaded, 16)
            sp.dma_start(b1_s, t["b1"].rearrange("e p -> p e"), allow_slow_non_contiguous=True).then_inc(l1_loaded, 16)
            sp.dma_start(sb1_s, t["sb1"].rearrange("(c p) -> p c", p=P), allow_slow_non_contiguous=True).then_inc(l1_loaded, 16)
            sp.dma_start(b2_s[0:8, :], t["b2"]).then_inc(l1_loaded, 16)
            sp.dma_start(b2_s[8:9, :], t["sb2"].rearrange("(o n) -> o n", o=1)).then_inc(l1_loaded, 16)
            drained(sp, Af, PAIRS - 1, "logit")
            sp.wait_ge(written_out, 16)
            sp.dma_start(written, wl_d.rearrange("(o n) -> o n", o=1).broadcast_to([P, NSEQ * P])).then_inc(written_in, 16)
            sp.dma_start(row_no, t["row_no"].rearrange("(o n) -> o n", o=1).broadcast_to([P, NSEQ * P])).then_inc(written_in, 16)
            sp.wait_ge(scattered, 16 * 2 * NSEQ)
            C_load(0, 0)
            C_load(0, 1)
            C_load(0, 2)

            def step(j, k):
                C_load(j, k + 2)
                C_store(j, k - 1)

            step(0, 1)
            sp.dma_start(x_all[:, :, :], t["x"].rearrange("s p d -> p s d")).then_inc(x_again, 16)
            step(0, 2)
            with sp.Fori(1, STEPS - 1) as j:
                step(j, 1)
                step(j, 2)
            C_store(STEPS - 1, 0)
            C_store(STEPS - 1, 1)
            C_store(STEPS - 1, 2)
            D_run(sp, D_store)
            loop(sp, F_store, PAIRS)
            for i in range(2):
                sp.wait_ge(row_stored[i], 16 * ((TILES0 + 1 - i) // 2))
            for i in range(2):
                sp.wait_ge(kv_stored[i], 16 * PAIRS)
            sp.wait_ge(zero_filled, ZERO_FILLS * 16)
            sp.wait_ge(scattered, 16 * 2 * NSEQ)
            sp.wait_ge(written_out, 16)
            sp.wait_ge(out_stored, 16 * PAIRS)

        @block.gpsimd
        def _(pool):
            nc.gpsimd.memset(neg_half[:, :], -0.5).then_inc(neg_half_ready, 1)
            pool.wait_ge(neg_half_ready, 1)
            pool.wait_ge(consts_loaded, 16)
            pool.wait_ge(table_at_ready, 1)
            A_run(pool, A_pool)
            B_pool()
            cache_pool()
            D_add_x()
            pool.wait_ge(rope_loaded, 16 * NSEQ)
            D_run(pool, D_pool)
            pool.wait_ge(winner_ready, 1)
            pool.wait_ge(cache_read, 16 * 2 * NSEQ * G1)
            for i in range(2):
                pool.wait_ge(kv_stored[i], 16 * PAIRS)
            F_run(pool, E_pool, F_pool)

        @block.scalar
        def _(act):
            act.wait_ge(beta_ready, 1)
            act.wait_ge(cv_zero, 1)
            A_run(act, A_act)
            B_act()

            def first():
                C_act_step(0, 0)

            C_run(act, first, C_act_step, lambda: (C_act_step(STEPS - 1, 2), C_act_down(STEPS - 1, 2)))
            act.wait_ge(x_added, 1)
            D_run(act, D_act)
            act.wait_ge(l1_loaded, 16 * 12)
            F_run(act, lambda p: None, F_act)

        @block.vector
        def _(dve):
            dve.wait_ge(consts_loaded, 16)
            places_dve()
            dve.wait_ge(cond_w_loaded, 128)
            nc.vector.tensor_scalar(beta[:, :], beta[:, :], 4.0, CHD ** -0.5, ALU.min, ALU.mult).then_inc(beta_ready, 1)
            A_run(dve, A_dve)
            B_dve()
            dve.wait_ge(written_in, 32)

            def first():
                C_rowsT_copy(0, 0)
                C_dve_step(0, 0)

            C_run(dve, first, C_dve_step, lambda: (C_dve_step(STEPS - 1, 2, more=False), C_hidT_copy(STEPS - 1, 2)))
            winners_dve()
            dve.wait_ge(l1_loaded, 16 * 12)
            dve.wait_ge(rope_loaded, 16 * NSEQ)
            nc.vector.tensor_scalar(norm_w[:, 0:NQK * HD1], norm_w[:, 0:NQK * HD1], 1.0, None, ALU.add).then_inc(norm_w_ready, 1)
            dve.wait_ge(norm_w_ready, 1)
            dve.wait_ge(x_added, 1)
            D_run(dve, D_dve)
            F_run(dve, E_dve, F_dve)

        @block.tensor
        def _(pe):
            pe.wait_ge(consts_loaded, 16)
            pe.wait_ge(cond_w_loaded, 128)
            A_run(pe, A_pe)
            B_pe()
            pe.wait_ge(expert_w_loaded, 16 * 2 * E0)
            pe.wait_ge(tile_e_ready, 1)

            def first():
                C_transpose_rows(0, 0)
                C_pe_step(0, 0)
                pe.wait_ge(w2_loaded, 16 * E0)

            C_run(pe, first, C_pe_step, lambda: (C_pe_step(STEPS - 1, 2, more=False), C_transpose_hidden(STEPS - 1, 2),
                                                 C_down(STEPS - 1, 2)))
            pe.wait_ge(l1_loaded, 16 * 12)
            D_run(pe, D_pe)
            F_run(pe, E_pe, F_pe)


def constants(np):
    a = {k: np.zeros((P, w), np.float32) for k, w in CONST_COLS.items()}
    i = np.arange(P)
    a["ident"][:] = np.eye(P)
    a["causal"][:] = np.where(i[None, :] <= i[:, None], 0.0, NEG)
    a["older"][:] = np.where(i[None, :] > i[:, None], 0.0, NEG)
    inv = (1.0 / np.float32(1000000.0) ** (np.arange(0, FHD, 2, dtype=np.float32) / np.float32(FHD))).astype(np.float32)
    ang = i.astype(np.float32)[None, :] * inv[:, None]
    a["cos"][:] = np.concatenate([np.cos(ang), np.cos(ang)])
    a["sin"][:] = np.concatenate([-np.sin(ang), np.sin(ang)])
    a["ones"][:] = 1.0
    a["before"][:] = i[:, None] < i[None, :]
    a["key_row"][:] = i[None, :]
    a["expert"][:] = np.tile(np.arange(8), 8)[None, :]
    a["expert8"][:] = np.tile(np.arange(8) + 8, 8)[None, :]
    a["below"][:] = np.tril(np.ones((8, 8)), -1).reshape(1, 64)
    a["tile_no"][:] = np.repeat(np.arange(TILES0), E0)[None, :]
    a["even"][:, 0] = (i // CHD) % 2 == 0
    a["odd"][:, 0] = (i // CHD) % 2 == 1
    a["row"][:, 0] = i
    a["seq_base"][:] = np.tile(np.arange(NSEQ) * NBLK, 2)[None, :]
    return np.ascontiguousarray(np.concatenate([a[k] for k in CONST_COLS], axis=1))


def kernel(**inputs):
    import numpy as np
    import concourse.bacc as bacc
    from concourse import mybir as mb
    from concourse.bass_utils import run_bass_kernel_spmd

    nc = bacc.Bacc("TRN2", target_bir_lowering=False, num_devices=1)
    g = {k: np.asarray(v) for k, v in inputs.items()}
    arrays = {"const": constants(np), "x": g["x"], "cond_1": g["cond_1"]}
    for n in ("Wq", "Wk", "Wv", "Wo"):
        arrays["c" + n] = np.ascontiguousarray(g["L0_cond_" + n].T)
    for n, k in (("norm1", "norm1_w"), ("norm2", "norm2_w"), ("wq", "wq"), ("wk", "wk"), ("wv", "wv"), ("wo", "wo"),
                 ("gate0", "gate_w"), ("w1", "w1"), ("w3", "w3"), ("w2", "w2")):
        arrays[n] = np.ascontiguousarray(g["L0_ffn_" + k])
    wq1 = g["L1_cond_Wq"].reshape(G1, C1, HD1, D).transpose(1, 0, 2, 3).reshape(D, D)
    arrays["Wqkv1"] = np.ascontiguousarray(np.concatenate([wq1, g["L1_cond_Wk"], g["L1_cond_Wv"]], axis=0).T)
    arrays["Wo1"] = np.ascontiguousarray(g["L1_cond_Wo"].reshape(D, G1, C1, HD1).transpose(2, 1, 3, 0).reshape(D, D))
    arrays["qk_scale"] = np.concatenate([np.tile(g["L1_cond_q_norm_scale"], 8), np.tile(g["L1_cond_k_norm_scale"], G1)])
    arrays["k_blocks"], arrays["v_blocks"] = g["L1_cond_k_blocks"], g["L1_cond_v_blocks"]
    arrays["table"] = g["itok_Bx257_0_4111"].reshape(NSEQ * NBLK, 1)
    arrays["kv_lens"] = g["itok_B_37_3939"]
    for n, k in (("gate1", "gate_w"), ("l1w1", "w1"), ("b1", "b1"), ("l1w2", "w2"), ("b2", "b2"), ("sw1", "shared_w1"),
                 ("sb1", "shared_b1"), ("sw2", "shared_w2"), ("sb2", "shared_b2")):
        arrays[n] = np.ascontiguousarray(g["L1_ffn_" + k])
    inv = (1.0 / np.float32(10000.0) ** (np.arange(HD1 // 2, dtype=np.float32) / np.float32(HD1 // 2))).astype(np.float32)
    ang = np.arange(NBLK * BLOCK, dtype=np.float32)[:, None] * inv[None, :]
    arrays["rope"] = np.concatenate([np.cos(ang), np.sin(ang)], axis=1).astype(np.float32)
    arrays["row_no"] = np.arange(1, NSEQ * P + 1, dtype=np.float32)
    t = {n: nc.dram_tensor("in_" + n, a.shape, mb.dt.from_np(a.dtype), kind="ExternalInput").ap() for n, a in arrays.items()}
    out = nc.dram_tensor("out", (NSEQ, P, D), mb.dt.float32, kind="ExternalOutput").ap()
    program(nc, t, out)
    r = run_bass_kernel_spmd(nc, [{"in_" + n: a for n, a in arrays.items()}], core_ids=[0])
    return r.results[0]["out"]
```
